# Optimizing a Trainium2 kernel written in Bass

```python
import numpy as np
import jax
import jax.numpy as jnp

def _softmax(x, axis=-1):
    return jax.nn.softmax(x, axis=axis)

def _gelu(x):
    return jax.nn.gelu(x, approximate=True)

def _silu(x):
    return jax.nn.silu(x)

def _sigmoid(x):
    return jax.nn.sigmoid(x)

def _layernorm(x, axis=-1, eps=1e-05):
    m = jnp.mean(x, axis=axis, keepdims=True)
    v = jnp.var(x, axis=axis, keepdims=True)
    return (x - m) / jnp.sqrt(v + eps)

def _scatter_add(tgt, idx, src, axis=0):
    return tgt.at[idx].add(src)

def _segment_sum(src, seg, n):
    return jax.ops.segment_sum(src, seg, n)
kernel_name = 'mk_decoder_preln_d2_seqx_r8_7674d2'

def setup_inputs(seed: int=0):
    np.random.seed(seed)
    _w = jnp.asarray

    def _rec_inputs():
        import jax
        import jax.numpy as jnp
        _rk = jax.random.key(seed)
        x = -0.0003929 + 0.9999 * jax.random.normal(jax.random.fold_in(_rk, 1), (16, 64, 256), jnp.float32)
        _lenS = 64 - jax.random.randint(jax.random.fold_in(_rk, 7), (16,), 0, max(1, 64 // 4) + 1, jnp.int32)
        _lenS2 = 64 - jax.random.randint(jax.random.fold_in(_rk, 8), (16,), 0, max(1, 64 // 4) + 1, jnp.int32)
        _ctx_2048P = jax.random.normal(jax.random.fold_in(_rk, 11), (16, 16, 256), jnp.float32)
        _ctx_2048c = jax.random.dirichlet(jax.random.fold_in(_rk, 511), 0.3 * jnp.ones((16,), jnp.float32), (16, 64))
        _ctx_2048t = jnp.einsum('bsk,bkd->bsd', _ctx_2048c, _ctx_2048P)
        _ctx_2048t = _ctx_2048t * jax.lax.rsqrt(jnp.mean(jnp.square(_ctx_2048t)) + 1e-12) * 0.953939
        ctx_2048 = -0.000514642 + 1.00011 * (_ctx_2048t + 0.3 * jax.random.normal(jax.random.fold_in(_rk, 611), (16, 64, 256), jnp.float32))
        pos_BxS2 = jnp.broadcast_to(jnp.arange(64, dtype=jnp.int32), (16, 64))
        itok_BxS_4096_4607 = jax.random.randint(jax.random.fold_in(_rk, 14), (16, 64), 512, 576, jnp.int32)
        _validS = jnp.arange(64)[None, :] < _lenS[:, None]
        _validS2 = jnp.arange(64)[None, :] < _lenS2[:, None]
        _causal = jnp.tril(jnp.ones((64, 64), dtype=bool))
        mask_BxS2_ik0 = jnp.where(jnp.broadcast_to(_validS2[:, :], (16, 64)), 0, 1).astype(jnp.int32)
        return (x, ctx_2048, pos_BxS2, itok_BxS_4096_4607, mask_BxS2_ik0)
    x, ctx_2048, pos_BxS2, itok_BxS_4096_4607, mask_BxS2_ik0 = _rec_inputs()

    def _L0_attn_setup():
        import jax, jax.numpy as jnp
        import numpy as np
        B, S, D, H = (2, 256, 256, 16)
        HD = D // H
        key = jax.random.key(seed)
        ks = jax.random.split(key, 5)
        scale = 0.02
        return {'hidden_states': jax.random.normal(ks[0], (B, S, D), dtype=jnp.float32), 'Wqkv_w': jax.random.normal(ks[1], (3 * D, D), dtype=jnp.float32) * scale, 'Wqkv_b': jax.random.normal(ks[2], (3 * D,), dtype=jnp.float32) * scale, 'out_w': jax.random.normal(ks[3], (D, D), dtype=jnp.float32) * scale, 'out_b': jax.random.normal(ks[4], (D,), dtype=jnp.float32) * scale}
    _L0_attn_all = _L0_attn_setup()
    _L0_attn_in = {k: v for k, v in _L0_attn_all.items() if k in ('Wqkv_w', 'Wqkv_b', 'out_w', 'out_b')}
    del _L0_attn_all

    def _L0_xattn_setup():
        import jax, jax.numpy as jnp
        import numpy as np
        import math
        H = 256
        NH = 16
        HD = H // NH
        EPS_LN = 1e-05
        RES_SCALE_MAX = 0.3

        def _nan_clean(x, lim=10000.0):
            return jnp.nan_to_num(x, nan=0.0, posinf=lim, neginf=-lim)
        key = jax.random.key(seed)
        ks = jax.random.split(key, 12)
        B, S, T = (4, 256, 32)
        std = 1.0 / math.sqrt(H)
        return {'hidden_states': jax.random.normal(ks[0], (B, S, H), jnp.float32), 'audio_tokens': jax.random.normal(ks[1], (B, T, H), jnp.float32), 'attention_mask': jax.random.randint(ks[2], (B, T), 0, 2, jnp.int32), 'Wq': jax.random.normal(ks[3], (H, H), jnp.float32) * std, 'bq': jnp.zeros((H,), jnp.float32), 'Wk': jax.random.normal(ks[4], (H, H), jnp.float32) * std, 'bk': jnp.zeros((H,), jnp.float32), 'Wv': jax.random.normal(ks[5], (H, H), jnp.float32) * std, 'bv': jnp.zeros((H,), jnp.float32), 'Wo': jax.random.normal(ks[6], (H, H), jnp.float32) * std, 'bo': jnp.zeros((H,), jnp.float32), 'ln_gamma': jnp.ones((H,), jnp.float32), 'ln_beta': jnp.zeros((H,), jnp.float32), 'residual_scale': jnp.float32(0.05)}
    _L0_xattn_all = _L0_xattn_setup()
    _L0_xattn_in = {k: v for k, v in _L0_xattn_all.items() if k in ('Wq', 'bq', 'Wk', 'bk', 'Wv', 'bv', 'Wo', 'bo', 'ln_gamma', 'ln_beta', 'residual_scale')}
    del _L0_xattn_all

    def _L0_ffn_setup():
        import jax, jax.numpy as jnp
        import numpy as np
        H = 256
        I = 128
        E = 32
        K = 4
        N_SHARED = 1
        EPS = 1e-06

        def _rmsnorm(x, w, eps=EPS):
            var = jnp.mean(jnp.square(x), axis=-1, keepdims=True)
            return x * jax.lax.rsqrt(var + eps) * w

        def _moe_core(x, gate_w, w13, w2):
            T = x.shape[0]
            N = T * K
            C = 2 * N // E
            logits = jnp.einsum('th,eh->te', x.astype(jnp.float32), gate_w.astype(jnp.float32))
            scores = jax.nn.softmax(logits, axis=-1)
            topk_w, topk_ids = jax.lax.top_k(scores, K)
            topk_w = topk_w / jnp.sum(topk_w, axis=-1, keepdims=True)
            flat_ids = topk_ids.reshape(-1)
            flat_w = topk_w.reshape(-1)
            order = jnp.argsort(flat_ids)
            sorted_eid = flat_ids[order]
            tok = order // K
            counts = jnp.zeros((E,), jnp.int32).at[flat_ids].add(1)
            starts = jnp.cumsum(counts) - counts
            pos = jnp.arange(N) - starts[sorted_eid]
            buf = jnp.zeros((E, C, x.shape[1]), x.dtype).at[sorted_eid, pos].set(x[tok], mode='drop')
            gu = jnp.einsum('ech,ehf->ecf', buf, w13)
            g, u = jnp.split(gu, 2, axis=-1)
            act = jax.nn.silu(g) * u
            eo = jnp.einsum('eci,eih->ech', act, w2)
            out_slots = eo[sorted_eid, pos]
            routed = jnp.zeros_like(x).at[tok].add(out_slots * flat_w[order][:, None])
            return routed
        key = jax.random.key(seed)
        ks = jax.random.split(key, 8)
        s = 1.0 / np.sqrt(H)
        si = 1.0 / np.sqrt(I)
        return {'hidden_states': jax.random.normal(ks[0], (1, 512, H), jnp.float32), 'norm_w': jnp.ones((H,), jnp.float32), 'gate_w': jax.random.normal(ks[1], (E, H), jnp.float32) * s, 'w13': jax.random.normal(ks[2], (E, H, 2 * I), jnp.float32) * s, 'w2': jax.random.normal(ks[3], (E, I, H), jnp.float32) * si, 'shared_gate_w': jax.random.normal(ks[4], (H, I * N_SHARED), jnp.float32) * s, 'shared_up_w': jax.random.normal(ks[5], (H, I * N_SHARED), jnp.float32) * s, 'shared_down_w': jax.random.normal(ks[6], (I * N_SHARED, H), jnp.float32) * si}
    _L0_ffn_all = _L0_ffn_setup()
    _L0_ffn_in = {k: v for k, v in _L0_ffn_all.items() if k in ('norm_w', 'gate_w', 'w13', 'w2', 'shared_gate_w', 'shared_up_w', 'shared_down_w')}
    del _L0_ffn_all

    def _L1_attn_setup():
        import jax, jax.numpy as jnp
        import numpy as np
        B, S, D, H = (64, 32, 256, 16)
        HD = D // H
        key = jax.random.key(seed)
        k1, k2, k3 = jax.random.split(key, 3)
        x = jax.random.normal(k1, (B, S, D), dtype=jnp.float32)
        w_qkv = jax.random.normal(k2, (3 * D, D), dtype=jnp.float32) * (1.0 / np.sqrt(D))
        w_o = jax.random.normal(k3, (D, D), dtype=jnp.float32) * (1.0 / np.sqrt(D))
        return {'x': x, 'w_qkv': w_qkv, 'w_o': w_o}
    _L1_attn_all = _L1_attn_setup()
    _L1_attn_in = {k: v for k, v in _L1_attn_all.items() if k in ('w_qkv', 'w_o')}
    del _L1_attn_all

    def _L1_xattn_setup():
        import jax, jax.numpy as jnp
        import numpy as np
        B, CTX, DRAFT, D = (2, 512, 64, 256)
        H, KVH, HD = (16, 4, 128)
        N_REP = H // KVH
        EPS = 1e-06
        THETA = 10000.0
        SCALE = 1.0 / np.sqrt(HD).astype(np.float32)

        def _rms_norm(x, w):
            v = jnp.mean(jnp.square(x.astype(jnp.float32)), axis=-1, keepdims=True)
            return (w * (x.astype(jnp.float32) * jax.lax.rsqrt(v + EPS))).astype(x.dtype)

        def _rotate_half(x):
            x1, x2 = jnp.split(x, 2, axis=-1)
            return jnp.concatenate((-x2, x1), axis=-1)

        def _rope(x, pos):
            inv_freq = 1.0 / THETA ** (jnp.arange(0, HD, 2, dtype=jnp.float32) / HD)
            freqs = pos.astype(jnp.float32)[:, None, :, None] * inv_freq
            emb = jnp.concatenate((freqs, freqs), axis=-1)
            return x * jnp.cos(emb) + _rotate_half(x) * jnp.sin(emb)
        key = jax.random.key(seed)
        ks = jax.random.split(key, 6)
        return {'draft_hidden': jax.random.normal(ks[0], (B, DRAFT, D), jnp.float32), 'context_hidden': jax.random.normal(ks[1], (B, CTX, D), jnp.float32), 'Wq': jax.random.normal(ks[2], (H * HD, D), jnp.float32) * 0.02, 'Wk': jax.random.normal(ks[3], (KVH * HD, D), jnp.float32) * 0.02, 'Wv': jax.random.normal(ks[4], (KVH * HD, D), jnp.float32) * 0.02, 'Wo': jax.random.normal(ks[5], (D, H * HD), jnp.float32) * 0.02, 'q_norm_w': jnp.ones((HD,), jnp.float32), 'k_norm_w': jnp.ones((HD,), jnp.float32), 'context_position_ids': jnp.broadcast_to(jnp.arange(CTX, dtype=jnp.int32), (B, CTX)), 'draft_position_ids': jnp.broadcast_to(CTX + jnp.arange(DRAFT, dtype=jnp.int32), (B, DRAFT))}
    _L1_xattn_all = _L1_xattn_setup()
    _L1_xattn_in = {k: v for k, v in _L1_xattn_all.items() if k in ('Wq', 'Wk', 'Wv', 'Wo', 'q_norm_w', 'k_norm_w')}
    del _L1_xattn_all

    def _L1_ffn_setup():
        import jax, jax.numpy as jnp
        import numpy as np
        H = 256
        E = 64
        I = 64
        SI = 64
        TOP_K = 8
        B, T = (2, 64)
        key = jax.random.key(seed)
        ks = jax.random.split(key, 8)
        s = 0.02
        return {'h': jax.random.normal(ks[0], (B, T, H), jnp.float32), 'gate_w': jax.random.normal(ks[1], (E, H), jnp.float32) * s, 'gu_w': jax.random.normal(ks[2], (E, 2 * I, H), jnp.float32) * s, 'dp_w': jax.random.normal(ks[3], (E, H, I), jnp.float32) * s, 'sh_gate_w': jax.random.normal(ks[4], (SI, H), jnp.float32) * s, 'sh_up_w': jax.random.normal(ks[5], (SI, H), jnp.float32) * s, 'sh_down_w': jax.random.normal(ks[6], (H, SI), jnp.float32) * s, 'sh_gate1_w': jax.random.normal(ks[7], (1, H), jnp.float32) * s}
    _L1_ffn_all = _L1_ffn_setup()
    _L1_ffn_in = {k: v for k, v in _L1_ffn_all.items() if k in ('gate_w', 'gu_w', 'dp_w', 'sh_gate_w', 'sh_up_w', 'sh_down_w', 'sh_gate1_w')}
    del _L1_ffn_all
    return {'x': x, 'ctx_2048': ctx_2048, 'pos_BxS2': pos_BxS2, 'itok_BxS_4096_4607': itok_BxS_4096_4607, 'mask_BxS2_ik0': mask_BxS2_ik0, 'L0_attn_Wqkv_w': _L0_attn_in['Wqkv_w'], 'L0_attn_Wqkv_b': _L0_attn_in['Wqkv_b'], 'L0_attn_out_w': _L0_attn_in['out_w'], 'L0_attn_out_b': _L0_attn_in['out_b'], 'L0_xattn_Wq': _L0_xattn_in['Wq'], 'L0_xattn_bq': _L0_xattn_in['bq'], 'L0_xattn_Wk': _L0_xattn_in['Wk'], 'L0_xattn_bk': _L0_xattn_in['bk'], 'L0_xattn_Wv': _L0_xattn_in['Wv'], 'L0_xattn_bv': _L0_xattn_in['bv'], 'L0_xattn_Wo': _L0_xattn_in['Wo'], 'L0_xattn_bo': _L0_xattn_in['bo'], 'L0_xattn_ln_gamma': _L0_xattn_in['ln_gamma'], 'L0_xattn_ln_beta': _L0_xattn_in['ln_beta'], 'L0_xattn_residual_scale': _L0_xattn_in['residual_scale'], 'L0_ffn_norm_w': _L0_ffn_in['norm_w'], 'L0_ffn_gate_w': _L0_ffn_in['gate_w'], 'L0_ffn_w13': _L0_ffn_in['w13'], 'L0_ffn_w2': _L0_ffn_in['w2'], 'L0_ffn_shared_gate_w': _L0_ffn_in['shared_gate_w'], 'L0_ffn_shared_up_w': _L0_ffn_in['shared_up_w'], 'L0_ffn_shared_down_w': _L0_ffn_in['shared_down_w'], 'L1_attn_w_qkv': _L1_attn_in['w_qkv'], 'L1_attn_w_o': _L1_attn_in['w_o'], 'L1_xattn_Wq': _L1_xattn_in['Wq'], 'L1_xattn_Wk': _L1_xattn_in['Wk'], 'L1_xattn_Wv': _L1_xattn_in['Wv'], 'L1_xattn_Wo': _L1_xattn_in['Wo'], 'L1_xattn_q_norm_w': _L1_xattn_in['q_norm_w'], 'L1_xattn_k_norm_w': _L1_xattn_in['k_norm_w'], 'L1_ffn_gate_w': _L1_ffn_in['gate_w'], 'L1_ffn_gu_w': _L1_ffn_in['gu_w'], 'L1_ffn_dp_w': _L1_ffn_in['dp_w'], 'L1_ffn_sh_gate_w': _L1_ffn_in['sh_gate_w'], 'L1_ffn_sh_up_w': _L1_ffn_in['sh_up_w'], 'L1_ffn_sh_down_w': _L1_ffn_in['sh_down_w'], 'L1_ffn_sh_gate1_w': _L1_ffn_in['sh_gate1_w']}

def reference(x, ctx_2048, pos_BxS2, itok_BxS_4096_4607, mask_BxS2_ik0, L0_attn_Wqkv_w, L0_attn_Wqkv_b, L0_attn_out_w, L0_attn_out_b, L0_xattn_Wq, L0_xattn_bq, L0_xattn_Wk, L0_xattn_bk, L0_xattn_Wv, L0_xattn_bv, L0_xattn_Wo, L0_xattn_bo, L0_xattn_ln_gamma, L0_xattn_ln_beta, L0_xattn_residual_scale, L0_ffn_norm_w, L0_ffn_gate_w, L0_ffn_w13, L0_ffn_w2, L0_ffn_shared_gate_w, L0_ffn_shared_up_w, L0_ffn_shared_down_w, L1_attn_w_qkv, L1_attn_w_o, L1_xattn_Wq, L1_xattn_Wk, L1_xattn_Wv, L1_xattn_Wo, L1_xattn_q_norm_w, L1_xattn_k_norm_w, L1_ffn_gate_w, L1_ffn_gu_w, L1_ffn_dp_w, L1_ffn_sh_gate_w, L1_ffn_sh_up_w, L1_ffn_sh_down_w, L1_ffn_sh_gate1_w):
    import jax
    import jax.numpy as jnp

    def _L0_attn_ref(hidden_states, Wqkv_w, Wqkv_b, out_w, out_b):
        import jax, jax.numpy as jnp
        import numpy as np
        B, S, D, H = (2, 256, 256, 16)
        HD = D // H
        b, s, d = hidden_states.shape
        qkv = hidden_states @ Wqkv_w.T + Wqkv_b
        qkv = qkv.reshape(b, s, 3, H, HD)
        q, k, v = (qkv[:, :, 0], qkv[:, :, 1], qkv[:, :, 2])
        softmax_scale = 1.0 / np.float32(np.sqrt(HD))
        scores = jnp.einsum('bthd,bshd->bhts', q, k) * softmax_scale
        attn = jax.nn.softmax(scores, axis=-1)
        ctx = jnp.einsum('bhts,bshd->bthd', attn, v)
        ctx = ctx.reshape(b, s, d)
        return ctx @ out_w.T + out_b

    def _L0_xattn_ref(hidden_states, audio_tokens, attention_mask, Wq, bq, Wk, bk, Wv, bv, Wo, bo, ln_gamma, ln_beta, residual_scale):
        import jax, jax.numpy as jnp
        import numpy as np
        import math
        H = 256
        NH = 16
        HD = H // NH
        EPS_LN = 1e-05
        RES_SCALE_MAX = 0.3

        def _nan_clean(x, lim=10000.0):
            return jnp.nan_to_num(x, nan=0.0, posinf=lim, neginf=-lim)
        B, S, _ = hidden_states.shape
        T = audio_tokens.shape[1]
        hs = _nan_clean(hidden_states).astype(jnp.float32)
        at = _nan_clean(audio_tokens).astype(jnp.float32)

        def proj(x, W, b, L):
            y = x @ W.T + b
            return y.reshape(B, L, NH, HD).transpose(0, 2, 1, 3)
        q = _nan_clean(proj(hs, Wq, bq, S))
        k = _nan_clean(proj(at, Wk, bk, T))
        v = _nan_clean(proj(at, Wv, bv, T))
        scale = max(math.sqrt(HD), 1e-08)
        scores = jnp.einsum('bhsd,bhtd->bhst', q, k) / scale
        scores = jnp.clip(scores, -50.0, 50.0)
        scores = jnp.nan_to_num(scores, nan=0.0, posinf=50.0, neginf=-50.0)
        attend = (attention_mask.astype(jnp.float32) > 0.5)[:, None, None, :]
        scores = jnp.where(attend, scores, -10000.0)
        scores = jnp.clip(scores, -50.0, 50.0)
        probs = jax.nn.softmax(scores, axis=-1)
        probs = jnp.nan_to_num(probs, nan=0.0, posinf=1.0, neginf=0.0)
        probs = probs / (probs.sum(axis=-1, keepdims=True) + 1e-08)
        ctx = jnp.einsum('bhst,bhtd->bhsd', probs, v)
        ctx = ctx.transpose(0, 2, 1, 3).reshape(B, S, H)
        delta = _nan_clean(ctx @ Wo.T + bo)
        rs = jnp.clip(residual_scale, 0.0, RES_SCALE_MAX)
        delta = rs * delta
        mu = delta.mean(axis=-1, keepdims=True)
        var = jnp.mean((delta - mu) ** 2, axis=-1, keepdims=True)
        delta = (delta - mu) / jnp.sqrt(var + EPS_LN) * ln_gamma + ln_beta
        return delta

    def _L0_ffn_ref(hidden_states, norm_w, gate_w, w13, w2, shared_gate_w, shared_up_w, shared_down_w):
        import jax, jax.numpy as jnp
        import numpy as np
        H = 256
        I = 128
        E = 32
        K = 4
        N_SHARED = 1
        EPS = 1e-06

        def _rmsnorm(x, w, eps=EPS):
            var = jnp.mean(jnp.square(x), axis=-1, keepdims=True)
            return x * jax.lax.rsqrt(var + eps) * w

        def _moe_core(x, gate_w, w13, w2):
            T = x.shape[0]
            N = T * K
            C = 2 * N // E
            logits = jnp.einsum('th,eh->te', x.astype(jnp.float32), gate_w.astype(jnp.float32))
            scores = jax.nn.softmax(logits, axis=-1)
            topk_w, topk_ids = jax.lax.top_k(scores, K)
            topk_w = topk_w / jnp.sum(topk_w, axis=-1, keepdims=True)
            flat_ids = topk_ids.reshape(-1)
            flat_w = topk_w.reshape(-1)
            order = jnp.argsort(flat_ids)
            sorted_eid = flat_ids[order]
            tok = order // K
            counts = jnp.zeros((E,), jnp.int32).at[flat_ids].add(1)
            starts = jnp.cumsum(counts) - counts
            pos = jnp.arange(N) - starts[sorted_eid]
            buf = jnp.zeros((E, C, x.shape[1]), x.dtype).at[sorted_eid, pos].set(x[tok], mode='drop')
            gu = jnp.einsum('ech,ehf->ecf', buf, w13)
            g, u = jnp.split(gu, 2, axis=-1)
            act = jax.nn.silu(g) * u
            eo = jnp.einsum('eci,eih->ech', act, w2)
            out_slots = eo[sorted_eid, pos]
            routed = jnp.zeros_like(x).at[tok].add(out_slots * flat_w[order][:, None])
            return routed
        B, S, Hd = hidden_states.shape
        residual = hidden_states
        h = _rmsnorm(hidden_states, norm_w)
        x = h.reshape(-1, Hd)
        routed = _moe_core(x, gate_w, w13, w2)
        shared = jax.nn.silu(x @ shared_gate_w) * (x @ shared_up_w) @ shared_down_w
        out = residual + (routed + shared).reshape(B, S, Hd)
        return out

    def _L1_attn_ref(x, w_qkv, w_o):
        import jax, jax.numpy as jnp
        import numpy as np
        B, S, D, H = (64, 32, 256, 16)
        HD = D // H
        b, s, d = x.shape
        qkv = jnp.einsum('bsd,ed->bse', x, w_qkv)
        qkv = qkv.reshape(b, s, 3, H, HD).transpose(2, 0, 3, 1, 4)
        q, k, v = (qkv[0], qkv[1], qkv[2])
        scores = jnp.einsum('bhqd,bhkd->bhqk', q, k) * HD ** (-0.5)
        causal = jnp.triu(jnp.ones((s, s), dtype=bool), 1)
        scores = jnp.where(causal, jnp.float32(-1000000000.0), scores)
        a = jax.nn.softmax(scores, axis=-1)
        ctx = jnp.einsum('bhqk,bhkd->bhqd', a, v)
        ctx = ctx.transpose(0, 2, 1, 3).reshape(b, s, d)
        return jnp.einsum('bsd,ed->bse', ctx, w_o)

    def _L1_xattn_ref(draft_hidden, context_hidden, Wq, Wk, Wv, Wo, q_norm_w, k_norm_w, context_position_ids, draft_position_ids):
        import jax, jax.numpy as jnp
        import numpy as np
        B, CTX, DRAFT, D = (2, 512, 64, 256)
        H, KVH, HD = (16, 4, 128)
        N_REP = H // KVH
        EPS = 1e-06
        THETA = 10000.0
        SCALE = 1.0 / np.sqrt(HD).astype(np.float32)

        def _rms_norm(x, w):
            v = jnp.mean(jnp.square(x.astype(jnp.float32)), axis=-1, keepdims=True)
            return (w * (x.astype(jnp.float32) * jax.lax.rsqrt(v + EPS))).astype(x.dtype)

        def _rotate_half(x):
            x1, x2 = jnp.split(x, 2, axis=-1)
            return jnp.concatenate((-x2, x1), axis=-1)

        def _rope(x, pos):
            inv_freq = 1.0 / THETA ** (jnp.arange(0, HD, 2, dtype=jnp.float32) / HD)
            freqs = pos.astype(jnp.float32)[:, None, :, None] * inv_freq
            emb = jnp.concatenate((freqs, freqs), axis=-1)
            return x * jnp.cos(emb) + _rotate_half(x) * jnp.sin(emb)
        bsz, draft_len, _ = draft_hidden.shape
        ctx_len = context_hidden.shape[1]
        total_len = ctx_len + draft_len
        q = (draft_hidden @ Wq.T).reshape(bsz, draft_len, H, HD)
        q = _rms_norm(q, q_norm_w).transpose(0, 2, 1, 3)
        kv_in = jnp.concatenate([context_hidden, draft_hidden], axis=1)
        k = (kv_in @ Wk.T).reshape(bsz, total_len, KVH, HD)
        v = (kv_in @ Wv.T).reshape(bsz, total_len, KVH, HD).transpose(0, 2, 1, 3)
        k = _rms_norm(k, k_norm_w).transpose(0, 2, 1, 3)
        full_position_ids = jnp.concatenate([context_position_ids, draft_position_ids], axis=1)
        q = _rope(q, draft_position_ids)
        k = _rope(k, full_position_ids)
        k = jnp.repeat(k, N_REP, axis=1)
        v = jnp.repeat(v, N_REP, axis=1)
        scores = jnp.einsum('bhqd,bhkd->bhqk', q, k) * SCALE
        probs = jax.nn.softmax(scores, axis=-1)
        attn = jnp.einsum('bhqk,bhkd->bhqd', probs, v)
        attn = attn.transpose(0, 2, 1, 3).reshape(bsz, draft_len, H * HD)
        return attn @ Wo.T

    def _L1_ffn_ref(h, gate_w, gu_w, dp_w, sh_gate_w, sh_up_w, sh_down_w, sh_gate1_w):
        import jax, jax.numpy as jnp
        import numpy as np
        H = 256
        E = 64
        I = 64
        SI = 64
        TOP_K = 8
        B, T = (2, 64)
        Bb, Tt, Hh = h.shape
        x = h.reshape(Bb * Tt, Hh)
        N = x.shape[0]
        logits = x @ gate_w.T
        topv, topi = jax.lax.top_k(logits, TOP_K)
        rw = jax.nn.softmax(topv.astype(jnp.float32), axis=-1).astype(x.dtype)
        W = jnp.zeros((N, E), x.dtype).at[jnp.arange(N)[:, None], topi].set(rw)
        gu = jnp.einsum('nh,eih->nei', x, gu_w)
        gate, up = (gu[..., :I], gu[..., I:])
        inter = jax.nn.silu(gate) * up
        inter_w = inter * W[:, :, None]
        out = jnp.einsum('nei,ehi->nh', inter_w, dp_w)
        sh_inter = jax.nn.silu(x @ sh_gate_w.T) * (x @ sh_up_w.T)
        sh_out = sh_inter @ sh_down_w.T
        sh_g = jax.nn.sigmoid(x @ sh_gate1_w.T)
        out = out + sh_g * sh_out
        return out.reshape(Bb, Tt, Hh)
    x = x + _L0_attn_ref(_layernorm(x, axis=-1), L0_attn_Wqkv_w, L0_attn_Wqkv_b, L0_attn_out_w, L0_attn_out_b)
    x = x + _L0_xattn_ref(_layernorm(x, axis=-1), ctx_2048, mask_BxS2_ik0, L0_xattn_Wq, L0_xattn_bq, L0_xattn_Wk, L0_xattn_bk, L0_xattn_Wv, L0_xattn_bv, L0_xattn_Wo, L0_xattn_bo, L0_xattn_ln_gamma, L0_xattn_ln_beta, L0_xattn_residual_scale)
    x = x + _L0_ffn_ref(_layernorm(x, axis=-1), L0_ffn_norm_w, L0_ffn_gate_w, L0_ffn_w13, L0_ffn_w2, L0_ffn_shared_gate_w, L0_ffn_shared_up_w, L0_ffn_shared_down_w)
    x = x + _L1_attn_ref(_layernorm(x, axis=-1), L1_attn_w_qkv, L1_attn_w_o)
    x = x + _L1_xattn_ref(_layernorm(x, axis=-1), ctx_2048, L1_xattn_Wq, L1_xattn_Wk, L1_xattn_Wv, L1_xattn_Wo, L1_xattn_q_norm_w, L1_xattn_k_norm_w, pos_BxS2, itok_BxS_4096_4607)
    x = x + _L1_ffn_ref(_layernorm(x, axis=-1), L1_ffn_gate_w, L1_ffn_gu_w, L1_ffn_dp_w, L1_ffn_sh_gate_w, L1_ffn_sh_up_w, L1_ffn_sh_down_w, L1_ffn_sh_gate1_w)
    return x

_drawn_inputs = setup_inputs


def setup_inputs(seed=0):
    import zlib

    import numpy as np

    out = dict(_drawn_inputs(seed))
    spreads = {'L0_xattn_bq': (0.0, 0.1),
     'L0_xattn_bk': (0.0, 0.8),
     'L0_xattn_bv': (0.0, 0.1),
     'L0_xattn_bo': (0.0, 0.1),
     'L0_xattn_ln_gamma': (1.0, 0.2),
     'L0_xattn_ln_beta': (0.0, 0.1),
     'L0_ffn_norm_w': (1.0, 0.2),
     'L1_xattn_q_norm_w': (1.0, 0.6),
     'L1_xattn_k_norm_w': (1.0, 0.6)}
    factors = {'L0_attn_Wqkv_w': 3.606,
     'L0_attn_Wqkv_b': 5.475,
     'L0_attn_out_w': 3.308,
     'L0_attn_out_b': 2.725,
     'L1_xattn_Wq': 2.745,
     'L1_xattn_Wk': 2.747,
     'L1_ffn_gate_w': 8.0,
     'L1_ffn_gu_w': 8.0,
     'L1_ffn_dp_w': 8.0,
     'L1_ffn_sh_gate_w': 8.0,
     'L1_ffn_sh_up_w': 8.0,
     'L1_ffn_sh_down_w': 8.0,
     'L1_ffn_sh_gate1_w': 8.0}
    for name, (base, spread) in spreads.items():
        noise = np.random.default_rng([zlib.crc32(name.encode()), seed]).standard_normal(out[name].shape)
        drawn = base * np.exp(spread * noise) if base else spread * noise
        out[name] = jnp.asarray(drawn.astype(out[name].dtype))
    for name, factor in factors.items():
        out[name] = (out[name] * factor).astype(out[name].dtype)
    return out
```

```python
import numpy as np
import concourse.bass as bass
from concourse import mybir
from contextlib import ExitStack

F32 = mybir.dt.float32
F16 = mybir.dt.float16
I32 = mybir.dt.int32
U32 = mybir.dt.uint32
ALU = mybir.AluOpType
ACT = mybir.ActivationFunctionType
AX = mybir.AxisListType

P = 128
B, S, D = 16, 64, 256
NT = B * S // P
DC = D // P
H = 16
HD = D // H
HG = P // HD
NP = H // 2
OW = 2 * (HD + 1)
QSCALE = float(HD) ** -0.5
ONLY = 0


class Store:

    def __init__(self, nc, last=False):
        self.nc, self.stack, self.held = nc, ExitStack(), []
        if not last:
            self.stack.callback(self.clear)

    def sb(self, name, shape, dt=F32):
        return self.stack.enter_context(self.nc.sbuf_tensor(name, shape, dt))

    def ps(self, name, shape):
        return self.stack.enter_context(self.nc.psum_tensor(name, shape, F32))

    def sem(self, name):
        self.held.append(self.nc.alloc_semaphore(name))
        return self.held[-1]

    def clear(self):
        if self.held:
            self.nc.clear_and_free_semaphores(self.held)
            self.nc.all_engine_barrier()

    def sems(self, prefix, names):
        return [self.sem(f"{prefix}_{n}") for n in names.split()]


def bcast(ap, axis, n):
    shape = list(ap.shape)
    shape.insert(axis, n)
    return ap.unsqueeze(axis).to_broadcast(shape)


def looped(eng, body, tiles=NT):
    with eng.Fori(0, tiles // 2) as i:
        body(i * 2, 0)
        body(i * 2 + 1, 1)


def skewed(eng, early, mixed, late):
    early(0, 0)
    mixed(0, 0, 1, 1)
    with eng.Fori(0, (NT - 4) // 2) as i:
        mixed(i * 2 + 1, 1, i * 2 + 2, 0)
        mixed(i * 2 + 2, 0, i * 2 + 3, 1)
    mixed(NT - 3, 1, NT - 2, 0)
    mixed(NT - 2, 0, NT - 1, 1)
    late(NT - 1, 1)


def there(n, count=NT):
    return type(n) is not int or 0 <= n < count


def attention16(nc, C, tag, kind, w, ahead=None):
    cross, causal, biased = kind == "cross", kind == "causal", kind == "self"
    x, ident, hmask, neghalf = C["x"], C["ident"], C["hmask"], C["neghalf"]
    m = Store(nc)
    with m.stack:
        sb, ps = m.sb, m.ps
        wq, wk, wv, wo, loaded, nload = (w[k] for k in ("wq", "wk", "wv", "wo", "loaded", "count"))
        bq, bk = w.get("bq"), w.get("bk")
        bv, bo, gamma, beta = (w.get(k) for k in ("bv", "bo", "gamma", "beta"))
        st = sb(f"{tag}st", [P, 2, 6])
        mv = sb(f"{tag}mv", [P, 2, 4])
        hn = sb(f"{tag}hn", [P, 2, D])
        hT = sb(f"{tag}hT", [P, 2, DC, P])
        qT = sb(f"{tag}qT", [P, 2, DC, P])
        KB = sb(f"{tag}KB", [P, DC, HG, P])
        V2 = sb(f"{tag}V2", [P, 2, NP, 2, OW])
        sc = sb(f"{tag}sc", [P, 2, H, S])
        mx = sb(f"{tag}mx", [P, H])
        cs = sb(f"{tag}cs", [P, 2, DC, P])
        PT = sb(f"{tag}PT", [P, 2, NP, P])
        rs = sb(f"{tag}rs", [P, 3, H])
        cn = sb(f"{tag}cn", [P, 2, D])
        cT = sb(f"{tag}cT", [P, 2, DC, P])
        dl = sb(f"{tag}dl", [P, 2, D])
        dst = sb(f"{tag}dst", [P, 6])
        dmv = sb(f"{tag}dmv", [P, 4])
        p_qk = ps(f"{tag}pqk", [P, 2, DC, P])
        p_s = ps(f"{tag}ps", [P, 2, 512])
        p_t = ps(f"{tag}pt", [P, 2, 512])
        p_o = ps(f"{tag}po", [P, 2, 512])
        p_m = ps(f"{tag}pm", [P, 512])
        p_tp = p_t[:, :, :].rearrange("p a (n t) -> p (a n) t", t=P)
        p_sc = p_s[:, :, :].rearrange("p a (h k) -> p (a h) k", k=S)
        p_st = p_s[:, :, :].rearrange("p a (n t) -> p (a n) t", t=P)
        (var_ok, rstd_ok, hn_ok, turned, hT_ok, qk_ok, q_out, k_out, v_ok, v_out, s_ok, s_out,
         exp_ok, pt_ok, pt_out, o_ok, o_out, ct_ok, ct_out, proj_ok, zeroed, dve_step, dve_d,
         dvar_ok, drstd_ok, x_step, r_step, l_step, cs_ok, m_free, dn_ok, pool_step) = m.sems(tag, "var_ok rstd_ok hn_ok turned hT_ok qk_ok q_out k_out"
                                 " v_ok v_out s_ok s_out exp_ok pt_ok pt_out o_ok o_out ct_ok ct_out proj_ok"
                                 " zeroed dve_step dve_d dvar_ok drstd_ok x_step r_step l_step cs_ok m_free dn_ok pool_step")
        ctxT = C["ctxT"]
        block = m.stack.enter_context(nc.Block())

        if ahead:
            block.sync(ahead)

        @block.gpsimd
        def _(pool):
            pool.memset(V2[:, :, :, :, :], 0.0).then_inc(zeroed, 1)
            pool.wait_ge(zeroed, 1)
            for par in range(2):
                col = par * (HD + 1) + HD
                pool.memset(V2[64 * par:64 * par + 64, :, :, :, col:col + 1], 1.0).then_inc(zeroed, 1)

            def root(n, u):
                pool.wait_ge(var_ok, n + 1)
                pool.tensor_tensor(mv[:, u, 3:4], mv[:, u, 2:3], neghalf[:, 0:1], ALU.pow).then_inc(rstd_ok, 1)

            def droot(n, u):
                pool.wait_ge(dvar_ok, n + 1)
                pool.tensor_tensor(dmv[:, 3:4], dmv[:, 2:3], neghalf[:, 0:1], ALU.pow).then_inc(drstd_ok, 1)
                pool.wait_ge(dn_ok, n + 1)
                pool.tensor_tensor(dl[:, u, :], dl[:, u, :], gamma[:, :], ALU.mult).then_inc(pool_step, 1)
                pool.wait_ge(pool_step, n * 3 + 1)
                pool.tensor_tensor(dl[:, u, :], dl[:, u, :], beta[:, :], ALU.add).then_inc(pool_step, 1)
                pool.wait_ge(pool_step, n * 3 + 2)
                xt = x[:, bass.ds(n, 1), :].rearrange("p a d -> p (a d)")
                pool.tensor_tensor(xt, xt, dl[:, u, :], ALU.add).then_inc(pool_step, 1)

            def context(n, u):
                pool.tensor_copy(cs[:, u, :, :], ctxT[:, :, bass.ds(n * P, P)]).then_inc(cs_ok, 1)

            if not cross:
                looped(pool, root)
            else:
                root(0, 0)
                context(0, 0)
                root(1, 1)
                context(1, 1)

                def both(n, u):
                    pool.wait_ge(v_ok, n + 1)
                    context(n + 2, u)
                    root(n + 2, u)
                    droot(n, u)
                looped(pool, both, NT - 2)
                droot(NT - 2, 0)
                droot(NT - 1, 1)
                pool.wait_ge(pool_step, 3 * NT)

        @block.scalar
        def _(act):
            def h_out(n, u):
                act.wait_ge(turned, n + 1)
                act.activation(hT[:, u, :, :], p_tp[:, 0:DC, :], ACT.Copy).then_inc(hT_ok, 1)

            def q_copy(n, u):
                act.wait_ge(k_out, n + 1)
                for c in range(DC):
                    if causal:
                        ins = act.activation(qT[:, u, c, :], p_qk[:, 0, c, :], ACT.Copy)
                    else:
                        ins = act.activation(qT[:, u, c, :], p_qk[:, 0, c, :], ACT.Identity,
                                             bias=(bk if cross else bq)[:, c:c + 1])
                ins.then_inc(q_out, 1)

            def exps(n, u):
                act.wait_ge(s_out, n + 1)
                act.activation(sc[:, u, :, :], sc[:, u, :, :], ACT.Exp, scale=QSCALE).then_inc(exp_ok, 1)

            def pt_copy(n, u):
                act.wait_ge(pt_ok, n + 1)
                act.activation(PT[:, u, :, :], p_tp, ACT.Copy).then_inc(pt_out, 1)

            def ct_copy(n, u):
                act.wait_ge(ct_ok, n + 1)
                act.activation(cT[:, u, :, :], p_m[:, 0:D].rearrange("p (c t) -> p c t", c=DC), ACT.Copy).then_inc(ct_out, 1)

            act.wait_ge(loaded, nload)

            def early(n, u):
                h_out(0, 0)
                q_copy(0, 0)
                h_out(1, 1)
                exps(0, 0)

            def mixed(n, u, n1, u1):
                q_copy(n1, u1)
                if not cross:
                    pt_copy(n, u)
                ct_copy(n, u)
                if there(n + 2):
                    h_out(n + 2, u)
                exps(n1, u1)

            def late(n, u):
                if not cross:
                    pt_copy(n, u)
                ct_copy(n, u)

            skewed(act, early, mixed, late)

        @block.tensor
        def _(pe):
            def turn(n, u):
                pe.wait_ge(hn_ok, n + 1)
                for c in range(DC):
                    ins = pe.transpose(p_tp[:, c, :], hn[:, u, P * c:P * c + P], ident[:, :])
                ins.then_inc(turned, 1)

            def qk(n, u):
                pe.wait_ge(hT_ok, n + 1)
                if cross:
                    pe.wait_ge(cs_ok, n + 1)
                for slot in range(2):
                    weight = (wq, wk)[slot ^ cross]
                    for g in range(DC):
                        for c in range(DC):
                            src = hT[:, u, c, :]
                            if cross and slot == 0:
                                src = cs[:, u, c, :]
                            ins = pe.matmul(p_qk[:, slot, g, :], weight[:, c, P * g:P * g + P], src,
                                            start=(c == 0), stop=(c == DC - 1))
                ins.then_inc(qk_ok, 1)

            def values(n, u):
                for c in range(DC):
                    lhs = cs[:, u, c, :] if cross else hT[:, u, c, :]
                    ins = pe.matmul(p_m[:, 0:D], lhs, wv[:, c, :], start=(c == 0), stop=(c == DC - 1))
                ins.then_inc(v_ok, 1)

            def scores(n, u):
                pe.wait_ge(q_out, n + 1)
                pe.wait_ge(k_out, n + 1)
                for g in range(DC):
                    for b in range(2):
                        ts = slice(S * b, S * b + S)
                        if not cross:
                            ins = pe.matmul(p_sc[S * b:S * b + S, HG * g:HG * g + HG, :], qT[:, u, g, ts],
                                            KB[:, g, :, ts], start=True, stop=True)
                        else:
                            for par in range(2):
                                ins = pe.matmul(p_st[S * par:S * par + S, 4 * g:4 * g + 4, ts],
                                                qT[:, u, g, ts], KB[:, g, par:HG:2, ts], start=True, stop=True)
                ins.then_inc(s_ok, 1)

            def turn_probs(n, u):
                pe.wait_ge(exp_ok, n + 1)
                for pr in range(NP):
                    ins = pe.transpose(p_tp[:, pr, :], sc[:, u, 2 * pr:2 * pr + 2, :].rearrange("p a k -> p (a k)"), ident[:, :])
                ins.then_inc(pt_ok, 1)

            def pv(n, u):
                pe.wait_ge(exp_ok if cross else pt_out, n + 1)
                pe.wait_ge(v_out, n + 1)
                E = sc[:, u, :, :].rearrange("p (a c) k -> p a (c k)", c=2)
                for pr in range(NP):
                    lhs = E[:, pr, :] if cross else PT[:, u, pr, :]
                    ins = pe.matmul(p_o[:, pr // 4, 2 * OW * (pr % 4):2 * OW * (pr % 4 + 1)], lhs,
                                    V2[:, u, pr, :, :].rearrange("p b c -> p (b c)"), start=True, stop=True)
                ins.then_inc(o_ok, 1)

            def turn_ctx(n, u):
                pe.wait_ge(o_out, n + 1)
                for c in range(DC):
                    ins = pe.transpose(p_m[:, P * c:P * c + P], cn[:, u, P * c:P * c + P], ident[:, :])
                ins.then_inc(ct_ok, 1)

            def project(n, u):
                pe.wait_ge(ct_out, n + 1)
                for c in range(DC):
                    ins = pe.matmul(p_m[:, 0:D], cT[:, u, c, :], wo[:, c, :], start=(c == 0), stop=(c == DC - 1))
                ins.then_inc(proj_ok, 1)

            pe.wait_ge(loaded, nload)
            pe.wait_ge(zeroed, 3)

            def early(n, u):
                turn(0, 0)
                qk(0, 0)
                values(0, 0)
                scores(0, 0)
                turn(1, 1)

            def mixed(n, u, n1, u1):
                qk(n1, u1)
                if not cross:
                    turn_probs(n, u)
                if type(n) is int and n == 0:
                    pe.wait_ge(v_out, 1)
                else:
                    pe.wait_ge(m_free, n)
                values(n1, u1)
                pv(n, u)
                scores(n1, u1)
                pe.wait_ge(v_out, n1 + 1)
                turn_ctx(n, u)
                if there(n + 2):
                    turn(n + 2, u)
                project(n, u)

            def late(n, u):
                if not cross:
                    turn_probs(n, u)
                pv(n, u)
                pe.wait_ge(m_free, n)
                turn_ctx(n, u)
                project(n, u)

            skewed(pe, early, mixed, late)

        @block.vector
        def _(dve):
            def norm_a(n, u, src=None):
                dve.bn_stats(st[:, u, :], x[:, bass.ds(n, 1), :].rearrange("p a d -> p (a d)"))
                dve.drain()
                dve.bn_aggr(mv[:, u, 0:2], st[:, u, :]).then_inc(dve_step, 1)
                dve.wait_ge(dve_step, n + 1)
                dve.tensor_scalar(mv[:, u, 2:3], mv[:, u, 1:2], 1e-5, None, ALU.add).then_inc(var_ok, 1)

            def norm_b(n, u):
                dve.wait_ge(rstd_ok, n + 1)
                dve.tensor_scalar(hn[:, u, :], x[:, bass.ds(n, 1), :].rearrange("p a d -> p (a d)"), mv[:, u, 0:1], mv[:, u, 3:4],
                                  ALU.subtract, ALU.mult).then_inc(hn_ok, 1)

            def k_mask(n, u):
                dve.wait_ge(qk_ok, n + 1)
                for g in range(DC):
                    src = bcast(p_qk[:, 1, g, :], 1, HG)
                    mask = bcast(hmask[:, :], 2, P)
                    if causal:
                        ins = dve.tensor_tensor(KB[:, g, :, :], src, mask, ALU.mult)
                    else:
                        ins = dve.scalar_tensor_tensor(KB[:, g, :, :], src, (bq if cross else bk)[:, g:g + 1], mask, ALU.add, ALU.mult)
                ins.then_inc(k_out, 1)

            def v_copy(n, u):
                dve.wait_ge(v_ok, n + 1)
                for b in range(2):
                    for par in range(2):
                        src = p_m[S * b:S * b + S, 0:D].rearrange("p (n a d) -> p n a d", a=2, d=HD)[:, :, par, :]
                        dst = V2[64 * par:64 * par + 64, u, :, b, par * (HD + 1):par * (HD + 1) + HD]
                        if causal:
                            ins = dve.tensor_copy(dst, src)
                        else:
                            bias = bv[S * b:S * b + S, :].rearrange("p (n a d) -> p n a d", a=2, d=HD)[:, :, par, :]
                            ins = dve.tensor_tensor(dst, src, bias, ALU.add)
                ins.then_inc(v_out, 1)

            def soft(n, u):
                dve.wait_ge(s_ok, n + 1)
                if cross:
                    E = sc[:, u, :, :].rearrange("p (a c) k -> p a (c k)", c=2)
                    for b in range(2):
                        ts = slice(S * b, S * b + S)
                        hi = C["hi"][:, bass.ds(n * 2 + b, 1)]
                        ins = dve.tensor_scalar(E[:, :, ts], p_st[:, :, ts], -50.0 / QSCALE, hi, ALU.max, ALU.min)
                    ins.then_inc(s_out, 1)
                    return
                if causal:
                    dve.tensor_tensor(sc[:, u, :, :], p_sc, bcast(C["cmask"][:, :], 1, H), ALU.add).then_inc(dve_d, 1)
                    dve.wait_ge(dve_d, n * 2 + 1)
                src = sc[:, u, :, :] if causal else p_sc
                dve.tensor_reduce(mx[:, :], src, AX.X, ALU.max).then_inc(dve_d, 1)
                dve.wait_ge(dve_d, n * 2 + 2 if causal else n + 1)
                dve.tensor_tensor(sc[:, u, :, :], src, bcast(mx[:, :], 2, S), ALU.subtract).then_inc(s_out, 1)

            def o_norm(n, u):
                dve.wait_ge(o_ok, n + 1)
                O = p_o[:, :, 0:8 * OW].rearrange("p a (n b e d) -> p a n b e d", n=4, b=2, e=2)
                for b in range(2):
                    r = slice(S * b, S * b + S)
                    ins = dve.reciprocal(rs[r, 0, :].rearrange("p (a n e) -> p a n e", a=2, e=2), O[r, :, :, b, :, HD])
                    if cross:
                        ins = dve.tensor_copy(rs[r, 1, :].rearrange("p (a n e) -> p a n e", a=2, e=2), O[r, :, :, b, :, HD])
                steps = 4 if cross else 1
                ins.then_inc(x_step, 1)
                dve.wait_ge(x_step, n * steps + 1)
                if cross:
                    dve.tensor_tensor(rs[:, 1, :], rs[:, 1, :], rs[:, 0, :], ALU.mult).then_inc(x_step, 1)
                    dve.wait_ge(x_step, n * steps + 2)
                    dve.tensor_scalar(rs[:, 1, :], rs[:, 1, :], 1e-8, None, ALU.add).then_inc(x_step, 1)
                    dve.wait_ge(x_step, n * steps + 3)
                    dve.reciprocal(rs[:, 2, :], rs[:, 1, :]).then_inc(x_step, 1)
                    dve.wait_ge(x_step, n * steps + 4)
                    dve.tensor_tensor(rs[:, 0, :], rs[:, 0, :], rs[:, 2, :], ALU.mult).then_inc(r_step, 1)
                    dve.wait_ge(r_step, n + 1)
                for b in range(2):
                    r = slice(S * b, S * b + S)
                    for a in range(2):
                        dst = cn[r, u, P * a:P * a + P].rearrange("p (n e d) -> p n e d", e=2, d=HD)
                        rr = bcast(rs[r, 0, 8 * a:8 * a + 8].rearrange("p (n e) -> p n e", e=2), 3, HD)
                        ins = dve.tensor_tensor(dst, O[r, a, :, b, :, 0:HD], rr, ALU.mult)
                ins.then_inc(o_out, 1)

            def residual(n, u):
                xt = x[:, bass.ds(n, 1), :].rearrange("p a d -> p (a d)")
                dve.wait_ge(proj_ok, n + 1)
                if causal:
                    dve.tensor_tensor(xt, xt, p_m[:, 0:D], ALU.add).then_inc(m_free, 1)
                elif biased:
                    dve.tensor_tensor(dl[:, u, :], p_m[:, 0:D], bo[:, :], ALU.add).then_inc(m_free, 1)
                    dve.wait_ge(m_free, n + 1)
                    dve.tensor_tensor(xt, xt, dl[:, u, :], ALU.add)
                else:
                    dve.tensor_tensor(dl[:, u, :], p_m[:, 0:D], bo[:, :], ALU.add).then_inc(m_free, 1)
                    dve.wait_ge(m_free, n + 1)
                    dve.tensor_scalar(dl[:, u, :], dl[:, u, :], C["rs"][:, 0:1], None, ALU.mult)
                    dve.drain()
                    dve.bn_stats(dst[:, :], dl[:, u, :])
                    dve.drain()
                    dve.bn_aggr(dmv[:, 0:2], dst[:, :]).then_inc(l_step, 1)
                    dve.wait_ge(l_step, n + 1)
                    dve.tensor_scalar(dmv[:, 2:3], dmv[:, 1:2], 1e-5, None, ALU.add).then_inc(dvar_ok, 1)
                    dve.wait_ge(drstd_ok, n + 1)
                    dve.tensor_scalar(dl[:, u, :], dl[:, u, :], dmv[:, 0:1], dmv[:, 3:4], ALU.subtract, ALU.mult).then_inc(dn_ok, 1)

            dve.wait_ge(loaded, nload)
            dve.wait_ge(zeroed, 3)

            def early(n, u):
                norm_a(0, 0)
                norm_b(0, 0)
                norm_a(1, 1)
                norm_b(1, 1)
                k_mask(0, 0)
                v_copy(0, 0)
                soft(0, 0)

            def mixed(n, u, n1, u1):
                if there(n + 2):
                    norm_a(n + 2, u)
                k_mask(n1, u1)
                v_copy(n1, u1)
                o_norm(n, u)
                if there(n + 2):
                    norm_b(n + 2, u)
                soft(n1, u1)
                residual(n, u)

            def late(n, u):
                o_norm(n, u)
                residual(n, u)

            skewed(dve, early, mixed, late)


def moved(sp, done, pairs):
    for dst, src in pairs:
        sp.dma_start(dst, src).then_inc(done, 16)
    return 16 * len(pairs)


XH, KVH, XD = 16, 4, 128
XSCALE = float(1.0 / np.sqrt(np.float32(XD)))
RH = XD // 2
KEYS = 2 * S
NTAB = B + NT
TWO_PI = 6.283185307179586
PI_A = float(np.frombuffer(np.array([np.float32(TWO_PI).view(np.uint32) & 0xFFFF8000], np.uint32).tobytes(), np.float32)[0])
PI_B = float(np.frombuffer(np.array([np.float32(TWO_PI - PI_A).view(np.uint32) & 0xFFFF8000], np.uint32).tobytes(), np.float32)[0])
PI_C = float(np.float32(TWO_PI - PI_A - PI_B))
ROUND = 12582912.0
PI_MAX = 3.1415925


def rope_tables(nc, C, a):
    m = Store(nc)
    with m.stack:
        posi = m.sb("posi", [P, NTAB], I32)
        pos = m.sb("pos", [P, NTAB])
        inv = m.sb("inv", [P, RH])
        nw = m.sb("nw", [P, 2, XD])
        ang = m.sb("ang", [P, NTAB, RH])
        turns = m.sb("turns", [P, NTAB, RH])
        red = m.sb("red", [P, 2, NTAB, RH])
        tin, step, trig = m.sems("tab", "in step trig")
        tc, ts = C["tab_c"], C["tab_s"]
        with nc.Block() as block:
            @block.sync
            def _(sp):
                n = moved(sp, tin, [(posi[:, :], a["pos"]), (inv[:, :], a["inv"].to_broadcast([P, RH])),
                                    (nw[:, 0, :], a["kw"].to_broadcast([P, XD])), (nw[:, 1, :], a["qw"].to_broadcast([P, XD]))])
                sp.wait_ge(tin, n)

            @block.vector
            def _(dve):
                done = [0]

                def then(ins):
                    done[0] += 1
                    ins.then_inc(step, 1)
                    dve.wait_ge(step, done[0])

                dve.wait_ge(tin, 64)
                then(dve.tensor_copy(pos[:, :], posi[:, :]))
                then(dve.tensor_tensor(ang[:, :, :], bcast(pos[:, :], 2, RH), bcast(inv[:, :], 1, NTAB), ALU.mult))
                for k in range(2):
                    then(dve.tensor_scalar(turns[:, :, :], ang[:, :, :], 1.0 / TWO_PI, 0.25 * k, ALU.mult, ALU.add))
                    then(dve.tensor_scalar(turns[:, :, :], turns[:, :, :], ROUND, None, ALU.add))
                    then(dve.tensor_scalar(turns[:, :, :], turns[:, :, :], -ROUND, None, ALU.add))
                    then(dve.scalar_tensor_tensor(red[:, k, :, :], turns[:, :, :], -PI_A, ang[:, :, :], ALU.mult, ALU.add))
                    then(dve.scalar_tensor_tensor(red[:, k, :, :], turns[:, :, :], -PI_B, red[:, k, :, :], ALU.mult, ALU.add))
                    then(dve.scalar_tensor_tensor(red[:, k, :, :], turns[:, :, :], -PI_C, red[:, k, :, :], ALU.mult, ALU.add))
                    then(dve.tensor_scalar(red[:, k, :, :], red[:, k, :, :], k * TWO_PI / 4, PI_MAX, ALU.add, ALU.min))
                    then(dve.tensor_scalar(red[:, k, :, :], red[:, k, :, :], -PI_MAX, None, ALU.max))
                dve.wait_ge(trig, 1)
                for which, r in ((0, slice(0, B)), (1, slice(B, NTAB))):
                    n = r.stop - r.start
                    for half in range(2):
                        mine, other = slice(RH * half, RH * half + RH), slice(RH * (1 - half), RH * (1 - half) + RH)
                        dve.tensor_tensor(tc[:, r, mine], red[:, 1, r, :], bcast(nw[:, which, mine], 1, n), ALU.mult)
                        last = dve.scalar_tensor_tensor(ts[:, r, mine], red[:, 0, r, :], 2.0 * half - 1.0,
                                                        bcast(nw[:, which, other], 1, n), ALU.mult, ALU.mult)
                last.then_inc(step, 1)
                dve.wait_ge(step, done[0] + 1)

            @block.scalar
            def _(act):
                act.wait_ge(step, 18)
                act.activation(red[:, :, :, :], red[:, :, :, :], ACT.Sin).then_inc(trig, 1)
                act.wait_ge(trig, 1)


def attention128(nc, C, w):
    x, ident, neghalf, ctxT = C["x"], C["ident"], C["neghalf"], C["ctxT"]
    tc, ts = C["tab_c"], C["tab_s"]
    m = Store(nc)
    NSQ = XH + 2 * KVH
    with m.stack:
        sb, ps = m.sb, m.ps
        wq, wk, wv, wo, loaded = (w[k] for k in ("wq", "wk", "wv", "wo", "loaded"))
        st = sb("xst", [P, 2, 6])
        mv = sb("xmv", [P, 2, 4])
        hn = sb("xhn", [P, 2, D])
        kv = sb("xkv", [P, 2, DC, 2, KEYS])
        qr = sb("xqr", [P, NSQ, XD])
        t2 = sb("xt2", [P, 2, 4, XD])
        sq = sb("xsq", [P, 2, 4, XD])
        ss = sb("xss", [P, NSQ])
        sv = sb("xsv", [P, NSQ])
        sr = sb("xsr", [P, NSQ])
        V = sb("xV", [P, 2, 2, KVH, XD])
        QT = sb("xQT", [P, 2, XH, S])
        KT = sb("xKT", [P, 2 * KVH, KEYS])
        hT = sb("xhT", [P, 2, DC, P])
        E = sb("xE", [P, XH, KEYS])
        mx = sb("xmx", [P, XH])
        nb = sb("xnb", [P, XH])
        sm = sb("xsm", [P, XH])
        rc = sb("xrc", [P, XH])
        PT = sb("xPT", [P, 2, 4, P])
        OT = sb("xOT", [P, XH, 2, S])
        p_r = [ps(f"xpr{i}", [P, 4, XD]) for i in range(2)]
        p_t = [ps(f"xpt{i}", [P, 4, P]) for i in range(2)]
        p_s = [ps(f"xps{i}", [P, 4, KEYS]) for i in range(2)]
        p_o = [ps(f"xpo{i}", [P, 512]) for i in range(2)]
        (stat_ok, var_ok, rstd_ok, hn_ok, ctx_ok, r_ok, sq_ok, rope_ok, v_out, add_ok, ms_ok, sr_ok, ss_ok,
         scaled, t_ok, t_out, s_ok, max_ok, nb_ok, exp_ok, rc_ok, e_ok, o_ok, o_out, proj_ok, x_ok) = m.sems(
            "x", "stat_ok var_ok rstd_ok hn_ok ctx_ok r_ok sq_ok rope_ok v_out add_ok ms_ok sr_ok ss_ok"
                 " scaled t_ok t_out s_ok max_ok nb_ok exp_ok rc_ok e_ok o_ok o_out proj_ok x_ok")
        FIRST_T, STEP_T = 7, 11

        def t_base(n1):
            return 0 if type(n1) is int and n1 == 0 else n1 * STEP_T - (STEP_T - FIRST_T)

        block = m.stack.enter_context(nc.Block())

        @block.gpsimd
        def _(pool):
            def root(n, u):
                pool.wait_ge(var_ok, n + 1)
                pool.tensor_tensor(mv[:, u, 3:4], mv[:, u, 2:3], neghalf[:, 0:1], ALU.pow).then_inc(rstd_ok, 1)

            def context(n, u):
                pool.wait_ge(t_out, t_base(n) + 1)
                for c in range(DC):
                    pool.tensor_copy(kv[:, u, c, :, 0:S], ctxT[:, c, bass.ds(n * P, P)].rearrange("p (b k) -> p b k", b=2))
                for c in range(DC):
                    ins = pool.tensor_copy(kv[:, u, c, :, S:KEYS], hT[:, u, c, :].rearrange("p (b k) -> p b k", b=2))
                ins.then_inc(ctx_ok, 1)

            def adds(n, ahead=None):
                for k in range(6):
                    pool.wait_ge(rope_ok, n * 6 + k + 1)
                    blk = qr[:, 4 * k:4 * k + 4, :]
                    pool.tensor_tensor(blk, blk, t2[:, k % 2, :, :], ALU.add).then_inc(add_ok, 1)
                if ahead:
                    root(*ahead)
                pool.wait_ge(ms_ok, n + 1)
                pool.tensor_tensor(sr[:, :], sv[:, :], neghalf[:, 0:1].to_broadcast([P, NSQ]), ALU.pow).then_inc(sr_ok, 1)

            root(0, 0)
            root(1, 1)
            context(0, 0)
            adds(0)

            def body(n, u):
                context(n + 1, 1 - u)
                adds(n + 1, (n + 2, u))

            looped(pool, body, NT - 2)
            n = NT - 2
            context(n + 1, 1)
            adds(n + 1)

        @block.scalar
        def _(act):
            def turned(j, dst, src):
                act.wait_ge(t_ok, j + 1)
                act.activation(dst, src, ACT.Copy).then_inc(t_out, 1)

            def h_out(n, u, j, bank):
                turned(j, hT[:, u, :, :], p_t[bank][:, 0:DC, :])

            def qk_out(j, i, bank):
                if i < 4:
                    dst = QT[:, :, 4 * i:4 * i + 4, :]
                    turned(j, dst.rearrange("p b h q -> p h b q"), p_t[bank][:, :, :].rearrange("p h (b q) -> p h b q", b=2))
                else:
                    turned(j, KT[:, 4 * (i - 4):4 * (i - 4) + 4, :], p_t[bank][:, :, :])

            def square(n, k):
                act.wait_ge(r_ok, n * 8 + k + 1)
                act.activation(sq[:, SQI[k] % 2, :, :], p_r[k % 2][:, :, :], ACT.Square).then_inc(sq_ok, 1)

            def v_copy(n, u, k):
                act.wait_ge(r_ok, n * 8 + k + 1)
                act.activation(V[:, u, (k - 5) // 2, :, :], p_r[k % 2][:, :, :], ACT.Copy).then_inc(v_out, 1)

            def exps(n, k):
                act.wait_ge(nb_ok, n * 4 + k + 1)
                for i in range(4):
                    c = 4 * k + i
                    ins = act.activation(E[:, c, :], p_s[k % 2][:, i, :], ACT.Exp, bias=nb[:, c:c + 1], scale=XSCALE,
                                         accum_out=sm[:, c:c + 1])
                ins.then_inc(exp_ok, 1)

            def pt_copy(n, k, j, bank):
                turned(j, PT[:, k % 2, :, :], p_t[bank][:, :, :])

            def o_copy(n, u, k):
                act.wait_ge(o_ok, n * 4 + k + 1)
                act.activation(OT[:, 8 * (k % 2):8 * (k % 2) + 8, k // 2, :],
                               p_o[(u + k) % 2][:, :].rearrange("p (h q) -> p h q", q=S), ACT.Copy).then_inc(o_out, 1)

            def early(n, u):
                h_out(0, 0, 0, 0)
                for k in (0, 1, 2, 3, 4):
                    square(0, k)
                v_copy(0, 0, 5)
                square(0, 6)
                v_copy(0, 0, 7)
                for i in range(6):
                    qk_out(1 + i, i, (1 + i) % 2)

            def mixed(n, u, n1, u1):
                base = t_base(n1)
                bank = lambda k: (u + 1 + k) % 2
                h_out(n1, u1, base, bank(0))
                exps(n, 0)
                exps(n, 1)
                square(n1, 0)
                square(n1, 1)
                pt_copy(n, 0, base + 1, bank(1))
                square(n1, 2)
                pt_copy(n, 1, base + 2, bank(2))
                square(n1, 3)
                o_copy(n, u, 0)
                exps(n, 2)
                o_copy(n, u, 1)
                exps(n, 3)
                square(n1, 4)
                v_copy(n1, u1, 5)
                pt_copy(n, 2, base + 3, bank(3))
                square(n1, 6)
                v_copy(n1, u1, 7)
                pt_copy(n, 3, base + 4, bank(4))
                o_copy(n, u, 2)
                o_copy(n, u, 3)
                for i in range(6):
                    qk_out(base + 5 + i, i, bank(5 + i))

            def late(n, u):
                base = t_base(NT)
                bank = lambda k: (base + k) % 2
                exps(n, 0)
                exps(n, 1)
                pt_copy(n, 0, base, bank(0))
                pt_copy(n, 1, base + 1, bank(1))
                o_copy(n, u, 0)
                exps(n, 2)
                o_copy(n, u, 1)
                exps(n, 3)
                pt_copy(n, 2, base + 2, bank(2))
                pt_copy(n, 3, base + 3, bank(3))
                o_copy(n, u, 2)
                o_copy(n, u, 3)

            skewed(act, early, mixed, late)

        @block.tensor
        def _(pe):
            def turn_h(n, u, j, bank):
                pe.wait_ge(hn_ok, n + 1)
                for c in range(DC):
                    ins = pe.transpose(p_t[bank][:, c, :], hn[:, u, P * c:P * c + P], ident[:, :])
                ins.then_inc(t_ok, 1)

            def fill(n, u, k, first=False):
                freed = {0: (rope_ok, n * 6), 1: (v_out, n * 2), 2: (rope_ok, n * 6 + 1), 3: (rope_ok, n * 6 + 2),
                         4: (rope_ok, n * 6 + 3), 5: (rope_ok, n * 6 + 4), 6: (rope_ok, n * 6 + 5), 7: (v_out, n * 2 + 1)}
                pe.wait_ge(*freed[k])
                for c in range(DC):
                    if k < 4:
                        lhs, rhs = hT[:, u, c, :], wq[:, c, 512 * k:512 * k + 512]
                    else:
                        lhs, rhs = kv[:, u, c, (k - 4) // 2, :], (wk, wv)[k % 2][:, c, :]
                    ins = pe.matmul(p_r[k % 2][:, :, :].rearrange("p h d -> p (h d)"), lhs, rhs, start=(c == 0), stop=(c == DC - 1))
                ins.then_inc(r_ok, 1)

            def scores(n, k):
                b, half = k // 2, k % 2
                pe.wait_ge(exp_ok, n * 4 + max(k - 1, 0))
                for i in range(4):
                    h = 8 * half + 2 * i
                    ins = pe.matmul(p_s[k % 2][:, i, :], QT[:, b, h:h + 2, :].rearrange("p h q -> p (h q)"),
                                    KT[:, KVH * b + h // 4, :], start=True, stop=True)
                ins.then_inc(s_ok, 1)

            def turn_probs(n, k, j, bank):
                pe.wait_ge(e_ok, n * 4 + k + 1)
                pe.wait_ge(t_out, j - 1)
                for i in range(4):
                    ins = pe.transpose(p_t[bank][:, i, :], E[:, 4 * k + i, :], ident[:, :])
                ins.then_inc(t_ok, 1)

            def pv(n, u, k, j):
                pe.wait_ge(t_out, j + 1)
                if k == 1:
                    pe.wait_ge(x_ok, n)
                else:
                    pe.wait_ge(o_out, n * 4 + max(k - 1, 0))
                if k == 0:
                    pe.wait_ge(v_out, n * 2 + 2)
                for g in range(2):
                    ins = pe.matmul(p_o[(u + k) % 2][:, 256 * g:256 * g + 256], V[:, u, k // 2, 2 * (k % 2) + g, :],
                                    PT[:, k % 2, 2 * g:2 * g + 2, :].rearrange("p i q -> p (i q)"), start=True, stop=True)
                ins.then_inc(o_ok, 1)

            def project(n, u):
                pe.wait_ge(o_out, n * 4 + 4)
                for h in range(XH):
                    ins = pe.matmul(p_o[u][:, 0:D], OT[:, h, :, :].rearrange("p b q -> p (b q)"), wo[:, h, :],
                                    start=(h == 0), stop=(h == XH - 1))
                ins.then_inc(proj_ok, 1)

            def turn_qk(n, j0, bank):
                for i in range(6):
                    pe.wait_ge(scaled, n * 6 + i + 1)
                    pe.wait_ge(t_out, j0 + i - 1)
                    for c in range(4):
                        ins = pe.transpose(p_t[bank(i)][:, c, :], qr[:, 4 * i + c, :], ident[:, :])
                    ins.then_inc(t_ok, 1)

            pe.wait_ge(loaded, 64)

            def early(n, u):
                turn_h(0, 0, 0, 0)
                pe.wait_ge(t_out, 1)
                for k in range(8):
                    if k == 4:
                        pe.wait_ge(ctx_ok, 1)
                    fill(0, 0, k)
                turn_qk(0, 1, lambda i: (1 + i) % 2)

            def mixed(n, u, n1, u1):
                base = t_base(n1)
                bank = lambda k: (u + 1 + k) % 2
                pe.wait_ge(t_out, base - 1)
                turn_h(n1, u1, base, bank(0))
                pe.wait_ge(t_out, base)
                scores(n, 0)
                scores(n, 1)
                pe.wait_ge(t_out, base + 1)
                fill(n1, u1, 0)
                fill(n1, u1, 1)
                turn_probs(n, 0, base + 1, bank(1))
                fill(n1, u1, 2)
                turn_probs(n, 1, base + 2, bank(2))
                fill(n1, u1, 3)
                pv(n, u, 0, base + 1)
                scores(n, 2)
                pv(n, u, 1, base + 2)
                scores(n, 3)
                pe.wait_ge(ctx_ok, n1 + 1)
                fill(n1, u1, 4)
                fill(n1, u1, 5)
                turn_probs(n, 2, base + 3, bank(3))
                fill(n1, u1, 6)
                fill(n1, u1, 7)
                turn_probs(n, 3, base + 4, bank(4))
                pv(n, u, 2, base + 3)
                pv(n, u, 3, base + 4)
                project(n, u)
                turn_qk(n1, base + 5, lambda i: bank(5 + i))

            def late(n, u):
                base = t_base(NT)
                bank = lambda k: (base + k) % 2
                pe.wait_ge(t_out, base)
                scores(n, 0)
                scores(n, 1)
                turn_probs(n, 0, base, bank(0))
                turn_probs(n, 1, base + 1, bank(1))
                pv(n, u, 0, base)
                scores(n, 2)
                pv(n, u, 1, base + 1)
                scores(n, 3)
                turn_probs(n, 2, base + 2, bank(2))
                turn_probs(n, 3, base + 3, bank(3))
                pv(n, u, 2, base + 2)
                pv(n, u, 3, base + 3)
                project(n, u)

            skewed(pe, early, mixed, late)

        @block.vector
        def _(dve):
            def tile_of(n):
                return x[:, bass.ds(n, 1), :].rearrange("p a d -> p (a d)")

            def norm(n, u):
                dve.bn_stats(st[:, u, :], tile_of(n))
                dve.drain()
                dve.bn_aggr(mv[:, u, 0:2], st[:, u, :]).then_inc(stat_ok, 1)
                dve.wait_ge(stat_ok, n + 1)
                dve.tensor_scalar(mv[:, u, 2:3], mv[:, u, 1:2], 1e-5, None, ALU.add).then_inc(var_ok, 1)
                dve.wait_ge(rstd_ok, n + 1)
                dve.tensor_scalar(hn[:, u, :], tile_of(n), mv[:, u, 0:1], mv[:, u, 3:4], ALU.subtract, ALU.mult).then_inc(hn_ok, 1)

            def rope(n, i):
                k = RING[i]
                src, blk = p_r[k % 2], qr[:, 4 * i:4 * i + 4, :]
                row = n + B if i < 4 else n * 2 + (i - 4)
                dve.wait_ge(sq_ok, n * 6 + i + 1)
                if type(n) is not int or n * 6 + i > 1:
                    dve.wait_ge(add_ok, n * 6 + i - 1)
                cosw = tc[:, bass.ds(row, 1), :].rearrange("p a d -> p (a d)")
                sinw = ts[:, bass.ds(row, 1), :].rearrange("p a d -> p (a d)")
                dve.tensor_reduce(ss[:, 4 * i:4 * i + 4], sq[:, i % 2, :, :], AX.X, ALU.add).then_inc(ss_ok, 1)
                dve.tensor_tensor(blk, src[:, :, :], bcast(cosw, 1, 4), ALU.mult)
                for half in range(2):
                    mine, other = slice(RH * half, RH * half + RH), slice(RH * (1 - half), RH * (1 - half) + RH)
                    ins = dve.tensor_tensor(t2[:, i % 2, :, mine], src[:, :, other], bcast(sinw[:, mine], 1, 4), ALU.mult)
                ins.then_inc(rope_ok, 1)

            def rms(n):
                dve.wait_ge(ss_ok, n * 6 + 6)
                dve.tensor_scalar(sv[:, :], ss[:, :], 1.0 / XD, 1e-6, ALU.mult, ALU.add).then_inc(ms_ok, 1)
                dve.wait_ge(sr_ok, n + 1)
                dve.wait_ge(add_ok, n * 6 + 6)
                for i in range(6):
                    blk = qr[:, 4 * i:4 * i + 4, :]
                    dve.tensor_tensor(blk, blk, bcast(sr[:, 4 * i:4 * i + 4], 2, XD), ALU.mult).then_inc(scaled, 1)

            def maxes(n, k):
                c = slice(4 * k, 4 * k + 4)
                dve.wait_ge(s_ok, n * 4 + k + 1)
                dve.tensor_reduce(mx[:, c], p_s[k % 2][:, :, :], AX.X, ALU.max).then_inc(max_ok, 1)
                dve.wait_ge(max_ok, n * 4 + k + 1)
                dve.tensor_scalar(nb[:, c], mx[:, c], -XSCALE, None, ALU.mult).then_inc(nb_ok, 1)

            def normalise(n, k):
                c = slice(4 * k, 4 * k + 4)
                dve.wait_ge(exp_ok, n * 4 + k + 1)
                dve.reciprocal(rc[:, c], sm[:, c]).then_inc(rc_ok, 1)
                dve.wait_ge(rc_ok, n * 4 + k + 1)
                dve.tensor_tensor(E[:, c, :], E[:, c, :], bcast(rc[:, c], 2, KEYS), ALU.mult).then_inc(e_ok, 1)

            def residual(n, u):
                dve.wait_ge(proj_ok, n + 1)
                dve.tensor_tensor(tile_of(n), tile_of(n), p_o[u][:, 0:D], ALU.add).then_inc(x_ok, 1)

            def early(n, u):
                norm(0, 0)
                norm(1, 1)
                for i in range(6):
                    rope(0, i)
                rms(0)

            def mixed(n, u, n1, u1):
                maxes(n, 0)
                maxes(n, 1)
                rope(n1, 0)
                normalise(n, 0)
                rope(n1, 1)
                normalise(n, 1)
                rope(n1, 2)
                maxes(n, 2)
                rope(n1, 3)
                maxes(n, 3)
                normalise(n, 2)
                rope(n1, 4)
                normalise(n, 3)
                rope(n1, 5)
                if there(n + 2):
                    norm(n + 2, u)
                rms(n1)
                residual(n, u)

            def late(n, u):
                maxes(n, 0)
                maxes(n, 1)
                normalise(n, 0)
                normalise(n, 1)
                maxes(n, 2)
                maxes(n, 3)
                normalise(n, 2)
                normalise(n, 3)
                residual(n, u)

            skewed(dve, early, mixed, late)


SQI = {0: 0, 1: 1, 2: 2, 3: 3, 4: 4, 6: 5}
RING = (0, 1, 2, 3, 4, 6)


E1, K1, I1 = 64, 8, 64
NPAIR = E1 // 2 + 1
WROWS = 2 * NPAIR
CH = 512
NCH = B * S // CH
H_UP, W_UP = 32.0, 64.0
PASSES = ((0, 0), (1, 0), (0, 1))


def moe_dense(nc, C, a):
    x, ident, neghalf = C["x"], C["ident"], C["neghalf"]
    m = Store(nc)
    wt_dram = nc.dram_tensor("wt_dram", [WROWS, B * S], F32, kind="Internal").ap()
    with m.stack:
        hs = m.sb("m1hs", [P, 2, DC, B * S], F16)
        r = Store(nc)
        with r.stack:
            gate = r.sb("m1gate", [P, DC, E1 + 1])
            st = r.sb("m1st", [P, 2, 6])
            mv = r.sb("m1mv", [P, 2, 4])
            hn = r.sb("m1hn", [P, 2, D])
            hT = r.sb("m1hT", [P, 2, DC, P])
            lg = r.sb("m1lg", [P, E1 + 1])
            top = r.sb("m1top", [P, 8])
            nb = r.sb("m1nb", [P, 1])
            ex = r.sb("m1ex", [P, E1 + 1])
            sm = r.sb("m1sm", [P, 2])
            rc = r.sb("m1rc", [P, 2])
            W = r.sb("m1W", [P, 2, WROWS])
            WT = r.sb("m1WT", [WROWS, B * S])
            p_t = [r.ps(f"m1pt{i}", [P, DC, P]) for i in range(2)]
            p_l = [r.ps(f"m1pl{i}", [P, 512]) for i in range(2)]
            p_w = [r.ps(f"m1pw{i}", [P, 512]) for i in range(2)]
            (loaded, stat_ok, var_ok, rstd_ok, hn_ok, t_ok, hT_ok, hi_ok, lo_ok, l_ok, top_ok, nb_ok, ex_ok,
             step, rc_ok, W_ok, w_ok, WT_ok, stored) = r.sems(
                "m1", "loaded stat_ok var_ok rstd_ok hn_ok t_ok hT_ok hi_ok lo_ok l_ok top_ok nb_ok ex_ok"
                      " step rc_ok W_ok w_ok WT_ok stored")
            with nc.Block() as block:
                @block.sync
                def _(sp):
                    moved(sp, loaded, [(gate[:, :, :], a["m1_gate"])])
                    sp.wait_ge(WT_ok, NT)
                    sp.dma_start(wt_dram, WT[:, :]).then_inc(stored, 16)
                    sp.wait_ge(stored, 16)

                @block.gpsimd
                def _(pool):
                    def root(n, u):
                        pool.wait_ge(var_ok, n + 1)
                        pool.tensor_tensor(mv[:, u, 3:4], mv[:, u, 2:3], neghalf[:, 0:1], ALU.pow).then_inc(rstd_ok, 1)
                    looped(pool, root)

                @block.scalar
                def _(act):
                    def inputs(n, u):
                        act.wait_ge(t_ok, n + 1)
                        act.activation(hT[:, u, :, :], p_t[u][:, :, :], ACT.Copy).then_inc(hT_ok, 1)
                        act.activation(hs[:, 0, :, bass.ds(n * P, P)], p_t[u][:, :, :], ACT.Copy, scale=H_UP).then_inc(hi_ok, 1)

                    def weights(n, u):
                        act.wait_ge(nb_ok, n + 1)
                        act.activation(ex[:, 0:E1], lg[:, 0:E1], ACT.Exp, bias=nb[:, 0:1])
                        act.activation(ex[:, E1:E1 + 1], lg[:, E1:E1 + 1], ACT.Exp, scale=-1.0).then_inc(ex_ok, 1)

                    def out(n, u):
                        act.wait_ge(w_ok, n + 1)
                        act.activation(WT[:, bass.ds(n * P, P)], p_w[u][0:WROWS, 0:P], ACT.Copy).then_inc(WT_ok, 1)

                    def early(n, u):
                        inputs(n, u)
                        weights(n, u)

                    def mixed(n, u, n1, u1):
                        inputs(n1, u1)
                        out(n, u)
                        weights(n1, u1)
                    skewed(act, early, mixed, out)

                @block.tensor
                def _(pe):
                    def turn(n, u):
                        pe.wait_ge(hn_ok, n + 1)
                        pe.wait_ge(lo_ok, n - 1 if type(n) is not int else max(n - 1, 0))
                        for c in range(DC):
                            ins = pe.transpose(p_t[u][:, c, :], hn[:, u, P * c:P * c + P], ident[:, :])
                        ins.then_inc(t_ok, 1)

                    def route(n, u):
                        pe.wait_ge(hT_ok, n + 1)
                        for c in range(DC):
                            ins = pe.matmul(p_l[u][:, 0:E1 + 1], hT[:, u, c, :], gate[:, c, :], start=(c == 0), stop=(c == DC - 1))
                        ins.then_inc(l_ok, 1)

                    def turn_w(n, u):
                        pe.wait_ge(W_ok, n + 1)
                        pe.transpose(p_w[u][0:WROWS, 0:P], W[:, u, :], ident[:, :]).then_inc(w_ok, 1)

                    pe.wait_ge(loaded, 16)

                    def early(n, u):
                        turn(0, 0)
                        route(0, 0)
                        turn(1, 1)

                    def mixed(n, u, n1, u1):
                        route(n1, u1)
                        if there(n + 2):
                            turn(n + 2, u)
                        turn_w(n, u)
                    skewed(pe, early, mixed, turn_w)

                @block.vector
                def _(dve):
                    def tile_of(n):
                        return x[:, bass.ds(n, 1), :].rearrange("p a d -> p (a d)")

                    def norm(n, u):
                        dve.bn_stats(st[:, u, :], tile_of(n))
                        dve.drain()
                        dve.bn_aggr(mv[:, u, 0:2], st[:, u, :]).then_inc(stat_ok, 1)
                        dve.wait_ge(stat_ok, n + 1)
                        dve.tensor_scalar(mv[:, u, 2:3], mv[:, u, 1:2], 1e-5, None, ALU.add).then_inc(var_ok, 1)
                        dve.wait_ge(rstd_ok, n + 1)
                        dve.tensor_scalar(hn[:, u, :], tile_of(n), mv[:, u, 0:1], mv[:, u, 3:4], ALU.subtract, ALU.mult).then_inc(hn_ok, 1)

                    def low(n, u):
                        dve.wait_ge(hi_ok, n + 1)
                        cols = bass.ds(n * P, P)
                        dve.scalar_tensor_tensor(hs[:, 1, :, cols], p_t[u][:, :, :], H_UP, hs[:, 0, :, cols],
                                                 ALU.mult, ALU.subtract).then_inc(lo_ok, 1)

                    def weights(n, u):
                        def then(ins, k):
                            ins.then_inc(step, 1)
                            dve.wait_ge(step, n * 4 + k)
                        dve.wait_ge(l_ok, n + 1)
                        dve.tensor_copy(lg[:, :], p_l[u][:, 0:E1 + 1])
                        dve.drain()
                        dve.max(top[:, :], lg[:, 0:E1]).then_inc(top_ok, 1)
                        dve.wait_ge(top_ok, n + 1)
                        dve.tensor_scalar(nb[:, :], top[:, 0:1], -1.0, None, ALU.mult).then_inc(nb_ok, 1)
                        dve.wait_ge(ex_ok, n + 1)
                        then(dve.scalar_tensor_tensor(ex[:, 0:E1], lg[:, 0:E1], top[:, K1 - 1:K1], ex[:, 0:E1], ALU.is_ge, ALU.mult), 1)
                        dve.tensor_reduce(sm[:, 0:1], ex[:, 0:E1], AX.X, ALU.add)
                        then(dve.tensor_scalar(sm[:, 1:2], ex[:, E1:E1 + 1], 1.0, None, ALU.add), 2)
                        then(dve.reciprocal(rc[:, :], sm[:, :]), 3)
                        dve.tensor_scalar(W[:, u, 0:E1], ex[:, 0:E1], rc[:, 0:1], None, ALU.mult)
                        then(dve.tensor_copy(W[:, u, E1:E1 + 1], rc[:, 1:2]), 4)
                        dve.memset(W[:, u, E1 + 1:WROWS], 0.0).then_inc(W_ok, 1)

                    def early(n, u):
                        norm(0, 0)
                        norm(1, 1)
                        low(0, 0)
                        weights(0, 0)

                    def mixed(n, u, n1, u1):
                        if there(n + 2):
                            norm(n + 2, u)
                        low(n1, u1)
                        weights(n1, u1)
                    skewed(dve, early, mixed, lambda n, u: None)

        yT = m.sb("m1yT", [P, DC, B * S])
        e = Store(nc)
        with e.stack:
            NR = 2
            raw = e.sb("m1raw", [P, NR, DC * 2 * P + D])
            ws = e.sb("m1ws", [P, NR, 2, DC * 2 * P + D], F16)
            Wb = e.sb("m1Wb", [P, NR, B * S])
            sg = e.sb("m1sg", [P, 2, CH])
            ac = e.sb("m1ac", [P, 2, CH])
            ap = e.sb("m1ap", [P, 2, 2, CH], F16)
            p_g = [e.ps(f"m1pg{i}", [P, CH]) for i in range(2)]
            p_u = [e.ps(f"m1pu{i}", [P, CH]) for i in range(2)]
            p_y = [[e.ps(f"m1py{c}{q}", [P, CH]) for q in range(NCH)] for c in range(DC)]
            (hi_ok, prep_ok, g_ok, u_ok, silu_ok, sw_ok, act_ok, ah_ok, al_ok, y_ok, out_ok) = e.sems(
                "e1", "hi_ok prep_ok g_ok u_ok silu_ok sw_ok act_ok ah_ok al_ok y_ok out_ok")
            w_in = [e.sem(f"e1_w_in{u}") for u in range(NR)]
            b_in = [e.sem(f"e1_b_in{u}") for u in range(NR)]
            GU = DC * 2 * P

            def part(ap_, u, s, c, which):
                return ap_[:, u, s, P * (2 * c + which):P * (2 * c + which) + P]

            def over_pairs(eng, body, lead=0):
                body(0, 0, True, False)
                with eng.Fori(0, (NPAIR - 3) // 2) as i:
                    body(i * 2 + 1, 1, False, False)
                    body(i * 2 + 2, 0, False, False)
                body(NPAIR - 2, 1, False, False)
                body(NPAIR - 1, 0, False, True)

            with nc.Block() as block:
                @block.sync
                def _(sp):
                    def load(p, u, first, last):
                        if not first and not (type(p) is int and p < NR):
                            sp.wait_ge(prep_ok, p - 1)
                        sp.dma_start(raw[:, u, :], a["m1_w"][bass.ds(p, 1), :, :].rearrange("a p n -> p (a n)")).then_inc(w_in[u], 16)
                        if not first and not (type(p) is int and p < NR):
                            sp.wait_ge(sw_ok, p * 2 - 2)
                        for h in range(2):
                            sp.dma_start(Wb[64 * h:64 * h + 64, u, :],
                                         wt_dram[bass.ds(p * 2 + h, 1), :].to_broadcast([64, B * S])).then_inc(b_in[u], 16)
                    load(0, 0, True, False)
                    load(1, 1, True, False)
                    with sp.Fori(0, (NPAIR - 3) // 2) as i:
                        load(i * 2 + 2, 0, False, False)
                        load(i * 2 + 3, 1, False, False)
                    load(NPAIR - 1, 0, False, True)

                @block.gpsimd
                def _(pool):
                    def low(p, u, first, last):
                        pool.wait_ge(hi_ok, p + 1)
                        pool.tensor_tensor(ws[:, u, 1, :], raw[:, u, :], ws[:, u, 0, :], ALU.subtract).then_inc(prep_ok, 1)
                    over_pairs(pool, low)

                @block.scalar
                def _(act):
                    def high(p, u, early=False):
                        act.wait_ge(w_in[u], (p - u) * 8 + 16)
                        if not early:
                            act.wait_ge(y_ok, p * 2 - 2)
                        act.activation(ws[:, u, 0, :], raw[:, u, :], ACT.Copy, scale=W_UP)
                        act.activation(raw[:, u, :], raw[:, u, :], ACT.Copy, scale=W_UP).then_inc(hi_ok, 1)

                    def silu(j, q):
                        act.wait_ge(g_ok, j + 1)
                        act.activation(sg[:, q, :], p_g[q][:, :], ACT.Silu, scale=1.0 / (H_UP * W_UP)).then_inc(silu_ok, 1)

                    def ahigh(j, q):
                        act.wait_ge(act_ok, j + 1)
                        act.activation(ap[:, q, 0, :], ac[:, q, :], ACT.Copy).then_inc(ah_ok, 1)

                    high(0, 0, True)
                    silu(0, 0)
                    high(1, 1, True)

                    def pair(p, u, first, last):
                        silu(p * 2 + 1, 1)
                        ahigh(p * 2, 0)
                        if not last:
                            if not first:
                                high(p + 1, 1 - u)
                            silu(p * 2 + 2, 0)
                        ahigh(p * 2 + 1, 1)
                    over_pairs(act, pair)
                    for c in range(DC):
                        for q in range(NCH):
                            act.wait_ge(y_ok, 2 * NPAIR)
                            ins = act.activation(yT[:, c, CH * q:CH * q + CH], p_y[c][q][:, :], ACT.Copy, scale=1.0 / W_UP)
                    ins.then_inc(out_ok, 1)
                    act.wait_ge(out_ok, 1)

                @block.tensor
                def _(pe):
                    def hidden(p, u, q, first=False):
                        j = p * 2 + q
                        pe.wait_ge(prep_ok, p + 1)
                        if not (type(p) is int and p == 0):
                            pe.wait_ge(act_ok, j - 1)
                        for which, bank, ok in ((0, p_g[q], g_ok), (1, p_u[q], u_ok)):
                            k = 0
                            for c in range(DC):
                                for sw, sh in PASSES:
                                    ins = pe.matmul(bank[:, :], part(ws, u, sw, c, which), hs[:, sh, c, CH * q:CH * q + CH],
                                                    start=(k == 0), stop=(k == 5))
                                    k += 1
                            ins.then_inc(ok, 1)

                    def down(p, u, q, first, last):
                        j = p * 2 + q
                        pe.wait_ge(al_ok, j + 1)
                        for c in range(DC):
                            for k, (sw, sa) in enumerate(PASSES):
                                ins = pe.matmul(p_y[c][q][:, :], ws[:, u, sw, GU + P * c:GU + P * c + P], ap[:, q, sa, :],
                                                start=(first and k == 0), stop=(last and k == 2), skip_group_check=True)
                        ins.then_inc(y_ok, 1)

                    hidden(0, 0, 0)

                    def pair(p, u, first, last):
                        hidden(p, u, 1)
                        down(p, u, 0, first, last)
                        if not last:
                            hidden(p + 1, 1 - u, 0)
                        down(p, u, 1, first, last)
                    over_pairs(pe, pair)

                @block.vector
                def _(dve):
                    def weigh(p, u, q):
                        j = p * 2 + q
                        dve.wait_ge(b_in[u], (p - u) * 16 + 32)
                        dve.wait_ge(silu_ok, j + 1)
                        dve.tensor_tensor(sg[:, q, :], sg[:, q, :], Wb[:, u, CH * q:CH * q + CH], ALU.mult).then_inc(sw_ok, 1)

                    def times_up(p, u, q):
                        j = p * 2 + q
                        dve.wait_ge(sw_ok, j + 1)
                        dve.wait_ge(u_ok, j + 1)
                        dve.scalar_tensor_tensor(ac[:, q, :], p_u[q][:, :], 1.0 / (H_UP * W_UP), sg[:, q, :],
                                                 ALU.mult, ALU.mult).then_inc(act_ok, 1)

                    def alow(p, u, q):
                        j = p * 2 + q
                        dve.wait_ge(ah_ok, j + 1)
                        dve.tensor_tensor(ap[:, q, 1, :], ac[:, q, :], ap[:, q, 0, :], ALU.subtract).then_inc(al_ok, 1)

                    weigh(0, 0, 0)
                    times_up(0, 0, 0)

                    def pair(p, u, first, last):
                        alow(p, u, 0)
                        weigh(p, u, 1)
                        times_up(p, u, 1)
                        alow(p, u, 1)
                        if not last:
                            weigh(p + 1, 1 - u, 0)
                            times_up(p + 1, 1 - u, 0)
                    over_pairs(dve, pair)
        add_transposed(nc, C, yT, "m1")


def add_transposed(nc, C, yT, tag):
    m = Store(nc)
    with m.stack:
        p_t = [m.ps(f"{tag}pz{i}", [P, D]) for i in range(4)]
        t_ok, x_ok = m.sems(f"{tag}z", "t_ok x_ok")
        with nc.Block() as block:
            @block.tensor
            def _(pe):
                for n in range(NT):
                    if n >= 4:
                        pe.wait_ge(x_ok, n - 3)
                    for c in range(DC):
                        ins = pe.transpose(p_t[n % 4][:, P * c:P * c + P], yT[:, c, P * n:P * n + P], C["ident"][:, :])
                    ins.then_inc(t_ok, 1)

            @block.vector
            def _(dve):
                for n in range(NT):
                    dve.wait_ge(t_ok, n + 1)
                    ins = dve.tensor_tensor(C["x"][:, n, :], C["x"][:, n, :], p_t[n % 4][:, :], ALU.add)
                    ins.then_inc(x_ok, 1)
                dve.wait_ge(x_ok, NT)


E0, K0, I0 = 32, 4, 128
CAP = 2 * B * S * K0 // E0
SLOTS = E0 * CAP
ST = CAP // P
DROPPED = 2.0 ** 20


def moe_slots(nc, C, a):
    x, ident, neghalf = C["x"], C["ident"], C["neghalf"]
    slots_in, slots_out = C["slots_in"], C["slots_out"]
    m = Store(nc)
    with m.stack:
        hs = m.sb("m0hs", [P, 2, DC, B * S], F16)
        h2 = m.sb("m0h2", [P, NT, D])
        w4 = m.sb("m0w4", [P, NT, K0])
        slot = m.sb("m0slot", [P, NT, 2, K0], U32)
        scattered = m.sem("m0_scattered")
        r = Store(nc)
        with r.stack:
            gate = r.sb("m0gate", [P, DC, E0])
            normw = r.sb("m0normw", [P, D])
            eids = r.sb("m0eids", [P, E0])
            before = r.sb("m0before", [P, P])
            ones = r.sb("m0ones", [P, P])
            st = r.sb("m0st", [P, 2, 6])
            mv = r.sb("m0mv", [P, 2, 4])
            ms = r.sb("m0ms", [P, 2, 3])
            hn = r.sb("m0hn", [P, 2, D])
            junk = r.sb("m0junk", [P, D])
            hT = r.sb("m0hT", [P, 2, DC, P])
            lg = r.sb("m0lg", [P, E0])
            top = r.sb("m0top", [P, 8])
            idx = r.sb("m0idx", [P, 8], U32)
            idf = r.sb("m0idf", [P, K0])
            nb = r.sb("m0nb", [P, 1])
            ex = r.sb("m0ex", [P, K0])
            sm = r.sb("m0sm", [P, 2])
            OH = r.sb("m0OH", [P, K0, E0])
            M = r.sb("m0M", [P, 2, E0])
            Mp = r.sb("m0Mp", [P, E0])
            sv = r.sb("m0sv", [P, 2, E0])
            pk = r.sb("m0pk", [P, 2, K0, E0])
            sf = r.sb("m0sf", [P, 2, K0])
            p_t = [r.ps(f"m0pt{i}", [P, DC, P]) for i in range(2)]
            p_l = [r.ps(f"m0pl{i}", [P, 512]) for i in range(2)]
            p_p = [r.ps(f"m0pp{i}", [P, 512]) for i in range(2)]
            (loaded, const_ok, var_ok, rstd_ok, hn_ok, sq_ok, ms_ok, rr_ok, h2_ok, t_ok, hT_ok, hi_ok, lo_ok,
             l_ok, nb_ok, ex_ok, step, M_ok, pos_ok, slot_ok, stat_ok) = r.sems(
                "m0", "loaded const_ok var_ok rstd_ok hn_ok sq_ok ms_ok rr_ok h2_ok t_ok hT_ok hi_ok lo_ok"
                      " l_ok nb_ok ex_ok step M_ok pos_ok slot_ok stat_ok")
            with nc.Block() as block:
                @block.sync
                def _(sp):
                    moved(sp, loaded, [(gate[:, :, :], a["m0_gate"]), (normw[:, :], a["m0_normw"].to_broadcast([P, D])),
                                       (eids[:, :], a["eids"].to_broadcast([P, E0])), (before[:, :], a["before"])])

                @block.gpsimd
                def _(pool):
                    def roots(n):
                        u = n % 2
                        pool.wait_ge(var_ok, n + 1)
                        pool.tensor_tensor(mv[:, u, 3:4], mv[:, u, 2:3], neghalf[:, 0:1], ALU.pow).then_inc(rstd_ok, 1)
                        pool.wait_ge(ms_ok, n + 1)
                        pool.tensor_tensor(ms[:, u, 2:3], ms[:, u, 1:2], neghalf[:, 0:1], ALU.pow).then_inc(rr_ok, 1)

                    def scatter(n):
                        pool.wait_ge(slot_ok, n + 1)
                        for k in range(K0):
                            pool.indirect_dma_start(slots_in, bass.IndirectOffsetOnAxis(ap=slot[:, n, 1, k:k + 1], axis=0),
                                                    h2[:, n, :], None, bounds_check=SLOTS - 1, oob_is_err=False).then_inc(scattered, 16)

                    pool.memset(ones[:, :], 1.0).then_inc(const_ok, 1)
                    roots(0)
                    roots(1)
                    pool.wait_ge(C["zero_ok"], 16)
                    for n in range(NT):
                        if n + 2 < NT:
                            roots(n + 2)
                        scatter(n)

                @block.scalar
                def _(act):
                    def squares(n, u):
                        act.wait_ge(hn_ok, n + 1)
                        act.activation(junk[:, :], hn[:, u, :], ACT.Square, accum_out=ms[:, u, 0:1]).then_inc(sq_ok, 1)

                    def inputs(n, u):
                        act.wait_ge(t_ok, n + 1)
                        act.activation(hT[:, u, :, :], p_t[u][:, :, :], ACT.Copy).then_inc(hT_ok, 1)
                        act.activation(hs[:, 0, :, bass.ds(n * P, P)], p_t[u][:, :, :], ACT.Copy, scale=H_UP).then_inc(hi_ok, 1)

                    def weights(n, u):
                        act.wait_ge(nb_ok, n + 1)
                        act.activation(ex[:, :], top[:, 0:K0], ACT.Exp, bias=nb[:, 0:1], accum_out=sm[:, 0:1]).then_inc(ex_ok, 1)

                    squares(0, 0)
                    squares(1, 1)

                    def tile(n, u):
                        inputs(n, u)
                        if type(n) is not int:
                            squares(n + 2, u)
                        weights(n, u)
                    looped(act, tile, NT - 2)
                    tile(NT - 2, 0)
                    tile(NT - 1, 1)

                @block.tensor
                def _(pe):
                    def turn(n, u):
                        pe.wait_ge(h2_ok, n + 1)
                        for c in range(DC):
                            ins = pe.transpose(p_t[u][:, c, :], h2[:, n, P * c:P * c + P], ident[:, :])
                        ins.then_inc(t_ok, 1)

                    def route(n, u):
                        pe.wait_ge(hT_ok, n + 1)
                        for c in range(DC):
                            ins = pe.matmul(p_l[u][:, 0:E0], hT[:, u, c, :], gate[:, c, :], start=(c == 0), stop=(c == DC - 1))
                        ins.then_inc(l_ok, 1)

                    def places(n, u):
                        pe.wait_ge(M_ok, n + 1)
                        pe.matmul(p_p[u][:, 0:E0], before[:, :], M[:, u, :], start=True, stop=False)
                        pe.matmul(p_p[u][:, 0:E0], ones[:, :], Mp[:, :], start=False, stop=True).then_inc(pos_ok, 1)

                    pe.wait_ge(loaded, 64)
                    pe.wait_ge(const_ok, 1)
                    for n in range(NT):
                        u = n % 2
                        if n == 0:
                            turn(0, 0)
                        if n + 1 < NT:
                            if n >= 1:
                                pe.wait_ge(lo_ok, n)
                            turn(n + 1, 1 - u)
                        route(n, u)
                        places(n, u)

                @block.vector
                def _(dve):
                    def tile_of(n):
                        return x[:, bass.ds(n, 1), :].rearrange("p a d -> p (a d)")

                    def norm(n, u):
                        dve.bn_stats(st[:, u, :], tile_of(n))
                        dve.drain()
                        dve.bn_aggr(mv[:, u, 0:2], st[:, u, :]).then_inc(stat_ok, 1)
                        dve.wait_ge(stat_ok, n + 1)
                        dve.tensor_scalar(mv[:, u, 2:3], mv[:, u, 1:2], 1e-5, None, ALU.add).then_inc(var_ok, 1)
                        dve.wait_ge(rstd_ok, n + 1)
                        dve.tensor_scalar(hn[:, u, :], tile_of(n), mv[:, u, 0:1], mv[:, u, 3:4], ALU.subtract, ALU.mult).then_inc(hn_ok, 1)
                        dve.wait_ge(sq_ok, n + 1)
                        dve.tensor_scalar(ms[:, u, 1:2], ms[:, u, 0:1], 1.0 / D, 1e-6, ALU.mult, ALU.add).then_inc(ms_ok, 1)
                        dve.tensor_tensor(tile_of(n), tile_of(n), hn[:, u, :], ALU.add)
                        dve.wait_ge(rr_ok, n + 1)
                        dve.scalar_tensor_tensor(h2[:, bass.ds(n, 1), :].rearrange("p a d -> p (a d)"), hn[:, u, :],
                                                 ms[:, u, 2:3], normw[:, :], ALU.mult, ALU.mult).then_inc(h2_ok, 1)

                    def low(n, u):
                        dve.wait_ge(hi_ok, n + 1)
                        cols = bass.ds(n * P, P)
                        dve.scalar_tensor_tensor(hs[:, 1, :, cols], p_t[u][:, :, :], H_UP, hs[:, 0, :, cols],
                                                 ALU.mult, ALU.subtract).then_inc(lo_ok, 1)

                    def choose(n, u):
                        def then(ins, k):
                            ins.then_inc(step, 1)
                            dve.wait_ge(step, n * 7 + k)
                        dve.wait_ge(l_ok, n + 1)
                        dve.tensor_copy(lg[:, :], p_l[u][:, 0:E0])
                        dve.drain()
                        dve.max(top[:, :], lg[:, :])
                        dve.drain()
                        dve.tensor_scalar(nb[:, :], top[:, 0:1], -1.0, None, ALU.mult).then_inc(nb_ok, 1)
                        dve.max_index(idx[:, :], top[:, :], lg[:, :])
                        dve.drain()
                        then(dve.tensor_copy(idf[:, :], idx[:, 0:K0]), 1)
                        then(dve.tensor_tensor(OH[:, :, :], bcast(eids[:, :], 1, K0), bcast(idf[:, :], 2, E0), ALU.is_equal), 2)
                        dve.tensor_reduce(M[:, u, :], OH[:, :, :].rearrange("p k e -> p e k"), AX.X, ALU.add).then_inc(M_ok, 1)
                        dve.wait_ge(ex_ok, n + 1)
                        then(dve.reciprocal(sm[:, 1:2], sm[:, 0:1]), 3)
                        dve.tensor_scalar(w4[:, bass.ds(n, 1), :].rearrange("p a k -> p (a k)"), ex[:, :], sm[:, 1:2], None, ALU.mult)
                        dve.wait_ge(pos_ok, n + 1)
                        dve.tensor_tensor(Mp[:, :], Mp[:, :], M[:, u, :], ALU.add)
                        dve.tensor_scalar(sv[:, 0, :], p_p[u][:, 0:E0], CAP - 1.0, None, ALU.min)
                        then(dve.tensor_scalar(sv[:, 1, :], p_p[u][:, 0:E0], float(CAP), DROPPED, ALU.is_ge, ALU.mult), 4)
                        then(dve.scalar_tensor_tensor(sv[:, 0, :], eids[:, :], float(CAP), sv[:, 0, :], ALU.mult, ALU.add), 5)
                        then(dve.tensor_tensor(sv[:, 1, :], sv[:, 1, :], sv[:, 0, :], ALU.add), 6)
                        for j in range(2):
                            ins = dve.tensor_tensor(pk[:, j, :, :], OH[:, :, :], bcast(sv[:, j, :], 1, K0), ALU.mult)
                        then(ins, 7)
                        dve.tensor_reduce(sf[:, :, :], pk[:, :, :, :], AX.X, ALU.add)
                        dve.drain()
                        dve.tensor_copy(slot[:, bass.ds(n, 1), :, :].rearrange("p a j k -> p (a j) k"), sf[:, :, :]).then_inc(slot_ok, 1)

                    dve.wait_ge(loaded, 64)
                    dve.memset(Mp[:, :], 0.0)
                    norm(0, 0)
                    norm(1, 1)

                    def tile(n, u):
                        low(n, u)
                        if type(n) is not int:
                            norm(n + 2, u)
                        choose(n, u)
                    looped(dve, tile, NT - 2)
                    tile(NT - 2, 0)
                    tile(NT - 1, 1)

        e = Store(nc)
        with e.stack:
            GU = DC * 2 * P
            xg = e.sb("m0xg", [P, 2, ST, D])
            xs = e.sb("m0xs", [P, 2, 2, DC, CAP], F16)
            rg = e.sb("m0rg", [P, 2, GU])
            rd = e.sb("m0rd", [P, 2, D])
            wg = e.sb("m0wg", [P, 2, 2, GU], F16)
            wd = e.sb("m0wd", [P, 2, 2, D], F16)
            sg = e.sb("m0sg", [P, 2, CAP])
            ac = e.sb("m0ac", [P, 2, CAP])
            ap = e.sb("m0ap", [P, 2, 2, CAP], F16)
            yo = e.sb("m0yo", [P, 2, ST, D])
            rs_ = e.sb("m0rs", [P, GU + D])
            ws = e.sb("m0ws", [P, 2, GU + D], F16)
            ssg = e.sb("m0ssg", [P, 2, CH])
            sac = e.sb("m0sac", [P, 2, CH])
            sap = e.sb("m0sap", [P, 2, 2, CH], F16)
            p_x = [e.ps(f"m0px{i}", [P, DC, CAP]) for i in range(2)]
            p_h = [e.ps(f"m0ph{i}", [P, 2, CAP]) for i in range(2)]
            p_y = [e.ps(f"m0py{i}", [P, ST, D]) for i in range(2)]
            p_s = [e.ps(f"m0ps{i}", [P, CH]) for i in range(2)]
            xin = [e.sem(f"e0_xin{u}") for u in range(2)]
            gin = [e.sem(f"e0_gin{u}") for u in range(2)]
            din = [e.sem(f"e0_din{u}") for u in range(2)]
            stored = [e.sem(f"e0_stored{u}") for u in range(2)]
            (sin, sh_ok, sl_ok, sg_ok, su_ok, ssilu_ok, sact_ok, sah_ok, sal_ok, sy_ok, sx_ok,
             xt_ok, xh_ok, xl_ok, gh_ok, gl_ok, dh_ok, dl_ok, gu_ok, silu_ok, act_ok, ah_ok, al_ok, y_ok, yo_ok) = e.sems(
                "e0", "sin sh_ok sl_ok sg_ok su_ok ssilu_ok sact_ok sah_ok sal_ok sy_ok sx_ok"
                      " xt_ok xh_ok xl_ok gh_ok gl_ok dh_ok dl_ok gu_ok silu_ok act_ok ah_ok al_ok y_ok yo_ok")

            def periods(eng, body):
                for k in range(3):
                    body(k, k % 2)
                with eng.Fori(0, (E0 - 6) // 2) as i:
                    body(i * 2 + 3, 1)
                    body(i * 2 + 4, 0)
                for k in range(E0 - 3, E0):
                    body(k, k % 2)

            def has(k):
                return type(k) is not int or 0 <= k < E0

            with nc.Block() as block:
                @block.sync
                def _(sp):
                    def load_x(k, u):
                        if type(k) is not int or k >= 2:
                            sp.wait_ge(xt_ok, k - 1)
                        sp.dma_start(xg[:, u, :, :], slots_in[bass.ds(k * CAP, CAP), :].rearrange("(s p) d -> p s d", p=P)).then_inc(xin[u], 16)

                    def load_g(k, u):
                        if type(k) is not int or k >= 2:
                            sp.wait_ge(gl_ok, k - 1)
                        sp.dma_start(rg[:, u, :], a["m0_wgu"][bass.ds(k, 1), :, :].rearrange("a p n -> p (a n)")).then_inc(gin[u], 16)

                    def load_d(k, u):
                        if type(k) is not int or k >= 2:
                            sp.wait_ge(dl_ok, k - 1)
                        sp.dma_start(rd[:, u, :], a["m0_wd"][bass.ds(k, 1), :, :].rearrange("a p n -> p (a n)")).then_inc(din[u], 16)

                    def store(k, u):
                        sp.wait_ge(yo_ok, k + 1)
                        sp.dma_start(slots_out[bass.ds(k * CAP, CAP), :].rearrange("(s p) d -> p s d", p=P), yo[:, u, :, :]).then_inc(stored[u], 16)

                    sp.dma_start(rs_[:, :], a["m0_ws"]).then_inc(sin, 16)
                    load_g(0, 0)
                    load_g(1, 1)
                    load_d(0, 0)
                    load_d(1, 1)
                    sp.wait_ge(scattered, 16 * NT * K0)
                    load_x(0, 0)
                    load_x(1, 1)
                    load_x(2, 0)
                    load_g(2, 0)
                    load_x(3, 1)
                    load_g(3, 1)
                    load_d(2, 0)

                    def period(k, u):
                        if type(k) is not int or k >= 1:
                            if has(k + 3):
                                load_x(k + 3, 1 - u)
                                load_g(k + 3, 1 - u)
                            if has(k + 2):
                                load_d(k + 2, u)
                            store(k - 1, 1 - u)
                    periods(sp, period)
                    store(E0 - 1, 1)
                    for u in range(2):
                        sp.wait_ge(stored[u], 16 * E0 // 2)

                @block.gpsimd
                def _(pool):
                    pool.wait_ge(sh_ok, 1)
                    pool.tensor_tensor(ws[:, 1, :], rs_[:, :], ws[:, 0, :], ALU.subtract).then_inc(sl_ok, 1)

                    def low_g(k, u):
                        pool.wait_ge(gh_ok, k + 1)
                        pool.tensor_tensor(wg[:, u, 1, :], rg[:, u, :], wg[:, u, 0, :], ALU.subtract).then_inc(gl_ok, 1)

                    def low_d(k, u):
                        pool.wait_ge(dh_ok, k + 1)
                        pool.tensor_tensor(wd[:, u, 1, :], rd[:, u, :], wd[:, u, 0, :], ALU.subtract).then_inc(dl_ok, 1)
                    low_g(0, 0)
                    low_g(1, 1)
                    low_d(0, 0)

                    def period(k, u):
                        if has(k + 2):
                            low_g(k + 2, u)
                        if has(k + 1):
                            low_d(k + 1, 1 - u)
                    periods(pool, period)

                @block.scalar
                def _(act):
                    act.wait_ge(sin, 16)
                    act.activation(ws[:, 0, :], rs_[:, :], ACT.Copy, scale=W_UP)
                    act.activation(rs_[:, :], rs_[:, :], ACT.Copy, scale=W_UP).then_inc(sh_ok, 1)
                    for q in range(NCH):
                        act.wait_ge(su_ok, q + 1)
                        act.activation(ssg[:, q, :], p_s[0][:, :], ACT.Silu, scale=1.0 / (H_UP * W_UP)).then_inc(ssilu_ok, 1)
                        act.wait_ge(sact_ok, q + 1)
                        act.activation(sap[:, q, 0, :], sac[:, q, :], ACT.Copy).then_inc(sah_ok, 1)

                    def x_high(k, u):
                        act.wait_ge(xt_ok, k + 1)
                        act.activation(xs[:, u, 0, :, :], p_x[u][:, :, :], ACT.Copy, scale=H_UP).then_inc(xh_ok, 1)

                    def silu(k, u):
                        act.wait_ge(gu_ok, k + 1)
                        act.activation(sg[:, u, :], p_h[u][:, 0, :], ACT.Silu, scale=1.0 / (H_UP * W_UP)).then_inc(silu_ok, 1)

                    def a_high(k, u):
                        act.wait_ge(act_ok, k + 1)
                        act.activation(ap[:, u, 0, :], ac[:, u, :], ACT.Copy).then_inc(ah_ok, 1)

                    def y_out(k, u):
                        act.wait_ge(y_ok, k + 1)
                        if type(k) is not int or k >= 2:
                            act.wait_ge(stored[u], (k - u) * 8)
                        act.activation(yo[:, u, :, :], p_y[u][:, :, :], ACT.Copy, scale=1.0 / W_UP).then_inc(yo_ok, 1)

                    x_high(0, 0)
                    x_high(1, 1)

                    def period(k, u):
                        silu(k, u)
                        if has(k + 2):
                            x_high(k + 2, u)
                        a_high(k, u)
                        if has(k - 1):
                            y_out(k - 1, 1 - u)
                    periods(act, period)
                    y_out(E0 - 1, 1)

                @block.tensor
                def _(pe):
                    pe.wait_ge(sl_ok, 1)
                    for q in range(NCH):
                        if q >= 1:
                            pe.wait_ge(sact_ok, q)
                        for which in range(2):
                            k = 0
                            for c in range(DC):
                                for sw, sh in PASSES:
                                    ins = pe.matmul(p_s[which][:, :], ws[:, sw, P * (2 * c + which):P * (2 * c + which) + P],
                                                    hs[:, sh, c, CH * q:CH * q + CH], start=(k == 0), stop=(k == 5))
                                    k += 1
                        ins.then_inc(su_ok, 1)
                    for n in range(NT):
                        q, o = n * P // CH, n * P % CH
                        pe.wait_ge(sal_ok, q + 1)
                        if n >= 2:
                            pe.wait_ge(sx_ok, n - 1)
                        for k, (sw, sa) in enumerate(PASSES):
                            ins = pe.matmul(p_y[n % 2][:, 0, :], sap[:, q, sa, o:o + P], ws[:, sw, GU:GU + D],
                                            start=(k == 0), stop=(k == 2))
                        ins.then_inc(sy_ok, 1)

                    def turn(k, u):
                        pe.wait_ge(xin[u], (k - u) * 8 + 16)
                        if type(k) is not int or k >= 2:
                            pe.wait_ge(xl_ok, k - 1)
                        for c in range(DC):
                            for s in range(ST):
                                ins = pe.transpose(p_x[u][:, c, P * s:P * s + P], xg[:, u, s, P * c:P * c + P], ident[:, :])
                        ins.then_inc(xt_ok, 1)

                    def hidden(k, u):
                        pe.wait_ge(xl_ok, k + 1)
                        pe.wait_ge(gl_ok, k + 1)
                        if type(k) is not int or k >= 2:
                            pe.wait_ge(act_ok, k - 1)
                        for which in range(2):
                            i = 0
                            for c in range(DC):
                                for sw, sx in PASSES:
                                    ins = pe.matmul(p_h[u][:, which, :], wg[:, u, sw, P * (2 * c + which):P * (2 * c + which) + P],
                                                    xs[:, u, sx, c, :], start=(i == 0), stop=(i == 5))
                                    i += 1
                        ins.then_inc(gu_ok, 1)

                    def down(k, u):
                        pe.wait_ge(al_ok, k + 1)
                        pe.wait_ge(dl_ok, k + 1)
                        if type(k) is not int or k >= 2:
                            pe.wait_ge(yo_ok, k - 1)
                        elif k < 2:
                            pe.wait_ge(sx_ok, NT)
                        for s in range(ST):
                            for i, (sw, sa) in enumerate(PASSES):
                                ins = pe.matmul(p_y[u][:, s, :], ap[:, u, sa, P * s:P * s + P], wd[:, u, sw, :],
                                                start=(i == 0), stop=(i == 2))
                        ins.then_inc(y_ok, 1)

                    turn(0, 0)
                    turn(1, 1)

                    def period(k, u):
                        hidden(k, u)
                        if has(k + 2):
                            turn(k + 2, u)
                        if has(k - 1):
                            down(k - 1, 1 - u)
                    periods(pe, period)
                    down(E0 - 1, 1)

                @block.vector
                def _(dve):
                    def high_g(k, u):
                        dve.wait_ge(gin[u], (k - u) * 8 + 16)
                        if type(k) is not int or k >= 2:
                            dve.wait_ge(gu_ok, k - 1)
                        dve.tensor_scalar(wg[:, u, 0, :], rg[:, u, :], W_UP, None, ALU.mult)
                        dve.tensor_scalar(rg[:, u, :], rg[:, u, :], W_UP, None, ALU.mult).then_inc(gh_ok, 1)

                    def high_d(k, u):
                        dve.wait_ge(din[u], (k - u) * 8 + 16)
                        if type(k) is not int or k >= 2:
                            dve.wait_ge(y_ok, k - 1)
                        dve.tensor_scalar(wd[:, u, 0, :], rd[:, u, :], W_UP, None, ALU.mult)
                        dve.tensor_scalar(rd[:, u, :], rd[:, u, :], W_UP, None, ALU.mult).then_inc(dh_ok, 1)

                    def x_low(k, u):
                        dve.wait_ge(xh_ok, k + 1)
                        dve.scalar_tensor_tensor(xs[:, u, 1, :, :], p_x[u][:, :, :], H_UP, xs[:, u, 0, :, :],
                                                 ALU.mult, ALU.subtract).then_inc(xl_ok, 1)

                    def times_up(k, u):
                        dve.wait_ge(silu_ok, k + 1)
                        dve.scalar_tensor_tensor(ac[:, u, :], p_h[u][:, 1, :], 1.0 / (H_UP * W_UP), sg[:, u, :],
                                                 ALU.mult, ALU.mult).then_inc(act_ok, 1)

                    def a_low(k, u):
                        dve.wait_ge(ah_ok, k + 1)
                        dve.tensor_tensor(ap[:, u, 1, :], ac[:, u, :], ap[:, u, 0, :], ALU.subtract).then_inc(al_ok, 1)

                    high_g(0, 0)
                    high_g(1, 1)
                    high_d(0, 0)
                    for q in range(NCH):
                        dve.wait_ge(ssilu_ok, q + 1)
                        dve.scalar_tensor_tensor(sac[:, q, :], p_s[1][:, :], 1.0 / (H_UP * W_UP), ssg[:, q, :],
                                                 ALU.mult, ALU.mult).then_inc(sact_ok, 1)
                        dve.wait_ge(sah_ok, q + 1)
                        dve.tensor_tensor(sap[:, q, 1, :], sac[:, q, :], sap[:, q, 0, :], ALU.subtract).then_inc(sal_ok, 1)
                    for n in range(NT):
                        dve.wait_ge(sy_ok, n + 1)
                        dve.scalar_tensor_tensor(x[:, n, :], p_y[n % 2][:, 0, :], 1.0 / W_UP, x[:, n, :],
                                                 ALU.mult, ALU.add).then_inc(sx_ok, 1)
                    x_low(0, 0)
                    x_low(1, 1)

                    def period(k, u):
                        times_up(k, u)
                        if has(k + 2):
                            high_g(k + 2, u)
                            x_low(k + 2, u)
                        a_low(k, u)
                        if has(k + 1):
                            high_d(k + 1, 1 - u)
                    periods(dve, period)
                    dve.wait_ge(sx_ok, NT)

        c = Store(nc)
        with c.stack:
            rows = c.sb("m0rows", [P, NT, K0, D])
            fetched = [c.sem(f"m0_fetched{n}") for n in range(NT)]
            added = c.sem("m0_added")
            with nc.Block() as block:
                @block.gpsimd
                def _(pool):
                    for n in range(NT):
                        for k in range(K0):
                            pool.indirect_dma_start(rows[:, n, k, :], None, slots_out,
                                                    bass.IndirectOffsetOnAxis(ap=slot[:, n, 0, k:k + 1], axis=0),
                                                    bounds_check=SLOTS - 1, oob_is_err=False).then_inc(fetched[n], 16)

                @block.vector
                def _(dve):
                    for n in range(NT):
                        dve.wait_ge(fetched[n], 16 * K0)
                        for k in range(K0):
                            dve.scalar_tensor_tensor(x[:, n, :], rows[:, n, k, :], w4[:, n, k:k + 1], x[:, n, :],
                                                     ALU.mult, ALU.add).then_inc(added, 1)
                            dve.wait_ge(added, n * K0 + k + 1)


def decoder(nc, a, out):
    g = Store(nc, last=True)
    with g.stack:
        C = {"x": g.sb("x", [P, NT, D]), "ident": g.sb("ident", [P, P]), "hmask": g.sb("hmask", [P, HG]),
             "neghalf": g.sb("neghalf", [P, 1]), "ctxT": g.sb("ctxT", [P, DC, B * S]), "hi": g.sb("hi", [P, B]),
             "cmask": g.sb("cmask", [P, S]), "rs": g.sb("rs", [P, 1])}
        mi = g.sb("mi", [P, B], I32)
        C["slots_in"] = nc.dram_tensor("slots_in", [SLOTS, D], F32, kind="Internal").ap()
        C["slots_out"] = nc.dram_tensor("slots_out", [SLOTS, D], F32, kind="Internal").ap()
        C["zero_ok"] = zero_ok = g.sem("zero_ok")
        zeros = g.sb("zeros", [P, 2048])
        zeroed = g.sem("zeroed")
        in_sem, mask_ok, out_sem = g.sem("in_sem"), g.sem("mask_ok"), g.sem("out_sem")
        def weights(tag, names, rows):
            w = {k: g.sb(f"{tag}_{k}", [P, DC, D]) for k in ("wq", "wk", "wv", "wo")}
            w.update({k: g.sb(f"{tag}_{k}", [P, DC]) for k in names})
            w.update({k: g.sb(f"{tag}_{k}", [P, D]) for k in rows})
            pairs = [(t[:, :, :] if len(t.shape) == 3 else t[:, :],
                      a[f"{tag}_{k}"].to_broadcast([P, D]) if k in rows else a[f"{tag}_{k}"]) for k, t in w.items()]
            w["loaded"], w["count"] = g.sem(f"{tag}_loaded"), 16 * len(pairs)
            return w, pairs

        w_a0, load_a0 = weights("a0", ("bq", "bk"), ("bv", "bo"))
        w_c0, load_c0 = weights("c0", ("bq", "bk"), ("bv", "bo", "gamma", "beta"))
        w_a1, load_a1 = weights("a1", (), ())
        w_x = {"wq": g.sb("xwq", [P, DC, XH * XD]), "wk": g.sb("xwk", [P, DC, KVH * XD]),
               "wv": g.sb("xwv", [P, DC, KVH * XD]), "wo": g.sb("xwo", [P, XH, D])}
        w_x["loaded"] = g.sem("x_loaded")
        with nc.Block() as block:
            @block.sync
            def _(sp):
                n = moved(sp, in_sem, [
                    (C["x"][:, :, :], a["x"]), (C["ident"][:, :], a["ident"]), (C["hmask"][:, :], a["hmask"]),
                    (C["cmask"][:, :], a["cmask"]), (mi[:, :], a["mask"]), (C["rs"][:, :], a["rs"].to_broadcast([P, 1]))])
                moved(sp, w_a0["loaded"], load_a0)
                sp.wait_ge(in_sem, n)

            @block.vector
            def _(dve):
                dve.memset(zeros[:, :], 0.0).then_inc(zeroed, 1)
                dve.memset(C["neghalf"][:, :], -0.5)
                dve.wait_ge(in_sem, 16 * 6)
                dve.tensor_scalar(C["hi"][:, :], mi[:, :], 0.5, 100.0 / QSCALE, ALU.is_gt, ALU.mult).then_inc(mask_ok, 1)
                dve.wait_ge(mask_ok, 1)
                dve.tensor_scalar(C["hi"][:, :], C["hi"][:, :], -50.0 / QSCALE, None, ALU.add).then_inc(mask_ok, 1)
                dve.tensor_scalar(C["rs"][:, :], C["rs"][:, :], 0.0, 0.3, ALU.max, ALU.min).then_inc(mask_ok, 1)
                dve.wait_ge(mask_ok, 3)

        def ahead(sp):
            sp.dma_start(C["ctxT"][:, :, :], a["ctxT"]).then_inc(w_c0["loaded"], 16)
            moved(sp, w_c0["loaded"], load_c0)
            w_c0["count"] += 16
            sp.dma_start(C["slots_in"].rearrange("(p a s) d -> p a (s d)", p=P, a=8), bcast(zeros[:, :], 1, 8)).then_inc(zero_ok, 16)
            moved(sp, w_a1["loaded"], load_a1)
            moved(sp, w_x["loaded"], [(w_x["wq"][:, :, :], a["x_wq"]), (w_x["wk"][:, :, :], a["x_wk"]),
                                      (w_x["wv"][:, :, :], a["x_wv"]), (w_x["wo"][:, :, :], a["x_wo"])])

        if ONLY in (0, 1):
            attention16(nc, C, "a0", "self", w_a0, ahead)
        else:
            with nc.Block() as block:
                block.sync(ahead)
        if ONLY in (0, 2):
            attention16(nc, C, "c0", "cross", w_c0)
        if ONLY in (0, 3):
            moe_slots(nc, C, a)
        if ONLY in (0, 4):
            attention16(nc, C, "a1", "causal", w_a1)
        if ONLY in (0, 5):
            C["tab_c"], C["tab_s"] = g.sb("tab_c", [P, NTAB, XD]), g.sb("tab_s", [P, NTAB, XD])
            rope_tables(nc, C, a)
            attention128(nc, C, w_x)
        if ONLY in (0, 6):
            moe_dense(nc, C, a)
        with nc.Block() as block:
            @block.sync
            def _(sp):
                sp.dma_start(out.rearrange("(n p) d -> p n d", p=P), C["x"][:, :, :]).then_inc(out_sem, 16)
                sp.wait_ge(out_sem, 16)
                sp.wait_ge(zero_ok, 16)


def kernel(**inputs):
    import concourse.bacc as bacc
    from concourse.bass_utils import run_bass_kernel_spmd as run

    nc = bacc.Bacc("TRN2", target_bir_lowering=False, num_devices=1)
    v = {k: np.asarray(t) for k, t in inputs.items()}

    def chunked(t):
        return t.reshape(t.shape[0] // P, P, -1).transpose(1, 0, 2)

    def column(t):
        return t.reshape(DC, P).T

    arrays = {
        "x": v["x"].reshape(NT, P, D).transpose(1, 0, 2),
        "ctxT": chunked(v["ctx_2048"].reshape(B * S, D).T),
        "mask": np.concatenate([v["mask_BxS2_ik0"].T] * 2),
        "rs": v["L0_xattn_residual_scale"].reshape(1, 1),
        "ident": np.eye(P, dtype=np.float32),
        "hmask": (np.arange(P)[:, None] // HD == np.arange(HG)).astype(np.float32),
        "cmask": np.where(np.arange(S) > np.arange(P)[:, None] % S, np.float32(-1e9 / QSCALE), np.float32(0)),
    }
    for tag, qkv, bias, wo, bo in (("a0", "L0_attn_Wqkv_w", "L0_attn_Wqkv_b", "L0_attn_out_w", "L0_attn_out_b"),
                                   ("a1", "L1_attn_w_qkv", None, "L1_attn_w_o", None)):
        for i, n in enumerate("qkv"):
            arrays[f"{tag}_w{n}"] = chunked(v[qkv][D * i:D * i + D].T)
            if bias:
                part = v[bias][D * i:D * i + D]
                arrays[f"{tag}_b{n}"] = part.reshape(1, D) if n == "v" else column(part)
        arrays[f"{tag}_wo"] = chunked(v[wo].T)
        if bo:
            arrays[f"{tag}_bo"] = v[bo].reshape(1, D)
    for n in "qkvo":
        arrays[f"c0_w{n}"] = chunked(v[f"L0_xattn_W{n}"].T)
        part = v[f"L0_xattn_b{n}"]
        arrays[f"c0_b{n}"] = column(part) if n in "qk" else part.reshape(1, D)
    arrays["c0_gamma"] = v["L0_xattn_ln_gamma"].reshape(1, D)
    arrays["c0_beta"] = v["L0_xattn_ln_beta"].reshape(1, D)

    pos, itok = v["pos_BxS2"].T, v["itok_BxS_4096_4607"]
    arrays["pos"] = np.concatenate([np.concatenate([pos, itok.T]), itok.reshape(NT, P).T], axis=1)
    arrays["inv"] = (np.float32(1) / np.float32(10000) ** (np.arange(0, XD, 2, dtype=np.float32) / np.float32(XD))).reshape(1, RH)
    arrays["qw"] = v["L1_xattn_q_norm_w"].reshape(1, XD)
    arrays["kw"] = v["L1_xattn_k_norm_w"].reshape(1, XD)
    for n in "qkvo":
        arrays[f"x_w{n}"] = chunked(v[f"L1_xattn_W{n}"].T)
    def gate_up(t):
        return t.reshape(-1, DC, P, 2, I0).transpose(0, 2, 1, 3, 4).reshape(-1, P, DC * 2 * I0)

    arrays["m0_wgu"] = gate_up(v["L0_ffn_w13"])
    arrays["m0_wd"] = v["L0_ffn_w2"]
    shared = gate_up(np.concatenate([v["L0_ffn_shared_gate_w"], v["L0_ffn_shared_up_w"]], axis=1))[0]
    arrays["m0_ws"] = np.concatenate([shared, v["L0_ffn_shared_down_w"]], axis=1)
    arrays["m0_gate"] = chunked(v["L0_ffn_gate_w"].T)
    arrays["m0_normw"] = v["L0_ffn_norm_w"].reshape(1, D)
    arrays["eids"] = np.arange(E0, dtype=np.float32).reshape(1, E0)
    arrays["before"] = np.triu(np.ones((P, P), np.float32), 1)
    def with_shared(experts, shared):
        return np.concatenate([experts, shared[None], np.zeros_like(shared[None])])

    gu = with_shared(v["L1_ffn_gu_w"].reshape(E1, 2, I1, D), np.stack([v["L1_ffn_sh_gate_w"], v["L1_ffn_sh_up_w"]]))
    gu = gu.reshape(NPAIR, 2, 2, I1, DC, P).transpose(0, 5, 4, 2, 1, 3)
    dp = with_shared(v["L1_ffn_dp_w"], v["L1_ffn_sh_down_w"]).transpose(0, 2, 1)
    arrays["m1_w"] = np.concatenate([gu.reshape(NPAIR, P, -1), dp.reshape(NPAIR, P, D)], axis=2)
    arrays["m1_gate"] = chunked(np.concatenate([v["L1_ffn_gate_w"], v["L1_ffn_sh_gate1_w"]]).T)
    arrays = {k: np.ascontiguousarray(t) for k, t in arrays.items()}
    a = {k: nc.dram_tensor(f"in_{k}", t.shape, mybir.dt.from_np(t.dtype), kind="ExternalInput").ap()
         for k, t in arrays.items()}
    out = nc.dram_tensor("out_x", [B * S, D], F32, kind="ExternalOutput").ap()
    decoder(nc, a, out)
    r = run(nc, [{f"in_{k}": t for k, t in arrays.items()}], core_ids=[0])
    return r.results[0]["out_x"].reshape(B, S, D)
```

```python
import numpy as np
import concourse.bass as bass
from concourse import mybir
from contextlib import ExitStack

F32 = mybir.dt.float32
F16 = mybir.dt.float16
I32 = mybir.dt.int32
U32 = mybir.dt.uint32
ALU = mybir.AluOpType
ACT = mybir.ActivationFunctionType
AX = mybir.AxisListType

P = 128
B, S, D = 16, 64, 256
NT = B * S // P
DC = D // P
H = 16
HD = D // H
HG = P // HD
NP = H // 2
OW = 2 * (HD + 1)
QSCALE = float(HD) ** -0.5
ONLY = 0


class Store:

    def __init__(self, nc, last=False):
        self.nc, self.stack, self.held = nc, ExitStack(), []
        if not last:
            self.stack.callback(self.clear)

    def sb(self, name, shape, dt=F32):
        return self.stack.enter_context(self.nc.sbuf_tensor(name, shape, dt))

    def ps(self, name, shape):
        return self.stack.enter_context(self.nc.psum_tensor(name, shape, F32))

    def sem(self, name):
        self.held.append(self.nc.alloc_semaphore(name))
        return self.held[-1]

    def clear(self):
        if self.held:
            self.nc.clear_and_free_semaphores(self.held)
            self.nc.all_engine_barrier()

    def sems(self, prefix, names):
        return [self.sem(f"{prefix}_{n}") for n in names.split()]


def bcast(ap, axis, n):
    shape = list(ap.shape)
    shape.insert(axis, n)
    return ap.unsqueeze(axis).to_broadcast(shape)


def looped(eng, body, tiles=NT):
    with eng.Fori(0, tiles // 2) as i:
        body(i * 2, 0)
        body(i * 2 + 1, 1)


def skewed(eng, early, mixed, late):
    early(0, 0)
    mixed(0, 0, 1, 1)
    with eng.Fori(0, (NT - 4) // 2) as i:
        mixed(i * 2 + 1, 1, i * 2 + 2, 0)
        mixed(i * 2 + 2, 0, i * 2 + 3, 1)
    mixed(NT - 3, 1, NT - 2, 0)
    mixed(NT - 2, 0, NT - 1, 1)
    late(NT - 1, 1)


def there(n, count=NT):
    return type(n) is not int or 0 <= n < count


def attention16(nc, C, tag, kind, w, ahead=None):
    cross, causal, biased = kind == "cross", kind == "causal", kind == "self"
    x, ident, hmask, neghalf = C["x"], C["ident"], C["hmask"], C["neghalf"]
    m = Store(nc)
    with m.stack:
        sb, ps = m.sb, m.ps
        wq, wk, wv, wo, loaded, nload = (w[k] for k in ("wq", "wk", "wv", "wo", "loaded", "count"))
        bq, bk = w.get("bq"), w.get("bk")
        bv, bo, gamma, beta = (w.get(k) for k in ("bv", "bo", "gamma", "beta"))
        st = sb(f"{tag}st", [P, 2, 6])
        mv = sb(f"{tag}mv", [P, 2, 4])
        hn = sb(f"{tag}hn", [P, 2, D])
        hT = sb(f"{tag}hT", [P, 2, DC, P])
        qT = sb(f"{tag}qT", [P, 2, DC, P])
        KB = sb(f"{tag}KB", [P, DC, HG, P])
        V2 = sb(f"{tag}V2", [P, 2, NP, 2, OW])
        sc = sb(f"{tag}sc", [P, 2, H, S])
        mx = sb(f"{tag}mx", [P, H])
        cs = sb(f"{tag}cs", [P, 2, DC, P])
        PT = sb(f"{tag}PT", [P, 2, NP, P])
        rs = sb(f"{tag}rs", [P, 3, H])
        cn = sb(f"{tag}cn", [P, 2, D])
        cT = sb(f"{tag}cT", [P, 2, DC, P])
        dl = sb(f"{tag}dl", [P, 2, D])
        dst = sb(f"{tag}dst", [P, 6])
        dmv = sb(f"{tag}dmv", [P, 4])
        p_qk = ps(f"{tag}pqk", [P, 2, DC, P])
        p_s = ps(f"{tag}ps", [P, 2, 512])
        p_t = ps(f"{tag}pt", [P, 2, 512])
        p_o = ps(f"{tag}po", [P, 2, 512])
        p_m = ps(f"{tag}pm", [P, 512])
        p_tp = p_t[:, :, :].rearrange("p a (n t) -> p (a n) t", t=P)
        p_sc = p_s[:, :, :].rearrange("p a (h k) -> p (a h) k", k=S)
        p_st = p_s[:, :, :].rearrange("p a (n t) -> p (a n) t", t=P)
        (var_ok, rstd_ok, hn_ok, turned, hT_ok, qk_ok, q_out, k_out, v_ok, v_out, s_ok, s_out,
         exp_ok, pt_ok, pt_out, o_ok, o_out, ct_ok, ct_out, proj_ok, zeroed, dve_step, dve_d,
         dvar_ok, drstd_ok, x_step, r_step, l_step, cs_ok, m_free, dn_ok, pool_step) = m.sems(tag, "var_ok rstd_ok hn_ok turned hT_ok qk_ok q_out k_out"
                                 " v_ok v_out s_ok s_out exp_ok pt_ok pt_out o_ok o_out ct_ok ct_out proj_ok"
                                 " zeroed dve_step dve_d dvar_ok drstd_ok x_step r_step l_step cs_ok m_free dn_ok pool_step")
        ctxT = C["ctxT"]
        block = m.stack.enter_context(nc.Block())

        if ahead:
            block.sync(ahead)

        @block.gpsimd
        def _(pool):
            pool.memset(V2[:, :, :, :, :], 0.0).then_inc(zeroed, 1)
            pool.wait_ge(zeroed, 1)
            for par in range(2):
                col = par * (HD + 1) + HD
                pool.memset(V2[64 * par:64 * par + 64, :, :, :, col:col + 1], 1.0).then_inc(zeroed, 1)

            def root(n, u):
                pool.wait_ge(var_ok, n + 1)
                pool.tensor_tensor(mv[:, u, 3:4], mv[:, u, 2:3], neghalf[:, 0:1], ALU.pow).then_inc(rstd_ok, 1)

            def droot(n, u):
                pool.wait_ge(dvar_ok, n + 1)
                pool.tensor_tensor(dmv[:, 3:4], dmv[:, 2:3], neghalf[:, 0:1], ALU.pow).then_inc(drstd_ok, 1)
                pool.wait_ge(dn_ok, n + 1)
                pool.tensor_tensor(dl[:, u, :], dl[:, u, :], gamma[:, :], ALU.mult).then_inc(pool_step, 1)
                pool.wait_ge(pool_step, n * 3 + 1)
                pool.tensor_tensor(dl[:, u, :], dl[:, u, :], beta[:, :], ALU.add).then_inc(pool_step, 1)
                pool.wait_ge(pool_step, n * 3 + 2)
                xt = x[:, bass.ds(n, 1), :].rearrange("p a d -> p (a d)")
                pool.tensor_tensor(xt, xt, dl[:, u, :], ALU.add).then_inc(pool_step, 1)

            def context(n, u):
                pool.tensor_copy(cs[:, u, :, :], ctxT[:, :, bass.ds(n * P, P)]).then_inc(cs_ok, 1)

            if not cross:
                looped(pool, root)
            else:
                root(0, 0)
                context(0, 0)
                root(1, 1)
                context(1, 1)

                def both(n, u):
                    pool.wait_ge(v_ok, n + 1)
                    context(n + 2, u)
                    root(n + 2, u)
                    droot(n, u)
                looped(pool, both, NT - 2)
                droot(NT - 2, 0)
                droot(NT - 1, 1)
                pool.wait_ge(pool_step, 3 * NT)

        @block.scalar
        def _(act):
            def h_out(n, u):
                act.wait_ge(turned, n + 1)
                act.activation(hT[:, u, :, :], p_tp[:, 0:DC, :], ACT.Copy).then_inc(hT_ok, 1)

            def q_copy(n, u):
                act.wait_ge(k_out, n + 1)
                for c in range(DC):
                    if causal:
                        ins = act.activation(qT[:, u, c, :], p_qk[:, 0, c, :], ACT.Copy)
                    else:
                        ins = act.activation(qT[:, u, c, :], p_qk[:, 0, c, :], ACT.Identity,
                                             bias=(bk if cross else bq)[:, c:c + 1])
                ins.then_inc(q_out, 1)

            def exps(n, u):
                act.wait_ge(s_out, n + 1)
                act.activation(sc[:, u, :, :], sc[:, u, :, :], ACT.Exp, scale=QSCALE).then_inc(exp_ok, 1)

            def pt_copy(n, u):
                act.wait_ge(pt_ok, n + 1)
                act.activation(PT[:, u, :, :], p_tp, ACT.Copy).then_inc(pt_out, 1)

            def ct_copy(n, u):
                act.wait_ge(ct_ok, n + 1)
                act.activation(cT[:, u, :, :], p_m[:, 0:D].rearrange("p (c t) -> p c t", c=DC), ACT.Copy).then_inc(ct_out, 1)

            act.wait_ge(loaded, nload)

            def early(n, u):
                h_out(0, 0)
                q_copy(0, 0)
                h_out(1, 1)
                exps(0, 0)

            def mixed(n, u, n1, u1):
                q_copy(n1, u1)
                if not cross:
                    pt_copy(n, u)
                ct_copy(n, u)
                if there(n + 2):
                    h_out(n + 2, u)
                exps(n1, u1)

            def late(n, u):
                if not cross:
                    pt_copy(n, u)
                ct_copy(n, u)

            skewed(act, early, mixed, late)

        @block.tensor
        def _(pe):
            def turn(n, u):
                pe.wait_ge(hn_ok, n + 1)
                for c in range(DC):
                    ins = pe.transpose(p_tp[:, c, :], hn[:, u, P * c:P * c + P], ident[:, :])
                ins.then_inc(turned, 1)

            def qk(n, u):
                pe.wait_ge(hT_ok, n + 1)
                if cross:
                    pe.wait_ge(cs_ok, n + 1)
                for slot in range(2):
                    weight = (wq, wk)[slot ^ cross]
                    for g in range(DC):
                        for c in range(DC):
                            src = hT[:, u, c, :]
                            if cross and slot == 0:
                                src = cs[:, u, c, :]
                            ins = pe.matmul(p_qk[:, slot, g, :], weight[:, c, P * g:P * g + P], src,
                                            start=(c == 0), stop=(c == DC - 1))
                ins.then_inc(qk_ok, 1)

            def values(n, u):
                for c in range(DC):
                    lhs = cs[:, u, c, :] if cross else hT[:, u, c, :]
                    ins = pe.matmul(p_m[:, 0:D], lhs, wv[:, c, :], start=(c == 0), stop=(c == DC - 1))
                ins.then_inc(v_ok, 1)

            def scores(n, u):
                pe.wait_ge(q_out, n + 1)
                pe.wait_ge(k_out, n + 1)
                for g in range(DC):
                    for b in range(2):
                        ts = slice(S * b, S * b + S)
                        if not cross:
                            ins = pe.matmul(p_sc[S * b:S * b + S, HG * g:HG * g + HG, :], qT[:, u, g, ts],
                                            KB[:, g, :, ts], start=True, stop=True)
                        else:
                            for par in range(2):
                                ins = pe.matmul(p_st[S * par:S * par + S, 4 * g:4 * g + 4, ts],
                                                qT[:, u, g, ts], KB[:, g, par:HG:2, ts], start=True, stop=True)
                ins.then_inc(s_ok, 1)

            def turn_probs(n, u):
                pe.wait_ge(exp_ok, n + 1)
                for pr in range(NP):
                    ins = pe.transpose(p_tp[:, pr, :], sc[:, u, 2 * pr:2 * pr + 2, :].rearrange("p a k -> p (a k)"), ident[:, :])
                ins.then_inc(pt_ok, 1)

            def pv(n, u):
                pe.wait_ge(exp_ok if cross else pt_out, n + 1)
                pe.wait_ge(v_out, n + 1)
                E = sc[:, u, :, :].rearrange("p (a c) k -> p a (c k)", c=2)
                for pr in range(NP):
                    lhs = E[:, pr, :] if cross else PT[:, u, pr, :]
                    ins = pe.matmul(p_o[:, pr // 4, 2 * OW * (pr % 4):2 * OW * (pr % 4 + 1)], lhs,
                                    V2[:, u, pr, :, :].rearrange("p b c -> p (b c)"), start=True, stop=True)
                ins.then_inc(o_ok, 1)

            def turn_ctx(n, u):
                pe.wait_ge(o_out, n + 1)
                for c in range(DC):
                    ins = pe.transpose(p_m[:, P * c:P * c + P], cn[:, u, P * c:P * c + P], ident[:, :])
                ins.then_inc(ct_ok, 1)

            def project(n, u):
                pe.wait_ge(ct_out, n + 1)
                for c in range(DC):
                    ins = pe.matmul(p_m[:, 0:D], cT[:, u, c, :], wo[:, c, :], start=(c == 0), stop=(c == DC - 1))
                ins.then_inc(proj_ok, 1)

            pe.wait_ge(loaded, nload)
            pe.wait_ge(zeroed, 3)

            def early(n, u):
                turn(0, 0)
                qk(0, 0)
                values(0, 0)
                scores(0, 0)
                turn(1, 1)

            def mixed(n, u, n1, u1):
                qk(n1, u1)
                if not cross:
                    turn_probs(n, u)
                if type(n) is int and n == 0:
                    pe.wait_ge(v_out, 1)
                else:
                    pe.wait_ge(m_free, n)
                values(n1, u1)
                pv(n, u)
                scores(n1, u1)
                pe.wait_ge(v_out, n1 + 1)
                turn_ctx(n, u)
                if there(n + 2):
                    turn(n + 2, u)
                project(n, u)

            def late(n, u):
                if not cross:
                    turn_probs(n, u)
                pv(n, u)
                pe.wait_ge(m_free, n)
                turn_ctx(n, u)
                project(n, u)

            skewed(pe, early, mixed, late)

        @block.vector
        def _(dve):
            def norm_a(n, u, src=None):
                dve.bn_stats(st[:, u, :], x[:, bass.ds(n, 1), :].rearrange("p a d -> p (a d)"))
                dve.drain()
                dve.bn_aggr(mv[:, u, 0:2], st[:, u, :]).then_inc(dve_step, 1)
                dve.wait_ge(dve_step, n + 1)
                dve.tensor_scalar(mv[:, u, 2:3], mv[:, u, 1:2], 1e-5, None, ALU.add).then_inc(var_ok, 1)

            def norm_b(n, u):
                dve.wait_ge(rstd_ok, n + 1)
                dve.tensor_scalar(hn[:, u, :], x[:, bass.ds(n, 1), :].rearrange("p a d -> p (a d)"), mv[:, u, 0:1], mv[:, u, 3:4],
                                  ALU.subtract, ALU.mult).then_inc(hn_ok, 1)

            def k_mask(n, u):
                dve.wait_ge(qk_ok, n + 1)
                for g in range(DC):
                    src = bcast(p_qk[:, 1, g, :], 1, HG)
                    mask = bcast(hmask[:, :], 2, P)
                    if causal:
                        ins = dve.tensor_tensor(KB[:, g, :, :], src, mask, ALU.mult)
                    else:
                        ins = dve.scalar_tensor_tensor(KB[:, g, :, :], src, (bq if cross else bk)[:, g:g + 1], mask, ALU.add, ALU.mult)
                ins.then_inc(k_out, 1)

            def v_copy(n, u):
                dve.wait_ge(v_ok, n + 1)
                for b in range(2):
                    for par in range(2):
                        src = p_m[S * b:S * b + S, 0:D].rearrange("p (n a d) -> p n a d", a=2, d=HD)[:, :, par, :]
                        dst = V2[64 * par:64 * par + 64, u, :, b, par * (HD + 1):par * (HD + 1) + HD]
                        if causal:
                            ins = dve.tensor_copy(dst, src)
                        else:
                            bias = bv[S * b:S * b + S, :].rearrange("p (n a d) -> p n a d", a=2, d=HD)[:, :, par, :]
                            ins = dve.tensor_tensor(dst, src, bias, ALU.add)
                ins.then_inc(v_out, 1)

            def soft(n, u):
                dve.wait_ge(s_ok, n + 1)
                if cross:
                    E = sc[:, u, :, :].rearrange("p (a c) k -> p a (c k)", c=2)
                    for b in range(2):
                        ts = slice(S * b, S * b + S)
                        hi = C["hi"][:, bass.ds(n * 2 + b, 1)]
                        ins = dve.tensor_scalar(E[:, :, ts], p_st[:, :, ts], -50.0 / QSCALE, hi, ALU.max, ALU.min)
                    ins.then_inc(s_out, 1)
                    return
                if causal:
                    dve.tensor_tensor(sc[:, u, :, :], p_sc, bcast(C["cmask"][:, :], 1, H), ALU.add).then_inc(dve_d, 1)
                    dve.wait_ge(dve_d, n * 2 + 1)
                src = sc[:, u, :, :] if causal else p_sc
                dve.tensor_reduce(mx[:, :], src, AX.X, ALU.max).then_inc(dve_d, 1)
                dve.wait_ge(dve_d, n * 2 + 2 if causal else n + 1)
                dve.tensor_tensor(sc[:, u, :, :], src, bcast(mx[:, :], 2, S), ALU.subtract).then_inc(s_out, 1)

            def o_norm(n, u):
                dve.wait_ge(o_ok, n + 1)
                O = p_o[:, :, 0:8 * OW].rearrange("p a (n b e d) -> p a n b e d", n=4, b=2, e=2)
                for b in range(2):
                    r = slice(S * b, S * b + S)
                    ins = dve.reciprocal(rs[r, 0, :].rearrange("p (a n e) -> p a n e", a=2, e=2), O[r, :, :, b, :, HD])
                    if cross:
                        ins = dve.tensor_copy(rs[r, 1, :].rearrange("p (a n e) -> p a n e", a=2, e=2), O[r, :, :, b, :, HD])
                steps = 4 if cross else 1
                ins.then_inc(x_step, 1)
                dve.wait_ge(x_step, n * steps + 1)
                if cross:
                    dve.tensor_tensor(rs[:, 1, :], rs[:, 1, :], rs[:, 0, :], ALU.mult).then_inc(x_step, 1)
                    dve.wait_ge(x_step, n * steps + 2)
                    dve.tensor_scalar(rs[:, 1, :], rs[:, 1, :], 1e-8, None, ALU.add).then_inc(x_step, 1)
                    dve.wait_ge(x_step, n * steps + 3)
                    dve.reciprocal(rs[:, 2, :], rs[:, 1, :]).then_inc(x_step, 1)
                    dve.wait_ge(x_step, n * steps + 4)
                    dve.tensor_tensor(rs[:, 0, :], rs[:, 0, :], rs[:, 2, :], ALU.mult).then_inc(r_step, 1)
                    dve.wait_ge(r_step, n + 1)
                for b in range(2):
                    r = slice(S * b, S * b + S)
                    for a in range(2):
                        dst = cn[r, u, P * a:P * a + P].rearrange("p (n e d) -> p n e d", e=2, d=HD)
                        rr = bcast(rs[r, 0, 8 * a:8 * a + 8].rearrange("p (n e) -> p n e", e=2), 3, HD)
                        ins = dve.tensor_tensor(dst, O[r, a, :, b, :, 0:HD], rr, ALU.mult)
                ins.then_inc(o_out, 1)

            def residual(n, u):
                xt = x[:, bass.ds(n, 1), :].rearrange("p a d -> p (a d)")
                dve.wait_ge(proj_ok, n + 1)
                if causal:
                    dve.tensor_tensor(xt, xt, p_m[:, 0:D], ALU.add).then_inc(m_free, 1)
                elif biased:
                    dve.tensor_tensor(dl[:, u, :], p_m[:, 0:D], bo[:, :], ALU.add).then_inc(m_free, 1)
                    dve.wait_ge(m_free, n + 1)
                    dve.tensor_tensor(xt, xt, dl[:, u, :], ALU.add)
                else:
                    dve.tensor_tensor(dl[:, u, :], p_m[:, 0:D], bo[:, :], ALU.add).then_inc(m_free, 1)
                    dve.wait_ge(m_free, n + 1)
                    dve.tensor_scalar(dl[:, u, :], dl[:, u, :], C["rs"][:, 0:1], None, ALU.mult)
                    dve.drain()
                    dve.bn_stats(dst[:, :], dl[:, u, :])
                    dve.drain()
                    dve.bn_aggr(dmv[:, 0:2], dst[:, :]).then_inc(l_step, 1)
                    dve.wait_ge(l_step, n + 1)
                    dve.tensor_scalar(dmv[:, 2:3], dmv[:, 1:2], 1e-5, None, ALU.add).then_inc(dvar_ok, 1)
                    dve.wait_ge(drstd_ok, n + 1)
                    dve.tensor_scalar(dl[:, u, :], dl[:, u, :], dmv[:, 0:1], dmv[:, 3:4], ALU.subtract, ALU.mult).then_inc(dn_ok, 1)

            dve.wait_ge(loaded, nload)
            dve.wait_ge(zeroed, 3)

            def early(n, u):
                norm_a(0, 0)
                norm_b(0, 0)
                norm_a(1, 1)
                norm_b(1, 1)
                k_mask(0, 0)
                v_copy(0, 0)
                soft(0, 0)

            def mixed(n, u, n1, u1):
                if there(n + 2):
                    norm_a(n + 2, u)
                k_mask(n1, u1)
                v_copy(n1, u1)
                o_norm(n, u)
                if there(n + 2):
                    norm_b(n + 2, u)
                soft(n1, u1)
                residual(n, u)

            def late(n, u):
                o_norm(n, u)
                residual(n, u)

            skewed(dve, early, mixed, late)


def moved(sp, done, pairs):
    for dst, src in pairs:
        sp.dma_start(dst, src).then_inc(done, 16)
    return 16 * len(pairs)


XH, KVH, XD = 16, 4, 128
XSCALE = float(1.0 / np.sqrt(np.float32(XD)))
RH = XD // 2
KEYS = 2 * S
NTAB = B + NT
TWO_PI = 6.283185307179586
PI_A = float(np.frombuffer(np.array([np.float32(TWO_PI).view(np.uint32) & 0xFFFF8000], np.uint32).tobytes(), np.float32)[0])
PI_B = float(np.frombuffer(np.array([np.float32(TWO_PI - PI_A).view(np.uint32) & 0xFFFF8000], np.uint32).tobytes(), np.float32)[0])
PI_C = float(np.float32(TWO_PI - PI_A - PI_B))
ROUND = 12582912.0
PI_MAX = 3.1415925


def rope_tables(nc, C, a):
    m = Store(nc)
    with m.stack:
        posi = m.sb("posi", [P, NTAB], I32)
        pos = m.sb("pos", [P, NTAB])
        inv = m.sb("inv", [P, RH])
        nw = m.sb("nw", [P, 2, XD])
        ang = m.sb("ang", [P, NTAB, RH])
        turns = m.sb("turns", [P, NTAB, RH])
        red = m.sb("red", [P, 2, NTAB, RH])
        tin, step, trig = m.sems("tab", "in step trig")
        tc, ts = C["tab_c"], C["tab_s"]
        with nc.Block() as block:
            @block.sync
            def _(sp):
                n = moved(sp, tin, [(posi[:, :], a["pos"]), (inv[:, :], a["inv"].to_broadcast([P, RH])),
                                    (nw[:, 0, :], a["kw"].to_broadcast([P, XD])), (nw[:, 1, :], a["qw"].to_broadcast([P, XD]))])
                sp.wait_ge(tin, n)

            @block.vector
            def _(dve):
                done = [0]

                def then(ins):
                    done[0] += 1
                    ins.then_inc(step, 1)
                    dve.wait_ge(step, done[0])

                dve.wait_ge(tin, 64)
                then(dve.tensor_copy(pos[:, :], posi[:, :]))
                then(dve.tensor_tensor(ang[:, :, :], bcast(pos[:, :], 2, RH), bcast(inv[:, :], 1, NTAB), ALU.mult))
                for k in range(2):
                    then(dve.tensor_scalar(turns[:, :, :], ang[:, :, :], 1.0 / TWO_PI, 0.25 * k, ALU.mult, ALU.add))
                    then(dve.tensor_scalar(turns[:, :, :], turns[:, :, :], ROUND, None, ALU.add))
                    then(dve.tensor_scalar(turns[:, :, :], turns[:, :, :], -ROUND, None, ALU.add))
                    then(dve.scalar_tensor_tensor(red[:, k, :, :], turns[:, :, :], -PI_A, ang[:, :, :], ALU.mult, ALU.add))
                    then(dve.scalar_tensor_tensor(red[:, k, :, :], turns[:, :, :], -PI_B, red[:, k, :, :], ALU.mult, ALU.add))
                    then(dve.scalar_tensor_tensor(red[:, k, :, :], turns[:, :, :], -PI_C, red[:, k, :, :], ALU.mult, ALU.add))
                    then(dve.tensor_scalar(red[:, k, :, :], red[:, k, :, :], k * TWO_PI / 4, PI_MAX, ALU.add, ALU.min))
                    then(dve.tensor_scalar(red[:, k, :, :], red[:, k, :, :], -PI_MAX, None, ALU.max))
                dve.wait_ge(trig, 1)
                for which, r in ((0, slice(0, B)), (1, slice(B, NTAB))):
                    n = r.stop - r.start
                    for half in range(2):
                        mine, other = slice(RH * half, RH * half + RH), slice(RH * (1 - half), RH * (1 - half) + RH)
                        dve.tensor_tensor(tc[:, r, mine], red[:, 1, r, :], bcast(nw[:, which, mine], 1, n), ALU.mult)
                        last = dve.scalar_tensor_tensor(ts[:, r, mine], red[:, 0, r, :], 2.0 * half - 1.0,
                                                        bcast(nw[:, which, other], 1, n), ALU.mult, ALU.mult)
                last.then_inc(step, 1)
                dve.wait_ge(step, done[0] + 1)

            @block.scalar
            def _(act):
                act.wait_ge(step, 18)
                act.activation(red[:, :, :, :], red[:, :, :, :], ACT.Sin).then_inc(trig, 1)
                act.wait_ge(trig, 1)


def attention128(nc, C, w):
    x, ident, neghalf, ctxT = C["x"], C["ident"], C["neghalf"], C["ctxT"]
    tc, ts = C["tab_c"], C["tab_s"]
    m = Store(nc)
    NSQ = XH + 2 * KVH
    with m.stack:
        sb, ps = m.sb, m.ps
        wq, wk, wv, wo, loaded = (w[k] for k in ("wq", "wk", "wv", "wo", "loaded"))
        st = sb("xst", [P, 2, 6])
        mv = sb("xmv", [P, 2, 4])
        hn = sb("xhn", [P, 2, D])
        kv = sb("xkv", [P, 2, DC, 2, KEYS])
        qr = sb("xqr", [P, NSQ, XD])
        t2 = sb("xt2", [P, 2, 4, XD])
        sq = sb("xsq", [P, 2, 4, XD])
        ss = sb("xss", [P, NSQ])
        sv = sb("xsv", [P, NSQ])
        sr = sb("xsr", [P, NSQ])
        V = sb("xV", [P, 2, 2, KVH, XD])
        QT = sb("xQT", [P, 2, XH, S])
        KT = sb("xKT", [P, 2 * KVH, KEYS])
        hT = sb("xhT", [P, 2, DC, P])
        E = sb("xE", [P, XH, KEYS])
        mx = sb("xmx", [P, XH])
        nb = sb("xnb", [P, XH])
        sm = sb("xsm", [P, XH])
        rc = sb("xrc", [P, XH])
        PT = sb("xPT", [P, 2, 4, P])
        OT = sb("xOT", [P, XH, 2, S])
        p_r = [ps(f"xpr{i}", [P, 4, XD]) for i in range(2)]
        p_t = [ps(f"xpt{i}", [P, 4, P]) for i in range(2)]
        p_s = [ps(f"xps{i}", [P, 4, KEYS]) for i in range(2)]
        p_o = [ps(f"xpo{i}", [P, 512]) for i in range(2)]
        (stat_ok, var_ok, rstd_ok, hn_ok, ctx_ok, r_ok, sq_ok, rope_ok, v_out, add_ok, ms_ok, sr_ok, ss_ok,
         scaled, t_ok, t_out, s_ok, max_ok, nb_ok, exp_ok, rc_ok, e_ok, o_ok, o_out, proj_ok, x_ok) = m.sems(
            "x", "stat_ok var_ok rstd_ok hn_ok ctx_ok r_ok sq_ok rope_ok v_out add_ok ms_ok sr_ok ss_ok"
                 " scaled t_ok t_out s_ok max_ok nb_ok exp_ok rc_ok e_ok o_ok o_out proj_ok x_ok")
        FIRST_T, STEP_T = 6, 11
        T_K, T_P, T_Q, T_H = (0, 1), (2, 3, 4, 6), (5, 7, 8, 10), 9

        def turns(n, u):
            base = n * STEP_T + FIRST_T
            if type(n) is int and n == NT - 1:
                base -= 1
                return base, lambda k: (base + k) % 2
            return base, lambda k: (u + k) % 2

        def t_q(n, i):
            return T_Q[i] - (i == 3 and not there(n + 2))

        block = m.stack.enter_context(nc.Block())

        @block.gpsimd
        def _(pool):
            def root(n, u):
                pool.wait_ge(var_ok, n + 1)
                pool.tensor_tensor(mv[:, u, 3:4], mv[:, u, 2:3], neghalf[:, 0:1], ALU.pow).then_inc(rstd_ok, 1)

            def context(n, u):
                pool.wait_ge(t_out, n + 1 if type(n) is int and n < 2 else (n - 2) * STEP_T + FIRST_T + T_H + 1)
                for c in range(DC):
                    pool.tensor_copy(kv[:, u, c, :, 0:S], ctxT[:, c, bass.ds(n * P, P)].rearrange("p (b k) -> p b k", b=2))
                for c in range(DC):
                    ins = pool.tensor_copy(kv[:, u, c, :, S:KEYS], hT[:, u, c, :].rearrange("p (b k) -> p b k", b=2))
                ins.then_inc(ctx_ok, 1)

            def add(n, k):
                pool.wait_ge(rope_ok, n * 6 + k + 1)
                blk = qr[:, 4 * k:4 * k + 4, :]
                pool.tensor_tensor(blk, blk, t2[:, k % 2, :, :], ALU.add).then_inc(add_ok, 1)

            def rms_root(n, part):
                pool.wait_ge(ms_ok, n * 2 + part + 1)
                c = RMS[part]
                pool.tensor_tensor(sr[:, c], sv[:, c], neghalf[:, 0:1].to_broadcast([P, c.stop - c.start]), ALU.pow).then_inc(sr_ok, 1)

            def step(n1, u1):
                for k in range(4):
                    add(n1, k)
                rms_root(n1, 0)
                add(n1, 4)
                if type(n1) is not int or 1 <= n1 < NT - 1:
                    root(n1 + 1, 1 - u1)
                add(n1, 5)
                rms_root(n1, 1)
                if there(n1 + 1):
                    context(n1 + 1, 1 - u1)

            root(0, 0)
            root(1, 1)
            context(0, 0)
            step(0, 0)
            step(1, 1)
            with pool.Fori(0, (NT - 4) // 2) as i:
                step(i * 2 + 2, 0)
                step(i * 2 + 3, 1)
            step(NT - 2, 0)
            step(NT - 1, 1)

        @block.scalar
        def _(act):
            def turned(j, dst, src):
                act.wait_ge(t_ok, j + 1)
                act.activation(dst, src, ACT.Copy).then_inc(t_out, 1)

            def h_out(n, u, j, bank):
                turned(j, hT[:, u, :, :], p_t[bank][:, 0:DC, :])

            def qk_out(j, i, bank):
                if i < 4:
                    dst = QT[:, :, 4 * i:4 * i + 4, :]
                    turned(j, dst.rearrange("p b h q -> p h b q"), p_t[bank][:, :, :].rearrange("p h (b q) -> p h b q", b=2))
                else:
                    turned(j, KT[:, 4 * (i - 4):4 * (i - 4) + 4, :], p_t[bank][:, :, :])

            def square(n, k):
                act.wait_ge(r_ok, n * 8 + k + 1)
                act.activation(sq[:, SQI[k] % 2, :, :], p_r[k % 2][:, :, :], ACT.Square).then_inc(sq_ok, 1)

            def v_copy(n, u, k):
                act.wait_ge(r_ok, n * 8 + k + 1)
                act.activation(V[:, u, (k - 5) // 2, :, :], p_r[k % 2][:, :, :], ACT.Copy).then_inc(v_out, 1)

            def exps(n, k):
                act.wait_ge(nb_ok, n * 4 + k + 1)
                for i in range(4):
                    c = 4 * k + i
                    ins = act.activation(E[:, c, :], p_s[k % 2][:, i, :], ACT.Exp, bias=nb[:, c:c + 1], scale=XSCALE,
                                         accum_out=sm[:, c:c + 1])
                ins.then_inc(exp_ok, 1)

            def pt_copy(n, k, j, bank):
                turned(j, PT[:, k % 2, :, :], p_t[bank][:, :, :])

            def o_copy(n, u, k):
                act.wait_ge(o_ok, n * 4 + k + 1)
                act.activation(OT[:, 8 * (k % 2):8 * (k % 2) + 8, k // 2, :],
                               p_o[(u + k) % 2][:, :].rearrange("p (h q) -> p h q", q=S), ACT.Copy).then_inc(o_out, 1)

            def early(n, u):
                h_out(0, 0, 0, 0)
                h_out(1, 1, 1, 1)
                for k in (0, 1, 2, 3, 4):
                    square(0, k)
                v_copy(0, 0, 5)
                square(0, 6)
                v_copy(0, 0, 7)
                for i in range(4):
                    qk_out(2 + i, i, i % 2)

            def mixed(n, u, n1, u1):
                base, bank = turns(n, u)
                square(n1, 0)
                qk_out(base + T_K[0], 4, bank(T_K[0]))
                square(n1, 1)
                qk_out(base + T_K[1], 5, bank(T_K[1]))
                square(n1, 2)
                exps(n, 0)
                square(n1, 3)
                exps(n, 1)
                square(n1, 4)
                pt_copy(n, 0, base + T_P[0], bank(T_P[0]))
                v_copy(n1, u1, 5)
                pt_copy(n, 1, base + T_P[1], bank(T_P[1]))
                o_copy(n, u, 0)
                exps(n, 2)
                o_copy(n, u, 1)
                square(n1, 6)
                exps(n, 3)
                pt_copy(n, 2, base + T_P[2], bank(T_P[2]))
                qk_out(base + T_Q[0], 0, bank(T_Q[0]))
                v_copy(n1, u1, 7)
                pt_copy(n, 3, base + T_P[3], bank(T_P[3]))
                qk_out(base + T_Q[1], 1, bank(T_Q[1]))
                o_copy(n, u, 2)
                qk_out(base + T_Q[2], 2, bank(T_Q[2]))
                if there(n + 2):
                    h_out(n + 2, u, base + T_H, bank(T_H))
                o_copy(n, u, 3)
                qk_out(base + t_q(n, 3), 3, bank(t_q(n, 3)))

            def late(n, u):
                base, bank = turns(n, u)
                qk_out(base, 4, bank(0))
                qk_out(base + 1, 5, bank(1))
                exps(n, 0)
                exps(n, 1)
                pt_copy(n, 0, base + 2, bank(2))
                pt_copy(n, 1, base + 3, bank(3))
                o_copy(n, u, 0)
                exps(n, 2)
                o_copy(n, u, 1)
                exps(n, 3)
                pt_copy(n, 2, base + 4, bank(4))
                pt_copy(n, 3, base + 5, bank(5))
                o_copy(n, u, 2)
                o_copy(n, u, 3)

            skewed(act, early, mixed, late)

        @block.tensor
        def _(pe):
            def turn_h(n, u, j, bank):
                pe.wait_ge(hn_ok, n + 1)
                for c in range(DC):
                    ins = pe.transpose(p_t[bank][:, c, :], hn[:, u, P * c:P * c + P], ident[:, :])
                ins.then_inc(t_ok, 1)

            def fill(n, u, k, first=False):
                freed = {0: (rope_ok, n * 6), 1: (v_out, n * 2), 2: (rope_ok, n * 6 + 1), 3: (rope_ok, n * 6 + 2),
                         4: (rope_ok, n * 6 + 3), 5: (rope_ok, n * 6 + 4), 6: (rope_ok, n * 6 + 5), 7: (v_out, n * 2 + 1)}
                pe.wait_ge(*freed[k])
                for c in range(DC):
                    if k < 4:
                        lhs, rhs = hT[:, u, c, :], wq[:, c, 512 * k:512 * k + 512]
                    else:
                        lhs, rhs = kv[:, u, c, (k - 4) // 2, :], (wk, wv)[k % 2][:, c, :]
                    ins = pe.matmul(p_r[k % 2][:, :, :].rearrange("p h d -> p (h d)"), lhs, rhs, start=(c == 0), stop=(c == DC - 1))
                ins.then_inc(r_ok, 1)

            def scores(n, k):
                b, half = k // 2, k % 2
                pe.wait_ge(exp_ok, n * 4 + max(k - 1, 0))
                for i in range(4):
                    h = 8 * half + 2 * i
                    ins = pe.matmul(p_s[k % 2][:, i, :], QT[:, b, h:h + 2, :].rearrange("p h q -> p (h q)"),
                                    KT[:, KVH * b + h // 4, :], start=True, stop=True)
                ins.then_inc(s_ok, 1)

            def turn_probs(n, k, j, bank):
                pe.wait_ge(e_ok, n * 4 + k + 1)
                pe.wait_ge(t_out, j - 1)
                for i in range(4):
                    ins = pe.transpose(p_t[bank][:, i, :], E[:, 4 * k + i, :], ident[:, :])
                ins.then_inc(t_ok, 1)

            def pv(n, u, k, j):
                pe.wait_ge(t_out, j + 1)
                if k == 1:
                    pe.wait_ge(x_ok, n)
                else:
                    pe.wait_ge(o_out, n * 4 + max(k - 1, 0))
                if k == 0:
                    pe.wait_ge(v_out, n * 2 + 2)
                for g in range(2):
                    ins = pe.matmul(p_o[(u + k) % 2][:, 256 * g:256 * g + 256], V[:, u, k // 2, 2 * (k % 2) + g, :],
                                    PT[:, k % 2, 2 * g:2 * g + 2, :].rearrange("p i q -> p (i q)"), start=True, stop=True)
                ins.then_inc(o_ok, 1)

            def project(n, u, quarter):
                if quarter == 0:
                    pe.wait_ge(o_out, n * 4 + 4)
                for h in range(4 * quarter, 4 * quarter + 4):
                    ins = pe.matmul(p_o[u][:, 0:D], OT[:, h, :, :].rearrange("p b q -> p (b q)"), wo[:, h, :],
                                    start=(h == 0), stop=(h == XH - 1))
                if quarter == 3:
                    ins.then_inc(proj_ok, 1)

            def turn_qk(n, i, j, bank):
                pe.wait_ge(scaled, n * 6 + i + 1)
                pe.wait_ge(t_out, j - 1)
                for c in range(4):
                    ins = pe.transpose(p_t[bank][:, c, :], qr[:, 4 * i + c, :], ident[:, :])
                ins.then_inc(t_ok, 1)

            pe.wait_ge(loaded, 64)

            def early(n, u):
                turn_h(0, 0, 0, 0)
                turn_h(1, 1, 1, 1)
                pe.wait_ge(t_out, 1)
                for k in range(8):
                    if k == 4:
                        pe.wait_ge(ctx_ok, 1)
                    fill(0, 0, k)
                for i in range(4):
                    turn_qk(0, i, 2 + i, i % 2)

            def mixed(n, u, n1, u1):
                base, bank = turns(n, u)

                def project_before(quarter):
                    if there(n - 1):
                        project(n - 1, 1 - u, quarter)

                pe.wait_ge(t_out, base - 1)
                fill(n1, u1, 0)
                turn_qk(n, 4, base + T_K[0], bank(T_K[0]))
                project_before(0)
                fill(n1, u1, 1)
                turn_qk(n, 5, base + T_K[1], bank(T_K[1]))
                project_before(1)
                pe.wait_ge(t_out, base + 2)
                scores(n, 0)
                fill(n1, u1, 2)
                scores(n, 1)
                project_before(2)
                fill(n1, u1, 3)
                project_before(3)
                pe.wait_ge(ctx_ok, n1 + 1)
                fill(n1, u1, 4)
                turn_probs(n, 0, base + T_P[0], bank(T_P[0]))
                fill(n1, u1, 5)
                turn_probs(n, 1, base + T_P[1], bank(T_P[1]))
                pv(n, u, 0, base + T_P[0])
                scores(n, 2)
                pv(n, u, 1, base + T_P[1])
                scores(n, 3)
                fill(n1, u1, 6)
                turn_probs(n, 2, base + T_P[2], bank(T_P[2]))
                turn_qk(n1, 0, base + T_Q[0], bank(T_Q[0]))
                fill(n1, u1, 7)
                turn_probs(n, 3, base + T_P[3], bank(T_P[3]))
                turn_qk(n1, 1, base + T_Q[1], bank(T_Q[1]))
                pv(n, u, 2, base + T_P[2])
                turn_qk(n1, 2, base + T_Q[2], bank(T_Q[2]))
                if there(n + 2):
                    pe.wait_ge(t_out, base + T_H - 1)
                    turn_h(n + 2, u, base + T_H, bank(T_H))
                pv(n, u, 3, base + T_P[3])
                turn_qk(n1, 3, base + t_q(n, 3), bank(t_q(n, 3)))

            def late(n, u):
                base, bank = turns(n, u)
                turn_qk(n, 4, base, bank(0))
                turn_qk(n, 5, base + 1, bank(1))
                for quarter in range(4):
                    project(n - 1, 1 - u, quarter)
                pe.wait_ge(t_out, base + 2)
                scores(n, 0)
                scores(n, 1)
                turn_probs(n, 0, base + 2, bank(2))
                turn_probs(n, 1, base + 3, bank(3))
                pv(n, u, 0, base + 2)
                scores(n, 2)
                pv(n, u, 1, base + 3)
                scores(n, 3)
                turn_probs(n, 2, base + 4, bank(4))
                turn_probs(n, 3, base + 5, bank(5))
                pv(n, u, 2, base + 4)
                pv(n, u, 3, base + 5)
                for quarter in range(4):
                    project(n, u, quarter)

            skewed(pe, early, mixed, late)

        @block.vector
        def _(dve):
            def tile_of(n):
                return x[:, bass.ds(n, 1), :].rearrange("p a d -> p (a d)")

            def norm_a(n, u):
                dve.bn_stats(st[:, u, :], tile_of(n))
                dve.drain()
                dve.bn_aggr(mv[:, u, 0:2], st[:, u, :]).then_inc(stat_ok, 1)
                dve.wait_ge(stat_ok, n + 1)
                dve.tensor_scalar(mv[:, u, 2:3], mv[:, u, 1:2], 1e-5, None, ALU.add).then_inc(var_ok, 1)

            def norm_b(n, u):
                dve.wait_ge(rstd_ok, n + 1)
                dve.tensor_scalar(hn[:, u, :], tile_of(n), mv[:, u, 0:1], mv[:, u, 3:4], ALU.subtract, ALU.mult).then_inc(hn_ok, 1)

            def rope(n, i):
                k = RING[i]
                src, blk = p_r[k % 2], qr[:, 4 * i:4 * i + 4, :]
                row = n + B if i < 4 else n * 2 + (i - 4)
                dve.wait_ge(sq_ok, n * 6 + i + 1)
                if type(n) is not int or n * 6 + i > 1:
                    dve.wait_ge(add_ok, n * 6 + i - 1)
                cosw = tc[:, bass.ds(row, 1), :].rearrange("p a d -> p (a d)")
                sinw = ts[:, bass.ds(row, 1), :].rearrange("p a d -> p (a d)")
                dve.tensor_reduce(ss[:, 4 * i:4 * i + 4], sq[:, i % 2, :, :], AX.X, ALU.add).then_inc(ss_ok, 1)
                dve.tensor_tensor(blk, src[:, :, :], bcast(cosw, 1, 4), ALU.mult)
                for half in range(2):
                    mine, other = slice(RH * half, RH * half + RH), slice(RH * (1 - half), RH * (1 - half) + RH)
                    ins = dve.tensor_tensor(t2[:, i % 2, :, mine], src[:, :, other], bcast(sinw[:, mine], 1, 4), ALU.mult)
                ins.then_inc(rope_ok, 1)

            def mean_square(n, part):
                dve.wait_ge(ss_ok, n * 6 + (4, 6)[part])
                dve.tensor_scalar(sv[:, RMS[part]], ss[:, RMS[part]], 1.0 / XD, 1e-6, ALU.mult, ALU.add).then_inc(ms_ok, 1)

            def scale(n, i):
                dve.wait_ge(sr_ok, n * 2 + i // 4 + 1)
                dve.wait_ge(add_ok, n * 6 + i + 1)
                blk = qr[:, 4 * i:4 * i + 4, :]
                dve.tensor_tensor(blk, blk, bcast(sr[:, 4 * i:4 * i + 4], 2, XD), ALU.mult).then_inc(scaled, 1)

            def maxes(n, k):
                c = slice(4 * k, 4 * k + 4)
                dve.wait_ge(s_ok, n * 4 + k + 1)
                dve.tensor_reduce(mx[:, c], p_s[k % 2][:, :, :], AX.X, ALU.max).then_inc(max_ok, 1)
                dve.wait_ge(max_ok, n * 4 + k + 1)
                dve.tensor_scalar(nb[:, c], mx[:, c], -XSCALE, None, ALU.mult).then_inc(nb_ok, 1)

            def normalise(n, k):
                c = slice(4 * k, 4 * k + 4)
                dve.wait_ge(exp_ok, n * 4 + k + 1)
                dve.reciprocal(rc[:, c], sm[:, c]).then_inc(rc_ok, 1)
                dve.wait_ge(rc_ok, n * 4 + k + 1)
                dve.tensor_tensor(E[:, c, :], E[:, c, :], bcast(rc[:, c], 2, KEYS), ALU.mult).then_inc(e_ok, 1)

            def residual(n, u):
                dve.wait_ge(proj_ok, n + 1)
                dve.tensor_tensor(tile_of(n), tile_of(n), p_o[u][:, 0:D], ALU.add).then_inc(x_ok, 1)

            def early(n, u):
                norm_a(0, 0)
                norm_b(0, 0)
                norm_a(1, 1)
                norm_b(1, 1)
                for i in range(4):
                    rope(0, i)
                mean_square(0, 0)
                rope(0, 4)
                rope(0, 5)
                mean_square(0, 1)
                for i in range(6):
                    scale(0, i)

            def mixed(n, u, n1, u1):
                rope(n1, 0)
                rope(n1, 1)
                maxes(n, 0)
                rope(n1, 2)
                maxes(n, 1)
                normalise(n, 0)
                rope(n1, 3)
                mean_square(n1, 0)
                normalise(n, 1)
                if there(n - 1):
                    residual(n - 1, 1 - u)
                rope(n1, 4)
                if there(n + 2):
                    norm_a(n + 2, u)
                maxes(n, 2)
                scale(n1, 0)
                maxes(n, 3)
                normalise(n, 2)
                rope(n1, 5)
                mean_square(n1, 1)
                normalise(n, 3)
                scale(n1, 1)
                if there(n + 2):
                    norm_b(n + 2, u)
                for i in range(2, 6):
                    scale(n1, i)

            def late(n, u):
                maxes(n, 0)
                maxes(n, 1)
                residual(n - 1, 1 - u)
                normalise(n, 0)
                normalise(n, 1)
                maxes(n, 2)
                maxes(n, 3)
                normalise(n, 2)
                normalise(n, 3)
                residual(n, u)

            skewed(dve, early, mixed, late)


SQI = {0: 0, 1: 1, 2: 2, 3: 3, 4: 4, 6: 5}
RING = (0, 1, 2, 3, 4, 6)
RMS = (slice(0, XH), slice(XH, XH + 2 * KVH))


E1, K1, I1 = 64, 8, 64
NPAIR = E1 // 2 + 1
WROWS = 2 * NPAIR
CH = 512
NCH = B * S // CH
H_UP, W_UP = 32.0, 64.0
PASSES = ((0, 0), (1, 0), (0, 1))


def moe_dense(nc, C, a):
    x, ident, neghalf = C["x"], C["ident"], C["neghalf"]
    m = Store(nc)
    wt_dram = nc.dram_tensor("wt_dram", [WROWS, B * S], F32, kind="Internal").ap()
    with m.stack:
        hs = m.sb("m1hs", [P, 2, DC, B * S], F16)
        NR = 3
        GU = DC * 2 * P
        raw = m.sb("m1raw", [P, NR, GU + D])
        ws = m.sb("m1ws", [P, NR, 2, GU + D], F16)
        w_in = [m.sem(f"m1_w_in{u}") for u in range(NR)]
        high_ok, prep_ok = m.sems("m1", "high_ok prep_ok")

        def load_raw(sp, p, u):
            sp.dma_start(raw[:, u, :], a["m1_w"][bass.ds(p, 1), :, :].rearrange("a p n -> p (a n)")).then_inc(w_in[u], 16)

        def low_part(pool, p, u):
            pool.wait_ge(high_ok, p + 1)
            pool.tensor_tensor(ws[:, u, 1, :], raw[:, u, :], ws[:, u, 0, :], ALU.subtract).then_inc(prep_ok, 1)

        def scaled_raw(act, u):
            act.activation(raw[:, u, :], raw[:, u, :], ACT.Copy, scale=W_UP).then_inc(high_ok, 1)

        r = Store(nc)
        with r.stack:
            gate = r.sb("m1gate", [P, DC, E1 + 1])
            st = r.sb("m1st", [P, NT, 6])
            mv = r.sb("m1mv", [P, NT, 2])
            ve = r.sb("m1ve", [P, NT])
            rstd = r.sb("m1rstd", [P, NT])
            hn = r.sb("m1hn", [P, 2, D])
            hT = r.sb("m1hT", [P, 2, DC, P])
            lg = r.sb("m1lg", [P, NT, E1 + 1])
            top = r.sb("m1top", [P, NT, 8])
            rest = r.sb("m1rest", [P, NT, E1])
            df = r.sb("m1df", [P, NT, E1])
            ex = r.sb("m1ex", [P, NT, E1])
            sg1 = r.sb("m1sg1", [P, NT, 1])
            sm = r.sb("m1sm", [P, 2, NT])
            rc = r.sb("m1rc", [P, 2, NT])
            W = r.sb("m1W", [P, NT, WROWS])
            WT = r.sb("m1WT", [WROWS, B * S])
            p_t = [r.ps(f"m1pt{i}", [P, DC, P]) for i in range(2)]
            p_l = [r.ps(f"m1pl{i}", [P, 512]) for i in range(2)]
            p_w = [r.ps(f"m1pw{i}", [P, CH]) for i in range(NCH)]
            (loaded, stat_ok, var_ok, rstd_ok, hn_ok, t_ok, hT_ok, hi_ok, lo_ok, l_ok, lg_ok, top_ok, ex_ok,
             step, W_ok, w_ok, WT_ok, stored) = r.sems(
                "m1", "loaded stat_ok var_ok rstd_ok hn_ok t_ok hT_ok hi_ok lo_ok l_ok lg_ok top_ok ex_ok"
                      " step W_ok w_ok WT_ok stored")
            with nc.Block() as block:
                @block.sync
                def _(sp):
                    moved(sp, loaded, [(gate[:, :, :], a["m1_gate"])])
                    for p in range(NR):
                        load_raw(sp, p, p)
                    for q in range(NCH):
                        sp.wait_ge(WT_ok, q + 1)
                        sp.dma_start(wt_dram[:, CH * q:CH * q + CH], WT[:, CH * q:CH * q + CH]).then_inc(stored, 16)
                    sp.wait_ge(stored, 16 * NCH)

                @block.gpsimd
                def _(pool):
                    pool.wait_ge(var_ok, 1)
                    pool.tensor_tensor(rstd[:, :], ve[:, :], neghalf[:, 0:1].to_broadcast([P, NT]), ALU.pow).then_inc(rstd_ok, 1)
                    pool.memset(W[:, :, E1 + 1:WROWS], 0.0).then_inc(W_ok, 1)
                    for p in range(NR):
                        low_part(pool, p, p)

                @block.scalar
                def _(act):
                    def inputs(n, u):
                        act.wait_ge(t_ok, n + 1)
                        act.activation(hT[:, u, :, :], p_t[u][:, :, :], ACT.Copy).then_inc(hT_ok, 1)
                        act.activation(hs[:, 0, :, bass.ds(n * P, P)], p_t[u][:, :, :], ACT.Copy, scale=H_UP).then_inc(hi_ok, 1)

                    def logits(n, u):
                        act.wait_ge(l_ok, n + 1)
                        act.activation(lg[:, bass.ds(n, 1), :].rearrange("p a e -> p (a e)"), p_l[u][:, 0:E1 + 1], ACT.Copy).then_inc(lg_ok, 1)

                    def mixed(n, u, n1, u1):
                        inputs(n1, u1)
                        logits(n, u)
                    skewed(act, inputs, mixed, logits)
                    act.wait_ge(lg_ok, NT)
                    act.activation(sg1[:, :, :], lg[:, :, E1:E1 + 1], ACT.Exp, scale=-1.0).then_inc(ex_ok, 1)
                    act.wait_ge(top_ok, NT + 1)
                    act.activation(ex[:, :, :], df[:, :, :], ACT.Exp).then_inc(ex_ok, 1)
                    for p in range(NR):
                        act.wait_ge(w_in[p], 16)
                        act.activation(ws[:, p, 0, :], raw[:, p, :], ACT.Copy, scale=W_UP)
                        scaled_raw(act, p)
                    for q in range(NCH):
                        act.wait_ge(w_ok, q + 1)
                        act.activation(WT[:, CH * q:CH * q + CH], p_w[q][0:WROWS, :], ACT.Copy).then_inc(WT_ok, 1)

                @block.tensor
                def _(pe):
                    def turn(n, u):
                        pe.wait_ge(hn_ok, n + 1)
                        if type(n) is not int or n >= 2:
                            pe.wait_ge(lo_ok, n - 1)
                        for c in range(DC):
                            ins = pe.transpose(p_t[u][:, c, :], hn[:, u, P * c:P * c + P], ident[:, :])
                        ins.then_inc(t_ok, 1)

                    def route(n, u):
                        pe.wait_ge(hT_ok, n + 1)
                        if type(n) is not int or n >= 1:
                            pe.wait_ge(lg_ok, n)
                        for c in range(DC):
                            ins = pe.matmul(p_l[u][:, 0:E1 + 1], hT[:, u, c, :], gate[:, c, :], start=(c == 0), stop=(c == DC - 1))
                        ins.then_inc(l_ok, 1)

                    pe.wait_ge(loaded, 16)

                    def mixed(n, u, n1, u1):
                        turn(n1, u1)
                        route(n, u)
                    skewed(pe, turn, mixed, route)
                    pe.wait_ge(W_ok, 3)
                    for n in range(NT):
                        o = P * n % CH
                        ins = pe.transpose(p_w[P * n // CH][0:WROWS, o:o + P], W[:, n, :], ident[:, :])
                        if o + P == CH:
                            ins.then_inc(w_ok, 1)

                @block.vector
                def _(dve):
                    for n in range(NT):
                        dve.bn_stats(st[:, n, :], x[:, n, :])
                    dve.drain()
                    for n in range(NT):
                        ins = dve.bn_aggr(mv[:, n, :], st[:, n, :])
                    ins.then_inc(stat_ok, 1)
                    dve.wait_ge(stat_ok, 1)
                    dve.tensor_scalar(ve[:, :], mv[:, :, 1], 1e-5, None, ALU.add).then_inc(var_ok, 1)
                    dve.wait_ge(rstd_ok, 1)

                    def norm(n, u):
                        if type(n) is not int or n >= 2:
                            dve.wait_ge(t_ok, n - 1)
                        dve.tensor_scalar(hn[:, u, :], x[:, bass.ds(n, 1), :].rearrange("p a d -> p (a d)"),
                                          mv[:, bass.ds(n, 1), 0:1].rearrange("p a b -> p (a b)"), rstd[:, bass.ds(n, 1)],
                                          ALU.subtract, ALU.mult).then_inc(hn_ok, 1)

                    def low(n, u):
                        dve.wait_ge(hi_ok, n + 1)
                        cols = bass.ds(n * P, P)
                        dve.scalar_tensor_tensor(hs[:, 1, :, cols], p_t[u][:, :, :], H_UP, hs[:, 0, :, cols],
                                                 ALU.mult, ALU.subtract).then_inc(lo_ok, 1)

                    def mixed(n, u, n1, u1):
                        norm(n1, u1)
                        low(n, u)
                    skewed(dve, norm, mixed, low)
                    for n in range(NT):
                        dve.wait_ge(lg_ok, n + 1)
                        dve.max(top[:, n, :], lg[:, n, 0:E1]).then_inc(top_ok, 1)
                    dve.wait_ge(top_ok, NT)
                    dve.tensor_tensor(df[:, :, :], lg[:, :, 0:E1], top[:, :, 0:1].to_broadcast([P, NT, E1]), ALU.subtract).then_inc(top_ok, 1)
                    for n in range(NT):
                        dve.match_replace(rest[:, n, :], top[:, n, :], lg[:, n, 0:E1], -3.0e38).then_inc(step, 1)
                    dve.wait_ge(step, NT)
                    dve.tensor_tensor(rest[:, :, :], rest[:, :, :], lg[:, :, 0:E1], ALU.not_equal).then_inc(step, 1)
                    dve.wait_ge(ex_ok, 1)
                    dve.tensor_scalar(sm[:, 1, :], sg1[:, :, 0], 1.0, None, ALU.add)
                    dve.wait_ge(step, NT + 1)
                    dve.wait_ge(ex_ok, 2)
                    dve.tensor_tensor(ex[:, :, :], ex[:, :, :], rest[:, :, :], ALU.mult).then_inc(step, 1)
                    dve.wait_ge(step, NT + 2)
                    dve.tensor_reduce(sm[:, 0, :], ex[:, :, :], AX.X, ALU.add).then_inc(step, 1)
                    dve.wait_ge(step, NT + 3)
                    dve.reciprocal(rc[:, :, :], sm[:, :, :]).then_inc(step, 1)
                    dve.wait_ge(step, NT + 4)
                    dve.tensor_tensor(W[:, :, 0:E1], ex[:, :, :], bcast(rc[:, 0, :], 2, E1), ALU.mult).then_inc(W_ok, 1)
                    dve.tensor_copy(W[:, :, E1:E1 + 1], bcast(rc[:, 1, :], 2, 1)).then_inc(W_ok, 1)

        yT = m.sb("m1yT", [P, DC, B * S])
        e = Store(nc)
        with e.stack:
            Wb = e.sb("m1Wb", [P, NR, B * S])
            sg = e.sb("m1sg", [P, 2, CH])
            ac = e.sb("m1ac", [P, 2, CH])
            ap = e.sb("m1ap", [P, 2, 2, CH], F16)
            p_g = [e.ps(f"m1pg{i}", [P, CH]) for i in range(2)]
            p_u = [e.ps(f"m1pu{i}", [P, CH]) for i in range(2)]
            p_y = [[e.ps(f"m1py{c}{q}", [P, CH]) for q in range(NCH)] for c in range(DC)]
            (g_ok, u_ok, silu_ok, sw_ok, act_ok, ah_ok, al_ok, y_ok, out_ok) = e.sems(
                "e1", "g_ok u_ok silu_ok sw_ok act_ok ah_ok al_ok y_ok out_ok")
            b_in = [e.sem(f"e1_b_in{u}") for u in range(NR)]

            def part(ap_, u, s, c, which):
                return ap_[:, u, s, P * (2 * c + which):P * (2 * c + which) + P]

            def over_pairs(eng, body):
                body(0, 0, 0)
                with eng.Fori(0, (NPAIR - 6) // NR) as i:
                    body(i * NR + 1, 1, i)
                    body(i * NR + 2, 2, i)
                    body(i * NR + 3, 0, i + 1)
                for p in range(NPAIR - 5, NPAIR):
                    body(p, p % NR, p // NR)

            def is_pair(p):
                return type(p) is not int or 0 <= p < NPAIR

            with nc.Block() as block:
                @block.sync
                def _(sp):
                    def load_b(p, u):
                        for h in range(2):
                            sp.dma_start(Wb[64 * h:64 * h + 64, u, :],
                                         wt_dram[bass.ds(p * 2 + h, 1), :].to_broadcast([64, B * S])).then_inc(b_in[u], 16)
                    for p in range(NR):
                        load_b(p, p)

                    def pair(p, u, r):
                        if is_pair(p + NR):
                            sp.wait_ge(prep_ok, p + 1)
                            load_raw(sp, p + NR, u)
                            sp.wait_ge(sw_ok, p * 2 + 2)
                            load_b(p + NR, u)
                    over_pairs(sp, pair)

                @block.gpsimd
                def _(pool):
                    def pair(p, u, r):
                        if is_pair(p + 2) and not (type(p) is int and p == 0):
                            low_part(pool, p + 2, (u + 2) % NR)
                    over_pairs(pool, pair)

                @block.scalar
                def _(act):
                    def silu(j, q):
                        act.wait_ge(g_ok, j + 1)
                        act.activation(sg[:, q, :], p_g[q][:, :], ACT.Silu, scale=1.0 / (H_UP * W_UP)).then_inc(silu_ok, 1)

                    def ahigh(j, q):
                        act.wait_ge(act_ok, j + 1)
                        act.activation(ap[:, q, 0, :], ac[:, q, :], ACT.Copy).then_inc(ah_ok, 1)

                    silu(0, 0)

                    def pair(p, u, r):
                        prep = is_pair(p + 2) and not (type(p) is int and p == 0)
                        u2 = (u + 2) % NR
                        ahigh(p * 2, 0)
                        if prep:
                            act.wait_ge(w_in[u2], (r + (u > 0)) * 16 + 16)
                            act.wait_ge(y_ok, p * 2)
                            act.activation(ws[:, u2, 0, :], raw[:, u2, :], ACT.Copy, scale=W_UP)
                        silu(p * 2 + 1, 1)
                        ahigh(p * 2 + 1, 1)
                        if prep:
                            scaled_raw(act, u2)
                        if is_pair(p + 1):
                            silu(p * 2 + 2, 0)
                    over_pairs(act, pair)
                    for c in range(DC):
                        for q in range(NCH):
                            act.wait_ge(y_ok, 2 * NPAIR)
                            ins = act.activation(yT[:, c, CH * q:CH * q + CH], p_y[c][q][:, :], ACT.Copy, scale=1.0 / W_UP)
                    ins.then_inc(out_ok, 1)
                    act.wait_ge(out_ok, 1)

                @block.tensor
                def _(pe):
                    def hidden(p, u, q):
                        j = p * 2 + q
                        pe.wait_ge(prep_ok, p + 1)
                        if not (type(p) is int and p == 0):
                            pe.wait_ge(act_ok, j - 1)
                        for which, bank, ok in ((0, p_g[q], g_ok), (1, p_u[q], u_ok)):
                            k = 0
                            for c in range(DC):
                                for sw, sh in PASSES:
                                    ins = pe.matmul(bank[:, :], part(ws, u, sw, c, which), hs[:, sh, c, CH * q:CH * q + CH],
                                                    start=(k == 0), stop=(k == 5))
                                    k += 1
                            ins.then_inc(ok, 1)

                    def down(p, u, q):
                        j = p * 2 + q
                        first, last = (type(p) is int and p == k for k in (0, NPAIR - 1))
                        pe.wait_ge(al_ok, j + 1)
                        for c in range(DC):
                            for k, (sw, sa) in enumerate(PASSES):
                                ins = pe.matmul(p_y[c][q][:, :], ws[:, u, sw, GU + P * c:GU + P * c + P], ap[:, q, sa, :],
                                                start=(first and k == 0), stop=(last and k == 2), skip_group_check=True)
                        ins.then_inc(y_ok, 1)

                    hidden(0, 0, 0)

                    def pair(p, u, r):
                        hidden(p, u, 1)
                        down(p, u, 0)
                        if is_pair(p + 1):
                            hidden(p + 1, (u + 1) % NR, 0)
                        down(p, u, 1)
                    over_pairs(pe, pair)

                @block.vector
                def _(dve):
                    def weigh(p, u, r, q):
                        dve.wait_ge(b_in[u], r * 32 + 32)
                        dve.wait_ge(silu_ok, p * 2 + q + 1)
                        dve.tensor_tensor(sg[:, q, :], sg[:, q, :], Wb[:, u, CH * q:CH * q + CH], ALU.mult).then_inc(sw_ok, 1)

                    def times_up(p, q):
                        j = p * 2 + q
                        dve.wait_ge(sw_ok, j + 1)
                        dve.wait_ge(u_ok, j + 1)
                        dve.scalar_tensor_tensor(ac[:, q, :], p_u[q][:, :], 1.0 / (H_UP * W_UP), sg[:, q, :],
                                                 ALU.mult, ALU.mult).then_inc(act_ok, 1)

                    def alow(p, q):
                        j = p * 2 + q
                        dve.wait_ge(ah_ok, j + 1)
                        dve.tensor_tensor(ap[:, q, 1, :], ac[:, q, :], ap[:, q, 0, :], ALU.subtract).then_inc(al_ok, 1)

                    weigh(0, 0, 0, 0)
                    times_up(0, 0)

                    def pair(p, u, r):
                        alow(p, 0)
                        weigh(p, u, r, 1)
                        times_up(p, 1)
                        alow(p, 1)
                        if is_pair(p + 1):
                            weigh(p + 1, (u + 1) % NR, r + (u == NR - 1), 0)
                            times_up(p + 1, 0)
                    over_pairs(dve, pair)
        add_transposed(nc, C, yT, "m1")


def add_transposed(nc, C, yT, tag):
    m = Store(nc)
    with m.stack:
        p_t = [m.ps(f"{tag}pz{i}", [P, D]) for i in range(4)]
        t_ok, x_ok = m.sems(f"{tag}z", "t_ok x_ok")
        with nc.Block() as block:
            @block.tensor
            def _(pe):
                for n in range(NT):
                    if n >= 4:
                        pe.wait_ge(x_ok, n - 3)
                    for c in range(DC):
                        ins = pe.transpose(p_t[n % 4][:, P * c:P * c + P], yT[:, c, P * n:P * n + P], C["ident"][:, :])
                    ins.then_inc(t_ok, 1)

            @block.vector
            def _(dve):
                for n in range(NT):
                    dve.wait_ge(t_ok, n + 1)
                    ins = dve.tensor_tensor(C["x"][:, n, :], C["x"][:, n, :], p_t[n % 4][:, :], ALU.add)
                    ins.then_inc(x_ok, 1)
                dve.wait_ge(x_ok, NT)


E0, K0, I0 = 32, 4, 128
CAP = 2 * B * S * K0 // E0
SLOTS = E0 * CAP
ST = CAP // P
DROPPED = 2.0 ** 20


def moe_slots(nc, C, a):
    x, ident, neghalf = C["x"], C["ident"], C["neghalf"]
    slots_in, slots_out = C["slots_in"], C["slots_out"]
    m = Store(nc)
    with m.stack:
        hs = m.sb("m0hs", [P, 2, DC, B * S], F16)
        h2 = m.sb("m0h2", [P, NT, D])
        w4 = m.sb("m0w4", [P, NT, K0])
        slot = m.sb("m0slot", [P, NT, 2, K0], U32)
        scattered = m.sem("m0_scattered")
        r = Store(nc)
        with r.stack:
            gate = r.sb("m0gate", [P, DC, E0])
            normw = r.sb("m0normw", [P, D])
            eids = r.sb("m0eids", [P, E0])
            before = r.sb("m0before", [P, P])
            ones = r.sb("m0ones", [P, P])
            st = r.sb("m0st", [P, 2, 6])
            mv = r.sb("m0mv", [P, 2, 4])
            ms = r.sb("m0ms", [P, 2, 3])
            hn = r.sb("m0hn", [P, 2, D])
            junk = r.sb("m0junk", [P, D])
            hT = r.sb("m0hT", [P, 2, DC, P])
            lg = r.sb("m0lg", [P, E0])
            top = r.sb("m0top", [P, 8])
            idx = r.sb("m0idx", [P, 8], U32)
            idf = r.sb("m0idf", [P, K0])
            nb = r.sb("m0nb", [P, 1])
            ex = r.sb("m0ex", [P, K0])
            sm = r.sb("m0sm", [P, 2])
            OH = r.sb("m0OH", [P, K0, E0])
            M = r.sb("m0M", [P, 2, E0])
            Mp = r.sb("m0Mp", [P, E0])
            sv = r.sb("m0sv", [P, 2, E0])
            pk = r.sb("m0pk", [P, 2, K0, E0])
            sf = r.sb("m0sf", [P, 2, K0])
            p_t = [r.ps(f"m0pt{i}", [P, DC, P]) for i in range(2)]
            p_l = [r.ps(f"m0pl{i}", [P, 512]) for i in range(2)]
            p_p = [r.ps(f"m0pp{i}", [P, 512]) for i in range(2)]
            (loaded, const_ok, var_ok, rstd_ok, hn_ok, sq_ok, ms_ok, rr_ok, h2_ok, t_ok, hT_ok, hi_ok, lo_ok,
             l_ok, nb_ok, ex_ok, step, M_ok, pos_ok, slot_ok, stat_ok) = r.sems(
                "m0", "loaded const_ok var_ok rstd_ok hn_ok sq_ok ms_ok rr_ok h2_ok t_ok hT_ok hi_ok lo_ok"
                      " l_ok nb_ok ex_ok step M_ok pos_ok slot_ok stat_ok")
            with nc.Block() as block:
                @block.sync
                def _(sp):
                    moved(sp, loaded, [(gate[:, :, :], a["m0_gate"]), (normw[:, :], a["m0_normw"].to_broadcast([P, D])),
                                       (eids[:, :], a["eids"].to_broadcast([P, E0])), (before[:, :], a["before"])])

                @block.gpsimd
                def _(pool):
                    def roots(n):
                        u = n % 2
                        pool.wait_ge(var_ok, n + 1)
                        pool.tensor_tensor(mv[:, u, 3:4], mv[:, u, 2:3], neghalf[:, 0:1], ALU.pow).then_inc(rstd_ok, 1)
                        pool.wait_ge(ms_ok, n + 1)
                        pool.tensor_tensor(ms[:, u, 2:3], ms[:, u, 1:2], neghalf[:, 0:1], ALU.pow).then_inc(rr_ok, 1)

                    def scatter(n):
                        pool.wait_ge(slot_ok, n + 1)
                        for k in range(K0):
                            pool.indirect_dma_start(slots_in, bass.IndirectOffsetOnAxis(ap=slot[:, n, 1, k:k + 1], axis=0),
                                                    h2[:, n, :], None, bounds_check=SLOTS - 1, oob_is_err=False).then_inc(scattered, 16)

                    pool.memset(ones[:, :], 1.0).then_inc(const_ok, 1)
                    roots(0)
                    roots(1)
                    pool.wait_ge(C["zero_ok"], 16)
                    for n in range(NT):
                        if n + 2 < NT:
                            roots(n + 2)
                        scatter(n)

                @block.scalar
                def _(act):
                    def squares(n, u):
                        act.wait_ge(hn_ok, n + 1)
                        act.activation(junk[:, :], hn[:, u, :], ACT.Square, accum_out=ms[:, u, 0:1]).then_inc(sq_ok, 1)

                    def inputs(n, u):
                        act.wait_ge(t_ok, n + 1)
                        act.activation(hT[:, u, :, :], p_t[u][:, :, :], ACT.Copy).then_inc(hT_ok, 1)
                        act.activation(hs[:, 0, :, bass.ds(n * P, P)], p_t[u][:, :, :], ACT.Copy, scale=H_UP).then_inc(hi_ok, 1)

                    def weights(n, u):
                        act.wait_ge(nb_ok, n + 1)
                        act.activation(ex[:, :], top[:, 0:K0], ACT.Exp, bias=nb[:, 0:1], accum_out=sm[:, 0:1]).then_inc(ex_ok, 1)

                    squares(0, 0)
                    squares(1, 1)

                    def tile(n, u):
                        inputs(n, u)
                        if type(n) is not int:
                            squares(n + 2, u)
                        weights(n, u)
                    looped(act, tile, NT - 2)
                    tile(NT - 2, 0)
                    tile(NT - 1, 1)

                @block.tensor
                def _(pe):
                    def turn(n, u):
                        pe.wait_ge(h2_ok, n + 1)
                        for c in range(DC):
                            ins = pe.transpose(p_t[u][:, c, :], h2[:, n, P * c:P * c + P], ident[:, :])
                        ins.then_inc(t_ok, 1)

                    def route(n, u):
                        pe.wait_ge(hT_ok, n + 1)
                        for c in range(DC):
                            ins = pe.matmul(p_l[u][:, 0:E0], hT[:, u, c, :], gate[:, c, :], start=(c == 0), stop=(c == DC - 1))
                        ins.then_inc(l_ok, 1)

                    def places(n, u):
                        pe.wait_ge(M_ok, n + 1)
                        pe.matmul(p_p[u][:, 0:E0], before[:, :], M[:, u, :], start=True, stop=False)
                        pe.matmul(p_p[u][:, 0:E0], ones[:, :], Mp[:, :], start=False, stop=True).then_inc(pos_ok, 1)

                    pe.wait_ge(loaded, 64)
                    pe.wait_ge(const_ok, 1)
                    for n in range(NT):
                        u = n % 2
                        if n == 0:
                            turn(0, 0)
                        if n + 1 < NT:
                            if n >= 1:
                                pe.wait_ge(lo_ok, n)
                            turn(n + 1, 1 - u)
                        route(n, u)
                        places(n, u)

                @block.vector
                def _(dve):
                    def tile_of(n):
                        return x[:, bass.ds(n, 1), :].rearrange("p a d -> p (a d)")

                    def norm(n, u):
                        dve.bn_stats(st[:, u, :], tile_of(n))
                        dve.drain()
                        dve.bn_aggr(mv[:, u, 0:2], st[:, u, :]).then_inc(stat_ok, 1)
                        dve.wait_ge(stat_ok, n + 1)
                        dve.tensor_scalar(mv[:, u, 2:3], mv[:, u, 1:2], 1e-5, None, ALU.add).then_inc(var_ok, 1)
                        dve.wait_ge(rstd_ok, n + 1)
                        dve.tensor_scalar(hn[:, u, :], tile_of(n), mv[:, u, 0:1], mv[:, u, 3:4], ALU.subtract, ALU.mult).then_inc(hn_ok, 1)
                        dve.wait_ge(sq_ok, n + 1)
                        dve.tensor_scalar(ms[:, u, 1:2], ms[:, u, 0:1], 1.0 / D, 1e-6, ALU.mult, ALU.add).then_inc(ms_ok, 1)
                        dve.tensor_tensor(tile_of(n), tile_of(n), hn[:, u, :], ALU.add)
                        dve.wait_ge(rr_ok, n + 1)
                        dve.scalar_tensor_tensor(h2[:, bass.ds(n, 1), :].rearrange("p a d -> p (a d)"), hn[:, u, :],
                                                 ms[:, u, 2:3], normw[:, :], ALU.mult, ALU.mult).then_inc(h2_ok, 1)

                    def low(n, u):
                        dve.wait_ge(hi_ok, n + 1)
                        cols = bass.ds(n * P, P)
                        dve.scalar_tensor_tensor(hs[:, 1, :, cols], p_t[u][:, :, :], H_UP, hs[:, 0, :, cols],
                                                 ALU.mult, ALU.subtract).then_inc(lo_ok, 1)

                    def choose(n, u):
                        def then(ins, k):
                            ins.then_inc(step, 1)
                            dve.wait_ge(step, n * 7 + k)
                        dve.wait_ge(l_ok, n + 1)
                        dve.tensor_copy(lg[:, :], p_l[u][:, 0:E0])
                        dve.drain()
                        dve.max(top[:, :], lg[:, :])
                        dve.drain()
                        dve.tensor_scalar(nb[:, :], top[:, 0:1], -1.0, None, ALU.mult).then_inc(nb_ok, 1)
                        dve.max_index(idx[:, :], top[:, :], lg[:, :])
                        dve.drain()
                        then(dve.tensor_copy(idf[:, :], idx[:, 0:K0]), 1)
                        then(dve.tensor_tensor(OH[:, :, :], bcast(eids[:, :], 1, K0), bcast(idf[:, :], 2, E0), ALU.is_equal), 2)
                        dve.tensor_reduce(M[:, u, :], OH[:, :, :].rearrange("p k e -> p e k"), AX.X, ALU.add).then_inc(M_ok, 1)
                        dve.wait_ge(ex_ok, n + 1)
                        then(dve.reciprocal(sm[:, 1:2], sm[:, 0:1]), 3)
                        dve.tensor_scalar(w4[:, bass.ds(n, 1), :].rearrange("p a k -> p (a k)"), ex[:, :], sm[:, 1:2], None, ALU.mult)
                        dve.wait_ge(pos_ok, n + 1)
                        dve.tensor_tensor(Mp[:, :], Mp[:, :], M[:, u, :], ALU.add)
                        dve.tensor_scalar(sv[:, 0, :], p_p[u][:, 0:E0], CAP - 1.0, None, ALU.min)
                        then(dve.tensor_scalar(sv[:, 1, :], p_p[u][:, 0:E0], float(CAP), DROPPED, ALU.is_ge, ALU.mult), 4)
                        then(dve.scalar_tensor_tensor(sv[:, 0, :], eids[:, :], float(CAP), sv[:, 0, :], ALU.mult, ALU.add), 5)
                        then(dve.tensor_tensor(sv[:, 1, :], sv[:, 1, :], sv[:, 0, :], ALU.add), 6)
                        for j in range(2):
                            ins = dve.tensor_tensor(pk[:, j, :, :], OH[:, :, :], bcast(sv[:, j, :], 1, K0), ALU.mult)
                        then(ins, 7)
                        dve.tensor_reduce(sf[:, :, :], pk[:, :, :, :], AX.X, ALU.add)
                        dve.drain()
                        dve.tensor_copy(slot[:, bass.ds(n, 1), :, :].rearrange("p a j k -> p (a j) k"), sf[:, :, :]).then_inc(slot_ok, 1)

                    dve.wait_ge(loaded, 64)
                    dve.memset(Mp[:, :], 0.0)
                    norm(0, 0)
                    norm(1, 1)

                    def tile(n, u):
                        low(n, u)
                        if type(n) is not int:
                            norm(n + 2, u)
                        choose(n, u)
                    looped(dve, tile, NT - 2)
                    tile(NT - 2, 0)
                    tile(NT - 1, 1)

        e = Store(nc)
        with e.stack:
            GU = DC * 2 * P
            xg = e.sb("m0xg", [P, 2, ST, D])
            xs = e.sb("m0xs", [P, 2, 2, DC, CAP], F16)
            rg = e.sb("m0rg", [P, 2, GU])
            rd = e.sb("m0rd", [P, 2, D])
            wg = e.sb("m0wg", [P, 2, 2, GU], F16)
            wd = e.sb("m0wd", [P, 2, 2, D], F16)
            sg = e.sb("m0sg", [P, 2, CAP])
            ac = e.sb("m0ac", [P, 2, CAP])
            ap = e.sb("m0ap", [P, 2, 2, CAP], F16)
            yo = e.sb("m0yo", [P, 2, ST, D])
            rs_ = e.sb("m0rs", [P, GU + D])
            ws = e.sb("m0ws", [P, 2, GU + D], F16)
            ssg = e.sb("m0ssg", [P, 2, CH])
            sac = e.sb("m0sac", [P, 2, CH])
            sap = e.sb("m0sap", [P, 2, 2, CH], F16)
            p_x = [e.ps(f"m0px{i}", [P, DC, CAP]) for i in range(2)]
            p_h = [e.ps(f"m0ph{i}", [P, 2, CAP]) for i in range(2)]
            p_y = [e.ps(f"m0py{i}", [P, ST, D]) for i in range(2)]
            p_s = [e.ps(f"m0ps{i}", [P, CH]) for i in range(2)]
            xin = [e.sem(f"e0_xin{u}") for u in range(2)]
            gin = [e.sem(f"e0_gin{u}") for u in range(2)]
            din = [e.sem(f"e0_din{u}") for u in range(2)]
            stored = [e.sem(f"e0_stored{u}") for u in range(2)]
            (sin, sh_ok, sl_ok, sg_ok, su_ok, ssilu_ok, sact_ok, sah_ok, sal_ok, sy_ok, sx_ok,
             xt_ok, xh_ok, xl_ok, gh_ok, gl_ok, dh_ok, dl_ok, gu_ok, silu_ok, act_ok, ah_ok, al_ok, y_ok, yo_ok) = e.sems(
                "e0", "sin sh_ok sl_ok sg_ok su_ok ssilu_ok sact_ok sah_ok sal_ok sy_ok sx_ok"
                      " xt_ok xh_ok xl_ok gh_ok gl_ok dh_ok dl_ok gu_ok silu_ok act_ok ah_ok al_ok y_ok yo_ok")

            def periods(eng, body):
                for k in range(3):
                    body(k, k % 2)
                with eng.Fori(0, (E0 - 6) // 2) as i:
                    body(i * 2 + 3, 1)
                    body(i * 2 + 4, 0)
                for k in range(E0 - 3, E0):
                    body(k, k % 2)

            def has(k):
                return type(k) is not int or 0 <= k < E0

            with nc.Block() as block:
                @block.sync
                def _(sp):
                    def load_x(k, u):
                        if type(k) is not int or k >= 2:
                            sp.wait_ge(xt_ok, k - 1)
                        sp.dma_start(xg[:, u, :, :], slots_in[bass.ds(k * CAP, CAP), :].rearrange("(s p) d -> p s d", p=P)).then_inc(xin[u], 16)

                    def load_g(k, u):
                        if type(k) is not int or k >= 2:
                            sp.wait_ge(gl_ok, k - 1)
                        sp.dma_start(rg[:, u, :], a["m0_wgu"][bass.ds(k, 1), :, :].rearrange("a p n -> p (a n)")).then_inc(gin[u], 16)

                    def load_d(k, u):
                        if type(k) is not int or k >= 2:
                            sp.wait_ge(dl_ok, k - 1)
                        sp.dma_start(rd[:, u, :], a["m0_wd"][bass.ds(k, 1), :, :].rearrange("a p n -> p (a n)")).then_inc(din[u], 16)

                    def store(k, u):
                        sp.wait_ge(yo_ok, k + 1)
                        sp.dma_start(slots_out[bass.ds(k * CAP, CAP), :].rearrange("(s p) d -> p s d", p=P), yo[:, u, :, :]).then_inc(stored[u], 16)

                    sp.dma_start(rs_[:, :], a["m0_ws"]).then_inc(sin, 16)
                    load_g(0, 0)
                    load_g(1, 1)
                    load_d(0, 0)
                    load_d(1, 1)
                    sp.wait_ge(scattered, 16 * NT * K0)
                    load_x(0, 0)
                    load_x(1, 1)
                    load_x(2, 0)
                    load_g(2, 0)
                    load_x(3, 1)
                    load_g(3, 1)
                    load_d(2, 0)

                    def period(k, u):
                        if type(k) is not int or k >= 1:
                            if has(k + 3):
                                load_x(k + 3, 1 - u)
                                load_g(k + 3, 1 - u)
                            if has(k + 2):
                                load_d(k + 2, u)
                            store(k - 1, 1 - u)
                    periods(sp, period)
                    store(E0 - 1, 1)
                    for u in range(2):
                        sp.wait_ge(stored[u], 16 * E0 // 2)

                @block.gpsimd
                def _(pool):
                    pool.wait_ge(sh_ok, 1)
                    pool.tensor_tensor(ws[:, 1, :], rs_[:, :], ws[:, 0, :], ALU.subtract).then_inc(sl_ok, 1)

                    def low_g(k, u):
                        pool.wait_ge(gh_ok, k + 1)
                        pool.tensor_tensor(wg[:, u, 1, :], rg[:, u, :], wg[:, u, 0, :], ALU.subtract).then_inc(gl_ok, 1)

                    def low_d(k, u):
                        pool.wait_ge(dh_ok, k + 1)
                        pool.tensor_tensor(wd[:, u, 1, :], rd[:, u, :], wd[:, u, 0, :], ALU.subtract).then_inc(dl_ok, 1)
                    low_g(0, 0)
                    low_g(1, 1)
                    low_d(0, 0)

                    def period(k, u):
                        if has(k + 2):
                            low_g(k + 2, u)
                        if has(k + 1):
                            low_d(k + 1, 1 - u)
                    periods(pool, period)

                @block.scalar
                def _(act):
                    act.wait_ge(sin, 16)
                    act.activation(ws[:, 0, :], rs_[:, :], ACT.Copy, scale=W_UP)
                    act.activation(rs_[:, :], rs_[:, :], ACT.Copy, scale=W_UP).then_inc(sh_ok, 1)
                    for q in range(NCH):
                        act.wait_ge(su_ok, q + 1)
                        act.activation(ssg[:, q, :], p_s[0][:, :], ACT.Silu, scale=1.0 / (H_UP * W_UP)).then_inc(ssilu_ok, 1)
                        act.wait_ge(sact_ok, q + 1)
                        act.activation(sap[:, q, 0, :], sac[:, q, :], ACT.Copy).then_inc(sah_ok, 1)

                    def x_high(k, u):
                        act.wait_ge(xt_ok, k + 1)
                        act.activation(xs[:, u, 0, :, :], p_x[u][:, :, :], ACT.Copy, scale=H_UP).then_inc(xh_ok, 1)

                    def silu(k, u):
                        act.wait_ge(gu_ok, k + 1)
                        act.activation(sg[:, u, :], p_h[u][:, 0, :], ACT.Silu, scale=1.0 / (H_UP * W_UP)).then_inc(silu_ok, 1)

                    def a_high(k, u):
                        act.wait_ge(act_ok, k + 1)
                        act.activation(ap[:, u, 0, :], ac[:, u, :], ACT.Copy).then_inc(ah_ok, 1)

                    def y_out(k, u):
                        act.wait_ge(y_ok, k + 1)
                        if type(k) is not int or k >= 2:
                            act.wait_ge(stored[u], (k - u) * 8)
                        act.activation(yo[:, u, :, :], p_y[u][:, :, :], ACT.Copy, scale=1.0 / W_UP).then_inc(yo_ok, 1)

                    x_high(0, 0)
                    x_high(1, 1)

                    def period(k, u):
                        silu(k, u)
                        if has(k + 2):
                            x_high(k + 2, u)
                        a_high(k, u)
                        if has(k - 1):
                            y_out(k - 1, 1 - u)
                    periods(act, period)
                    y_out(E0 - 1, 1)

                @block.tensor
                def _(pe):
                    pe.wait_ge(sl_ok, 1)
                    for q in range(NCH):
                        if q >= 1:
                            pe.wait_ge(sact_ok, q)
                        for which in range(2):
                            k = 0
                            for c in range(DC):
                                for sw, sh in PASSES:
                                    ins = pe.matmul(p_s[which][:, :], ws[:, sw, P * (2 * c + which):P * (2 * c + which) + P],
                                                    hs[:, sh, c, CH * q:CH * q + CH], start=(k == 0), stop=(k == 5))
                                    k += 1
                        ins.then_inc(su_ok, 1)
                    for n in range(NT):
                        q, o = n * P // CH, n * P % CH
                        pe.wait_ge(sal_ok, q + 1)
                        if n >= 2:
                            pe.wait_ge(sx_ok, n - 1)
                        for k, (sw, sa) in enumerate(PASSES):
                            ins = pe.matmul(p_y[n % 2][:, 0, :], sap[:, q, sa, o:o + P], ws[:, sw, GU:GU + D],
                                            start=(k == 0), stop=(k == 2))
                        ins.then_inc(sy_ok, 1)

                    def turn(k, u):
                        pe.wait_ge(xin[u], (k - u) * 8 + 16)
                        if type(k) is not int or k >= 2:
                            pe.wait_ge(xl_ok, k - 1)
                        for c in range(DC):
                            for s in range(ST):
                                ins = pe.transpose(p_x[u][:, c, P * s:P * s + P], xg[:, u, s, P * c:P * c + P], ident[:, :])
                        ins.then_inc(xt_ok, 1)

                    def hidden(k, u):
                        pe.wait_ge(xl_ok, k + 1)
                        pe.wait_ge(gl_ok, k + 1)
                        if type(k) is not int or k >= 2:
                            pe.wait_ge(act_ok, k - 1)
                        for which in range(2):
                            i = 0
                            for c in range(DC):
                                for sw, sx in PASSES:
                                    ins = pe.matmul(p_h[u][:, which, :], wg[:, u, sw, P * (2 * c + which):P * (2 * c + which) + P],
                                                    xs[:, u, sx, c, :], start=(i == 0), stop=(i == 5))
                                    i += 1
                        ins.then_inc(gu_ok, 1)

                    def down(k, u):
                        pe.wait_ge(al_ok, k + 1)
                        pe.wait_ge(dl_ok, k + 1)
                        if type(k) is not int or k >= 2:
                            pe.wait_ge(yo_ok, k - 1)
                        elif k < 2:
                            pe.wait_ge(sx_ok, NT)
                        for s in range(ST):
                            for i, (sw, sa) in enumerate(PASSES):
                                ins = pe.matmul(p_y[u][:, s, :], ap[:, u, sa, P * s:P * s + P], wd[:, u, sw, :],
                                                start=(i == 0), stop=(i == 2))
                        ins.then_inc(y_ok, 1)

                    turn(0, 0)
                    turn(1, 1)

                    def period(k, u):
                        hidden(k, u)
                        if has(k + 2):
                            turn(k + 2, u)
                        if has(k - 1):
                            down(k - 1, 1 - u)
                    periods(pe, period)
                    down(E0 - 1, 1)

                @block.vector
                def _(dve):
                    def high_g(k, u):
                        dve.wait_ge(gin[u], (k - u) * 8 + 16)
                        if type(k) is not int or k >= 2:
                            dve.wait_ge(gu_ok, k - 1)
                        dve.tensor_scalar(wg[:, u, 0, :], rg[:, u, :], W_UP, None, ALU.mult)
                        dve.tensor_scalar(rg[:, u, :], rg[:, u, :], W_UP, None, ALU.mult).then_inc(gh_ok, 1)

                    def high_d(k, u):
                        dve.wait_ge(din[u], (k - u) * 8 + 16)
                        if type(k) is not int or k >= 2:
                            dve.wait_ge(y_ok, k - 1)
                        dve.tensor_scalar(wd[:, u, 0, :], rd[:, u, :], W_UP, None, ALU.mult)
                        dve.tensor_scalar(rd[:, u, :], rd[:, u, :], W_UP, None, ALU.mult).then_inc(dh_ok, 1)

                    def x_low(k, u):
                        dve.wait_ge(xh_ok, k + 1)
                        dve.scalar_tensor_tensor(xs[:, u, 1, :, :], p_x[u][:, :, :], H_UP, xs[:, u, 0, :, :],
                                                 ALU.mult, ALU.subtract).then_inc(xl_ok, 1)

                    def times_up(k, u):
                        dve.wait_ge(silu_ok, k + 1)
                        dve.scalar_tensor_tensor(ac[:, u, :], p_h[u][:, 1, :], 1.0 / (H_UP * W_UP), sg[:, u, :],
                                                 ALU.mult, ALU.mult).then_inc(act_ok, 1)

                    def a_low(k, u):
                        dve.wait_ge(ah_ok, k + 1)
                        dve.tensor_tensor(ap[:, u, 1, :], ac[:, u, :], ap[:, u, 0, :], ALU.subtract).then_inc(al_ok, 1)

                    high_g(0, 0)
                    high_g(1, 1)
                    high_d(0, 0)
                    for q in range(NCH):
                        dve.wait_ge(ssilu_ok, q + 1)
                        dve.scalar_tensor_tensor(sac[:, q, :], p_s[1][:, :], 1.0 / (H_UP * W_UP), ssg[:, q, :],
                                                 ALU.mult, ALU.mult).then_inc(sact_ok, 1)
                        dve.wait_ge(sah_ok, q + 1)
                        dve.tensor_tensor(sap[:, q, 1, :], sac[:, q, :], sap[:, q, 0, :], ALU.subtract).then_inc(sal_ok, 1)
                    for n in range(NT):
                        dve.wait_ge(sy_ok, n + 1)
                        dve.scalar_tensor_tensor(x[:, n, :], p_y[n % 2][:, 0, :], 1.0 / W_UP, x[:, n, :],
                                                 ALU.mult, ALU.add).then_inc(sx_ok, 1)
                    x_low(0, 0)
                    x_low(1, 1)

                    def period(k, u):
                        times_up(k, u)
                        if has(k + 2):
                            high_g(k + 2, u)
                            x_low(k + 2, u)
                        a_low(k, u)
                        if has(k + 1):
                            high_d(k + 1, 1 - u)
                    periods(dve, period)
                    dve.wait_ge(sx_ok, NT)

        c = Store(nc)
        with c.stack:
            rows = c.sb("m0rows", [P, NT, K0, D])
            fetched = [c.sem(f"m0_fetched{n}") for n in range(NT)]
            added = c.sem("m0_added")
            with nc.Block() as block:
                @block.gpsimd
                def _(pool):
                    for n in range(NT):
                        for k in range(K0):
                            pool.indirect_dma_start(rows[:, n, k, :], None, slots_out,
                                                    bass.IndirectOffsetOnAxis(ap=slot[:, n, 0, k:k + 1], axis=0),
                                                    bounds_check=SLOTS - 1, oob_is_err=False).then_inc(fetched[n], 16)

                @block.vector
                def _(dve):
                    for n in range(NT):
                        dve.wait_ge(fetched[n], 16 * K0)
                        for k in range(K0):
                            dve.scalar_tensor_tensor(x[:, n, :], rows[:, n, k, :], w4[:, n, k:k + 1], x[:, n, :],
                                                     ALU.mult, ALU.add).then_inc(added, 1)
                            dve.wait_ge(added, n * K0 + k + 1)


def decoder(nc, a, out):
    g = Store(nc, last=True)
    with g.stack:
        C = {"x": g.sb("x", [P, NT, D]), "ident": g.sb("ident", [P, P]), "hmask": g.sb("hmask", [P, HG]),
             "neghalf": g.sb("neghalf", [P, 1]), "ctxT": g.sb("ctxT", [P, DC, B * S]), "hi": g.sb("hi", [P, B]),
             "cmask": g.sb("cmask", [P, S]), "rs": g.sb("rs", [P, 1])}
        mi = g.sb("mi", [P, B], I32)
        C["slots_in"] = nc.dram_tensor("slots_in", [SLOTS, D], F32, kind="Internal").ap()
        C["slots_out"] = nc.dram_tensor("slots_out", [SLOTS, D], F32, kind="Internal").ap()
        C["zero_ok"] = zero_ok = g.sem("zero_ok")
        zeros = g.sb("zeros", [P, 2048])
        zeroed = g.sem("zeroed")
        in_sem, mask_ok, out_sem = g.sem("in_sem"), g.sem("mask_ok"), g.sem("out_sem")
        def weights(tag, names, rows):
            w = {k: g.sb(f"{tag}_{k}", [P, DC, D]) for k in ("wq", "wk", "wv", "wo")}
            w.update({k: g.sb(f"{tag}_{k}", [P, DC]) for k in names})
            w.update({k: g.sb(f"{tag}_{k}", [P, D]) for k in rows})
            pairs = [(t[:, :, :] if len(t.shape) == 3 else t[:, :],
                      a[f"{tag}_{k}"].to_broadcast([P, D]) if k in rows else a[f"{tag}_{k}"]) for k, t in w.items()]
            w["loaded"], w["count"] = g.sem(f"{tag}_loaded"), 16 * len(pairs)
            return w, pairs

        w_a0, load_a0 = weights("a0", ("bq", "bk"), ("bv", "bo"))
        w_c0, load_c0 = weights("c0", ("bq", "bk"), ("bv", "bo", "gamma", "beta"))
        w_a1, load_a1 = weights("a1", (), ())
        w_x = {"wq": g.sb("xwq", [P, DC, XH * XD]), "wk": g.sb("xwk", [P, DC, KVH * XD]),
               "wv": g.sb("xwv", [P, DC, KVH * XD]), "wo": g.sb("xwo", [P, XH, D])}
        w_x["loaded"] = g.sem("x_loaded")
        with nc.Block() as block:
            @block.sync
            def _(sp):
                n = moved(sp, in_sem, [
                    (C["x"][:, :, :], a["x"]), (C["ident"][:, :], a["ident"]), (C["hmask"][:, :], a["hmask"]),
                    (C["cmask"][:, :], a["cmask"]), (mi[:, :], a["mask"]), (C["rs"][:, :], a["rs"].to_broadcast([P, 1]))])
                moved(sp, w_a0["loaded"], load_a0)
                sp.wait_ge(in_sem, n)

            @block.vector
            def _(dve):
                dve.memset(zeros[:, :], 0.0).then_inc(zeroed, 1)
                dve.memset(C["neghalf"][:, :], -0.5)
                dve.wait_ge(in_sem, 16 * 6)
                dve.tensor_scalar(C["hi"][:, :], mi[:, :], 0.5, 100.0 / QSCALE, ALU.is_gt, ALU.mult).then_inc(mask_ok, 1)
                dve.wait_ge(mask_ok, 1)
                dve.tensor_scalar(C["hi"][:, :], C["hi"][:, :], -50.0 / QSCALE, None, ALU.add).then_inc(mask_ok, 1)
                dve.tensor_scalar(C["rs"][:, :], C["rs"][:, :], 0.0, 0.3, ALU.max, ALU.min).then_inc(mask_ok, 1)
                dve.wait_ge(mask_ok, 3)

        def ahead(sp):
            sp.dma_start(C["ctxT"][:, :, :], a["ctxT"]).then_inc(w_c0["loaded"], 16)
            moved(sp, w_c0["loaded"], load_c0)
            w_c0["count"] += 16
            sp.dma_start(C["slots_in"].rearrange("(p a s) d -> p a (s d)", p=P, a=8), bcast(zeros[:, :], 1, 8)).then_inc(zero_ok, 16)
            moved(sp, w_a1["loaded"], load_a1)
            moved(sp, w_x["loaded"], [(w_x["wq"][:, :, :], a["x_wq"]), (w_x["wk"][:, :, :], a["x_wk"]),
                                      (w_x["wv"][:, :, :], a["x_wv"]), (w_x["wo"][:, :, :], a["x_wo"])])

        if ONLY in (0, 1):
            attention16(nc, C, "a0", "self", w_a0, ahead)
        else:
            with nc.Block() as block:
                block.sync(ahead)
        if ONLY in (0, 2):
            attention16(nc, C, "c0", "cross", w_c0)
        if ONLY in (0, 3):
            moe_slots(nc, C, a)
        if ONLY in (0, 4):
            attention16(nc, C, "a1", "causal", w_a1)
        if ONLY in (0, 5):
            C["tab_c"], C["tab_s"] = g.sb("tab_c", [P, NTAB, XD]), g.sb("tab_s", [P, NTAB, XD])
            rope_tables(nc, C, a)
            attention128(nc, C, w_x)
        if ONLY in (0, 6):
            moe_dense(nc, C, a)
        with nc.Block() as block:
            @block.sync
            def _(sp):
                sp.dma_start(out.rearrange("(n p) d -> p n d", p=P), C["x"][:, :, :]).then_inc(out_sem, 16)
                sp.wait_ge(out_sem, 16)
                sp.wait_ge(zero_ok, 16)


def kernel(**inputs):
    import concourse.bacc as bacc
    from concourse.bass_utils import run_bass_kernel_spmd as run

    nc = bacc.Bacc("TRN2", target_bir_lowering=False, num_devices=1)
    v = {k: np.asarray(t) for k, t in inputs.items()}

    def chunked(t):
        return t.reshape(t.shape[0] // P, P, -1).transpose(1, 0, 2)

    def column(t):
        return t.reshape(DC, P).T

    arrays = {
        "x": v["x"].reshape(NT, P, D).transpose(1, 0, 2),
        "ctxT": chunked(v["ctx_2048"].reshape(B * S, D).T),
        "mask": np.concatenate([v["mask_BxS2_ik0"].T] * 2),
        "rs": v["L0_xattn_residual_scale"].reshape(1, 1),
        "ident": np.eye(P, dtype=np.float32),
        "hmask": (np.arange(P)[:, None] // HD == np.arange(HG)).astype(np.float32),
        "cmask": np.where(np.arange(S) > np.arange(P)[:, None] % S, np.float32(-1e9 / QSCALE), np.float32(0)),
    }
    for tag, qkv, bias, wo, bo in (("a0", "L0_attn_Wqkv_w", "L0_attn_Wqkv_b", "L0_attn_out_w", "L0_attn_out_b"),
                                   ("a1", "L1_attn_w_qkv", None, "L1_attn_w_o", None)):
        for i, n in enumerate("qkv"):
            arrays[f"{tag}_w{n}"] = chunked(v[qkv][D * i:D * i + D].T)
            if bias:
                part = v[bias][D * i:D * i + D]
                arrays[f"{tag}_b{n}"] = part.reshape(1, D) if n == "v" else column(part)
        arrays[f"{tag}_wo"] = chunked(v[wo].T)
        if bo:
            arrays[f"{tag}_bo"] = v[bo].reshape(1, D)
    for n in "qkvo":
        arrays[f"c0_w{n}"] = chunked(v[f"L0_xattn_W{n}"].T)
        part = v[f"L0_xattn_b{n}"]
        arrays[f"c0_b{n}"] = column(part) if n in "qk" else part.reshape(1, D)
    arrays["c0_gamma"] = v["L0_xattn_ln_gamma"].reshape(1, D)
    arrays["c0_beta"] = v["L0_xattn_ln_beta"].reshape(1, D)

    pos, itok = v["pos_BxS2"].T, v["itok_BxS_4096_4607"]
    arrays["pos"] = np.concatenate([np.concatenate([pos, itok.T]), itok.reshape(NT, P).T], axis=1)
    arrays["inv"] = (np.float32(1) / np.float32(10000) ** (np.arange(0, XD, 2, dtype=np.float32) / np.float32(XD))).reshape(1, RH)
    arrays["qw"] = v["L1_xattn_q_norm_w"].reshape(1, XD)
    arrays["kw"] = v["L1_xattn_k_norm_w"].reshape(1, XD)
    for n in "qkvo":
        arrays[f"x_w{n}"] = chunked(v[f"L1_xattn_W{n}"].T)
    def gate_up(t):
        return t.reshape(-1, DC, P, 2, I0).transpose(0, 2, 1, 3, 4).reshape(-1, P, DC * 2 * I0)

    arrays["m0_wgu"] = gate_up(v["L0_ffn_w13"])
    arrays["m0_wd"] = v["L0_ffn_w2"]
    shared = gate_up(np.concatenate([v["L0_ffn_shared_gate_w"], v["L0_ffn_shared_up_w"]], axis=1))[0]
    arrays["m0_ws"] = np.concatenate([shared, v["L0_ffn_shared_down_w"]], axis=1)
    arrays["m0_gate"] = chunked(v["L0_ffn_gate_w"].T)
    arrays["m0_normw"] = v["L0_ffn_norm_w"].reshape(1, D)
    arrays["eids"] = np.arange(E0, dtype=np.float32).reshape(1, E0)
    arrays["before"] = np.triu(np.ones((P, P), np.float32), 1)
    def with_shared(experts, shared):
        return np.concatenate([experts, shared[None], np.zeros_like(shared[None])])

    gu = with_shared(v["L1_ffn_gu_w"].reshape(E1, 2, I1, D), np.stack([v["L1_ffn_sh_gate_w"], v["L1_ffn_sh_up_w"]]))
    gu = gu.reshape(NPAIR, 2, 2, I1, DC, P).transpose(0, 5, 4, 2, 1, 3)
    dp = with_shared(v["L1_ffn_dp_w"], v["L1_ffn_sh_down_w"]).transpose(0, 2, 1)
    arrays["m1_w"] = np.concatenate([gu.reshape(NPAIR, P, -1), dp.reshape(NPAIR, P, D)], axis=2)
    arrays["m1_gate"] = chunked(np.concatenate([v["L1_ffn_gate_w"], v["L1_ffn_sh_gate1_w"]]).T)
    arrays = {k: np.ascontiguousarray(t) for k, t in arrays.items()}
    a = {k: nc.dram_tensor(f"in_{k}", t.shape, mybir.dt.from_np(t.dtype), kind="ExternalInput").ap()
         for k, t in arrays.items()}
    out = nc.dram_tensor("out_x", [B * S, D], F32, kind="ExternalOutput").ap()
    decoder(nc, a, out)
    r = run(nc, [{f"in_{k}": t for k, t in arrays.items()}], core_ids=[0])
    return r.results[0]["out_x"].reshape(B, S, D)
```

```python
import numpy as np
import concourse.bass as bass
from concourse import mybir
from contextlib import ExitStack

F32 = mybir.dt.float32
F16 = mybir.dt.float16
BF16 = mybir.dt.bfloat16
I32 = mybir.dt.int32
U32 = mybir.dt.uint32
ALU = mybir.AluOpType
ACT = mybir.ActivationFunctionType
AX = mybir.AxisListType

P = 128
B, S, D = 16, 64, 256
NT = B * S // P
DC = D // P
H = 16
HD = D // H
HG = P // HD
NP = H // 2
OW = 2 * (HD + 1)
QSCALE = float(HD) ** -0.5
H_UP, W_UP = 32.0, 64.0
PASSES = ((0, 0), (1, 0), (0, 1))


class Store:

    def __init__(self, nc, last=False):
        self.nc, self.stack, self.held = nc, ExitStack(), []
        if not last:
            self.stack.callback(self.clear)

    def sb(self, name, shape, dt=F32):
        return self.stack.enter_context(self.nc.sbuf_tensor(name, shape, dt))

    def ps(self, name, shape):
        return self.stack.enter_context(self.nc.psum_tensor(name, shape, F32))

    def sem(self, name):
        self.held.append(self.nc.alloc_semaphore(name))
        return self.held[-1]

    def clear(self):
        if self.held:
            self.nc.clear_and_free_semaphores(self.held)
            self.nc.all_engine_barrier()

    def sems(self, prefix, names):
        return [self.sem(f"{prefix}_{n}") for n in names.split()]


def bcast(ap, axis, n):
    shape = list(ap.shape)
    shape.insert(axis, n)
    return ap.unsqueeze(axis).to_broadcast(shape)


def looped(eng, body, tiles=NT):
    with eng.Fori(0, tiles // 2) as i:
        body(i * 2, 0)
        body(i * 2 + 1, 1)


def skewed(eng, early, mixed, late):
    early(0, 0)
    mixed(0, 0, 1, 1)
    with eng.Fori(0, (NT - 4) // 2) as i:
        mixed(i * 2 + 1, 1, i * 2 + 2, 0)
        mixed(i * 2 + 2, 0, i * 2 + 3, 1)
    mixed(NT - 3, 1, NT - 2, 0)
    mixed(NT - 2, 0, NT - 1, 1)
    late(NT - 1, 1)


def there(n, count=NT):
    return type(n) is not int or 0 <= n < count


def attention16(nc, C, tag, kind, w, ahead=None, slots=None, split=None):
    cross, causal, biased = kind == "cross", kind == "causal", kind == "self"
    x, ident, hmask, neghalf = C["x"], C["ident"], C["hmask"], C["neghalf"]
    m = Store(nc)
    with m.stack:
        sb, ps = m.sb, m.ps
        wq, wk, wv, wo, loaded, nload = (w[k] for k in ("wq", "wk", "wv", "wo", "loaded", "count"))
        bq, bk = w.get("bq"), w.get("bk")
        bv, bo, gamma, beta = (w.get(k) for k in ("bv", "bo", "gamma", "beta"))
        st = sb(f"{tag}st", [P, 2, 6])
        mv = sb(f"{tag}mv", [P, 2, 4])
        hn = sb(f"{tag}hn", [P, 2, D])
        hT = sb(f"{tag}hT", [P, 2, DC, P])
        qT = sb(f"{tag}qT", [P, 2, DC, P])
        KB = sb(f"{tag}KB", [P, DC, HG, P])
        if causal:
            ident16 = sb(f"{tag}ident16", [P, P], BF16)
            cmask16 = sb(f"{tag}cmask16", [P, HG, S], BF16)
        V2 = sb(f"{tag}V2", [P, 2, NP, 2, OW])
        sc = sb(f"{tag}sc", [P, 2, H, S])
        mx = sb(f"{tag}mx", [P, H])
        cs = sb(f"{tag}cs", [P, 2, DC, P])
        PT = sb(f"{tag}PT", [P, 2, NP, P])
        rs = sb(f"{tag}rs", [P, 3, H])
        cn = sb(f"{tag}cn", [P, 2, D])
        cT = sb(f"{tag}cT", [P, 2, DC, P])
        dl = sb(f"{tag}dl", [P, 2, D])
        dst = sb(f"{tag}dst", [P, 6])
        dmv = sb(f"{tag}dmv", [P, 2, 4])
        p_qk = ps(f"{tag}pqk", [P, 2, DC, P])
        p_s = ps(f"{tag}ps", [P, 2, 512])
        p_t = ps(f"{tag}pt", [P, 2, 512])
        p_o = ps(f"{tag}po", [P, 2, 512])
        p_m = ps(f"{tag}pm", [P, 512])
        p_tp = p_t[:, :, :].rearrange("p a (n t) -> p (a n) t", t=P)
        p_sc = p_s[:, :, :].rearrange("p a (h k) -> p (a h) k", k=S)
        p_st = p_s[:, :, :].rearrange("p a (n t) -> p (a n) t", t=P)
        (var_ok, rstd_ok, hn_ok, turned, hT_ok, qk_ok, q_out, k_out, v_ok, v_out, s_ok, s_out,
         exp_ok, pt_ok, pt_out, o_ok, o_out, ct_ok, ct_out, proj_ok, zeroed, dve_step, dve_d,
         dvar_ok, drstd_ok, x_step, r_step, l_step, cs_ok, m_free, pool_step, mask_ok) = m.sems(tag, "var_ok rstd_ok hn_ok turned hT_ok qk_ok q_out k_out"
                                 " v_ok v_out s_ok s_out exp_ok pt_ok pt_out o_ok o_out ct_ok ct_out proj_ok"
                                 " zeroed dve_step dve_d dvar_ok drstd_ok x_step r_step l_step cs_ok m_free pool_step mask_ok")
        ctxT = C["ctxT"]
        block = m.stack.enter_context(nc.Block())

        if ahead:
            block.sync(ahead)

        @block.gpsimd
        def _(pool):
            pool.memset(V2[:, :, :, :, :], 0.0).then_inc(zeroed, 1)
            pool.wait_ge(zeroed, 1)
            for par in range(2):
                col = par * (HD + 1) + HD
                pool.memset(V2[64 * par:64 * par + 64, :, :, :, col:col + 1], 1.0).then_inc(zeroed, 1)

            def root(n, u):
                pool.wait_ge(var_ok, n + 1)
                pool.tensor_tensor(mv[:, u, 3:4], mv[:, u, 2:3], neghalf[:, 0:1], ALU.pow).then_inc(rstd_ok, 1)

            def droot(n, u):
                pool.wait_ge(dvar_ok, n + 1)
                pool.tensor_tensor(dmv[:, u, 3:4], dmv[:, u, 2:3], neghalf[:, 0:1], ALU.pow).then_inc(drstd_ok, 1)
                xt, d = x[:, bass.ds(n, 1), :].rearrange("p a d -> p (a d)"), dl[:, u, :]
                pool.wait_ge(drstd_ok, n + 1)
                for k, (dst, src, other, op) in enumerate((
                        (d, d, dmv[:, u, 0:1].to_broadcast([P, D]), ALU.subtract), (d, d, dmv[:, u, 3:4].to_broadcast([P, D]), ALU.mult),
                        (d, d, gamma[:, :], ALU.mult), (d, d, beta[:, :], ALU.add), (xt, xt, d, ALU.add))):
                    pool.tensor_tensor(dst, src, other, op).then_inc(pool_step, 1)
                    pool.wait_ge(pool_step, n * 5 + k + 1)

            def context(n, u):
                pool.tensor_copy(cs[:, u, :, :], ctxT[:, :, bass.ds(n * P, P)]).then_inc(cs_ok, 1)

            if slots:
                pool.wait_ge(zeroed, 3)
                slots.fold(pool, 0)
                root(0, 0)
                slots.fetch(pool, 1)
                slots.fold(pool, 1)
                root(1, 1)
                slots.fetch(pool, 2)
                for n in range(1, NT):
                    if n >= 2:
                        root(n, n % 2)
                    if n + 2 < NT:
                        slots.fetch(pool, n + 2)
                    if n >= 2:
                        slots.rope.product(pool, n - 2)
                    if n + 1 < NT:
                        slots.fold(pool, n + 1)
                for i in range(NT - 2, 8):
                    slots.rope.product(pool, i)
            elif not cross:
                looped(pool, root)
            else:
                root(0, 0)
                context(0, 0)
                root(1, 1)
                context(1, 1)

                def both(n, u):
                    root(n + 2, u)
                    split.low(pool, n)
                    pool.wait_ge(v_ok, n + 1)
                    context(n + 2, u)
                    droot(n, u)
                looped(pool, both, NT - 2)
                for n in (NT - 2, NT - 1):
                    split.low(pool, n)
                    droot(n, n % 2)

        @block.scalar
        def _(act):
            def h_out(n, u):
                act.wait_ge(turned, n + 1)
                act.activation(hT[:, u, :, :], p_tp[:, 0:DC, :], ACT.Copy).then_inc(hT_ok, 1)

            def q_copy(n, u):
                act.wait_ge(k_out, n + 1)
                for c in range(DC):
                    if causal:
                        ins = act.activation(qT[:, u, c, :], p_qk[:, 0, c, :], ACT.Copy)
                    else:
                        ins = act.activation(qT[:, u, c, :], p_qk[:, 0, c, :], ACT.Identity,
                                             bias=(bk if cross else bq)[:, c:c + 1])
                ins.then_inc(q_out, 1)

            def exps(n, u):
                act.wait_ge(s_out, n + 1)
                act.activation(sc[:, u, :, :], sc[:, u, :, :], ACT.Exp, scale=QSCALE).then_inc(exp_ok, 1)

            def pt_copy(n, u):
                act.wait_ge(pt_ok, n + 1)
                act.activation(PT[:, u, :, :], p_tp, ACT.Copy).then_inc(pt_out, 1)

            def ct_copy(n, u):
                act.wait_ge(ct_ok, n + 1)
                act.activation(cT[:, u, :, :], p_m[:, 0:D].rearrange("p (c t) -> p c t", c=DC), ACT.Copy).then_inc(ct_out, 1)

            act.wait_ge(loaded, nload)

            def weigh(n, u):
                if slots and there(n):
                    slots.weigh(act, n, u)

            def high_part(n):
                if split:
                    split.high(act, n)

            def early(n, u):
                weigh(0, 0)
                h_out(0, 0)
                q_copy(0, 0)
                weigh(1, 1)
                h_out(1, 1)
                exps(0, 0)
                weigh(2, 0)
                high_part(0)

            def mixed(n, u, n1, u1):
                if not cross:
                    pt_copy(n, u)
                q_copy(n1, u1)
                high_part(n1)
                ct_copy(n, u)
                if there(n + 2):
                    h_out(n + 2, u)
                weigh(n + 3, u1)
                exps(n1, u1)

            def late(n, u):
                if not cross:
                    pt_copy(n, u)
                ct_copy(n, u)

            skewed(act, early, mixed, late)

        @block.tensor
        def _(pe):
            def turn(n, u):
                pe.wait_ge(hn_ok, n + 1)
                for c in range(DC):
                    ins = pe.transpose(p_tp[:, c, :], hn[:, u, P * c:P * c + P], ident[:, :])
                ins.then_inc(turned, 1)

            def qk(n, u):
                pe.wait_ge(hT_ok, n + 1)
                if cross:
                    pe.wait_ge(cs_ok, n + 1)
                for slot in range(2):
                    weight = (wq, wk)[slot ^ cross]
                    for g in range(DC):
                        for c in range(DC):
                            src = hT[:, u, c, :]
                            if cross and slot == 0:
                                src = cs[:, u, c, :]
                            ins = pe.matmul(p_qk[:, slot, g, :], weight[:, c, P * g:P * g + P], src,
                                            start=(c == 0), stop=(c == DC - 1))
                ins.then_inc(qk_ok, 1)

            def values(n, u):
                for c in range(DC):
                    lhs = cs[:, u, c, :] if cross else hT[:, u, c, :]
                    ins = pe.matmul(p_m[:, 0:D], lhs, wv[:, c, :], start=(c == 0), stop=(c == DC - 1))
                ins.then_inc(v_ok, 1)

            def scores(n, u):
                pe.wait_ge(q_out, n + 1)
                pe.wait_ge(k_out, n + 1)
                for g in range(DC):
                    if causal:
                        pe.matmul(p_s[:, g, :], ident16[:, :], cmask16[:, :, :].rearrange("p h k -> p (h k)"),
                                  start=True, stop=False, skip_group_check=True)
                    for b in range(2):
                        ts = slice(S * b, S * b + S)
                        if not cross:
                            ins = pe.matmul(p_sc[S * b:S * b + S, HG * g:HG * g + HG, :], qT[:, u, g, ts],
                                            KB[:, g, :, ts], start=not causal, stop=True, skip_group_check=causal)
                        else:
                            for par in range(2):
                                ins = pe.matmul(p_st[S * par:S * par + S, 4 * g:4 * g + 4, ts],
                                                qT[:, u, g, ts], KB[:, g, par:HG:2, ts], start=True, stop=True)
                ins.then_inc(s_ok, 1)

            def turn_probs(n, u):
                pe.wait_ge(exp_ok, n + 1)
                for pr in range(NP):
                    ins = pe.transpose(p_tp[:, pr, :], sc[:, u, 2 * pr:2 * pr + 2, :].rearrange("p a k -> p (a k)"), ident[:, :])
                ins.then_inc(pt_ok, 1)

            def pv(n, u):
                pe.wait_ge(exp_ok if cross else pt_out, n + 1)
                pe.wait_ge(v_out, n + 1)
                E = sc[:, u, :, :].rearrange("p (a c) k -> p a (c k)", c=2)
                for pr in range(NP):
                    lhs = E[:, pr, :] if cross else PT[:, u, pr, :]
                    ins = pe.matmul(p_o[:, pr // 4, 2 * OW * (pr % 4):2 * OW * (pr % 4 + 1)], lhs,
                                    V2[:, u, pr, :, :].rearrange("p b c -> p (b c)"), start=True, stop=True)
                ins.then_inc(o_ok, 1)

            def turn_ctx(n, u):
                pe.wait_ge(o_out, n + 1)
                for c in range(DC):
                    ins = pe.transpose(p_m[:, P * c:P * c + P], cn[:, u, P * c:P * c + P], ident[:, :])
                ins.then_inc(ct_ok, 1)

            def project(n, u):
                pe.wait_ge(ct_out, n + 1)
                for c in range(DC):
                    ins = pe.matmul(p_m[:, 0:D], cT[:, u, c, :], wo[:, c, :], start=(c == 0), stop=(c == DC - 1))
                ins.then_inc(proj_ok, 1)

            pe.wait_ge(loaded, nload)
            pe.wait_ge(zeroed, 3)
            if causal:
                pe.wait_ge(mask_ok, 1)

            def early(n, u):
                turn(0, 0)
                qk(0, 0)
                values(0, 0)
                scores(0, 0)
                turn(1, 1)

            def mixed(n, u, n1, u1):
                qk(n1, u1)
                if not cross:
                    turn_probs(n, u)
                if type(n) is int and n == 0:
                    pe.wait_ge(v_out, 1)
                else:
                    pe.wait_ge(m_free, n)
                values(n1, u1)
                pv(n, u)
                scores(n1, u1)
                pe.wait_ge(v_out, n1 + 1)
                turn_ctx(n, u)
                if there(n + 2):
                    turn(n + 2, u)
                project(n, u)

            def late(n, u):
                if not cross:
                    turn_probs(n, u)
                pv(n, u)
                pe.wait_ge(m_free, n)
                turn_ctx(n, u)
                project(n, u)

            skewed(pe, early, mixed, late)

        @block.vector
        def _(dve):
            def norm_a(n, u):
                if slots:
                    slots.add(dve, n, u)
                dve.bn_stats(st[:, u, :], x[:, bass.ds(n, 1), :].rearrange("p a d -> p (a d)"))
                dve.drain()
                dve.bn_aggr(mv[:, u, 0:2], st[:, u, :]).then_inc(dve_step, 1)
                dve.wait_ge(dve_step, n + 1)
                dve.tensor_scalar(mv[:, u, 2:3], mv[:, u, 1:2], 1e-5, None, ALU.add).then_inc(var_ok, 1)

            def norm_b(n, u):
                dve.wait_ge(rstd_ok, n + 1)
                dve.tensor_scalar(hn[:, u, :], x[:, bass.ds(n, 1), :].rearrange("p a d -> p (a d)"), mv[:, u, 0:1], mv[:, u, 3:4],
                                  ALU.subtract, ALU.mult).then_inc(hn_ok, 1)

            def k_mask(n, u):
                dve.wait_ge(qk_ok, n + 1)
                for g in range(DC):
                    src = bcast(p_qk[:, 1, g, :], 1, HG)
                    mask = bcast(hmask[:, :], 2, P)
                    if causal:
                        ins = dve.tensor_tensor(KB[:, g, :, :], src, mask, ALU.mult)
                    else:
                        ins = dve.scalar_tensor_tensor(KB[:, g, :, :], src, (bq if cross else bk)[:, g:g + 1], mask, ALU.add, ALU.mult)
                ins.then_inc(k_out, 1)

            def v_copy(n, u):
                dve.wait_ge(v_ok, n + 1)
                for b in range(2):
                    for par in range(2):
                        src = p_m[S * b:S * b + S, 0:D].rearrange("p (n a d) -> p n a d", a=2, d=HD)[:, :, par, :]
                        dst = V2[64 * par:64 * par + 64, u, :, b, par * (HD + 1):par * (HD + 1) + HD]
                        if causal:
                            ins = dve.tensor_copy(dst, src)
                        else:
                            bias = bv[S * b:S * b + S, :].rearrange("p (n a d) -> p n a d", a=2, d=HD)[:, :, par, :]
                            ins = dve.tensor_tensor(dst, src, bias, ALU.add)
                ins.then_inc(v_out, 1)

            def soft(n, u):
                dve.wait_ge(s_ok, n + 1)
                if cross:
                    E = sc[:, u, :, :].rearrange("p (a c) k -> p a (c k)", c=2)
                    for b in range(2):
                        ts = slice(S * b, S * b + S)
                        hi = C["hi"][:, bass.ds(n * 2 + b, 1)]
                        ins = dve.tensor_scalar(E[:, :, ts], p_st[:, :, ts], -50.0 / QSCALE, hi, ALU.max, ALU.min)
                    ins.then_inc(s_out, 1)
                    return
                dve.tensor_reduce(mx[:, :], p_sc, AX.X, ALU.max).then_inc(dve_d, 1)
                dve.wait_ge(dve_d, n + 1)
                dve.tensor_tensor(sc[:, u, :, :], p_sc, bcast(mx[:, :], 2, S), ALU.subtract).then_inc(s_out, 1)

            def o_norm(n, u):
                dve.wait_ge(o_ok, n + 1)
                O = p_o[:, :, 0:8 * OW].rearrange("p a (n b e d) -> p a n b e d", n=4, b=2, e=2)
                for b in range(2):
                    r = slice(S * b, S * b + S)
                    ins = dve.reciprocal(rs[r, 0, :].rearrange("p (a n e) -> p a n e", a=2, e=2), O[r, :, :, b, :, HD])
                    if cross:
                        ins = dve.tensor_copy(rs[r, 1, :].rearrange("p (a n e) -> p a n e", a=2, e=2), O[r, :, :, b, :, HD])
                steps = 4 if cross else 1
                ins.then_inc(x_step, 1)
                dve.wait_ge(x_step, n * steps + 1)
                if cross:
                    dve.tensor_tensor(rs[:, 1, :], rs[:, 1, :], rs[:, 0, :], ALU.mult).then_inc(x_step, 1)
                    dve.wait_ge(x_step, n * steps + 2)
                    dve.tensor_scalar(rs[:, 1, :], rs[:, 1, :], 1e-8, None, ALU.add).then_inc(x_step, 1)
                    dve.wait_ge(x_step, n * steps + 3)
                    dve.reciprocal(rs[:, 2, :], rs[:, 1, :]).then_inc(x_step, 1)
                    dve.wait_ge(x_step, n * steps + 4)
                    dve.tensor_tensor(rs[:, 0, :], rs[:, 0, :], rs[:, 2, :], ALU.mult).then_inc(r_step, 1)
                    dve.wait_ge(r_step, n + 1)
                for b in range(2):
                    r = slice(S * b, S * b + S)
                    for a in range(2):
                        dst = cn[r, u, P * a:P * a + P].rearrange("p (n e d) -> p n e d", e=2, d=HD)
                        rr = bcast(rs[r, 0, 8 * a:8 * a + 8].rearrange("p (n e) -> p n e", e=2), 3, HD)
                        ins = dve.tensor_tensor(dst, O[r, a, :, b, :, 0:HD], rr, ALU.mult)
                ins.then_inc(o_out, 1)

            def residual(n, u):
                xt = x[:, bass.ds(n, 1), :].rearrange("p a d -> p (a d)")
                dve.wait_ge(proj_ok, n + 1)
                if causal:
                    dve.tensor_tensor(xt, xt, p_m[:, 0:D], ALU.add).then_inc(m_free, 1)
                elif biased:
                    dve.tensor_tensor(dl[:, u, :], p_m[:, 0:D], bo[:, :], ALU.add).then_inc(m_free, 1)
                    dve.wait_ge(m_free, n + 1)
                    dve.tensor_tensor(xt, xt, dl[:, u, :], ALU.add)
                else:
                    if type(n) is not int or n >= 1:
                        dve.wait_ge(pool_step, n * 5 - 4)
                    dve.tensor_tensor(dl[:, u, :], p_m[:, 0:D], bo[:, :], ALU.add).then_inc(m_free, 1)
                    dve.wait_ge(m_free, n + 1)
                    dve.tensor_scalar(dl[:, u, :], dl[:, u, :], C["rs"][:, 0:1], None, ALU.mult)
                    dve.drain()
                    dve.bn_stats(dst[:, :], dl[:, u, :])
                    dve.drain()
                    dve.bn_aggr(dmv[:, u, 0:2], dst[:, :]).then_inc(l_step, 1)
                    dve.wait_ge(l_step, n + 1)
                    dve.tensor_scalar(dmv[:, u, 2:3], dmv[:, u, 1:2], 1e-5, None, ALU.add).then_inc(dvar_ok, 1)

            dve.wait_ge(loaded, nload)
            dve.wait_ge(zeroed, 3)
            if causal:
                dve.tensor_copy(ident16[:, :], ident[:, :])
                dve.tensor_copy(cmask16[:, :, :], bcast(C["cmask"][:, :], 1, HG)).then_inc(mask_ok, 1)

            def early(n, u):
                norm_a(0, 0)
                norm_b(0, 0)
                k_mask(0, 0)
                v_copy(0, 0)
                norm_a(1, 1)
                norm_b(1, 1)
                soft(0, 0)

            def mixed(n, u, n1, u1):
                k_mask(n1, u1)
                v_copy(n1, u1)
                if there(n + 2):
                    norm_a(n + 2, u)
                o_norm(n, u)
                if there(n + 2):
                    norm_b(n + 2, u)
                soft(n1, u1)
                residual(n, u)

            def late(n, u):
                o_norm(n, u)
                residual(n, u)

            skewed(dve, early, mixed, late)


def moved(sp, done, pairs):
    for dst, src in pairs:
        sp.dma_start(dst, src).then_inc(done, 16)
    return 16 * len(pairs)


XH, KVH, XD = 16, 4, 128
XSCALE = float(1.0 / np.sqrt(np.float32(XD)))
RH = XD // 2
KEYS = 2 * S
NTAB = B + NT
TWO_PI = 6.283185307179586
PI_A = float(np.frombuffer(np.array([np.float32(TWO_PI).view(np.uint32) & 0xFFFF8000], np.uint32).tobytes(), np.float32)[0])
PI_B = float(np.frombuffer(np.array([np.float32(TWO_PI - PI_A).view(np.uint32) & 0xFFFF8000], np.uint32).tobytes(), np.float32)[0])
PI_C = float(np.float32(TWO_PI - PI_A - PI_B))
ROUND = 12582912.0
PI_MAX = 3.1415925


class Split:
    COLS = DC * (XH + 2 * KVH) * XD

    def __init__(self, g, loaded):
        self.raw = g.sb("xraw", [P, self.COLS])
        self.parts = g.sb("xparts", [P, 2, self.COLS], F16)
        self.loaded, self.high_ok, self.low_ok = loaded, g.sem("xw_high_ok"), g.sem("xw_low_ok")

    def share(self, n):
        return bass.ds(n * (self.COLS // NT), self.COLS // NT)

    def high(self, act, n):
        if type(n) is int and n == 0:
            act.wait_ge(self.loaded, 64)
        act.activation(self.parts[:, 0, self.share(n)], self.raw[:, self.share(n)], ACT.Copy, scale=W_UP)
        act.activation(self.raw[:, self.share(n)], self.raw[:, self.share(n)], ACT.Copy, scale=W_UP).then_inc(self.high_ok, 1)

    def low(self, pool, n):
        pool.wait_ge(self.high_ok, n + 1)
        pool.tensor_tensor(self.parts[:, 1, self.share(n)], self.raw[:, self.share(n)], self.parts[:, 0, self.share(n)],
                           ALU.subtract).then_inc(self.low_ok, 1)

    def block(self, first, heads):
        cols = slice(DC * first * XD, DC * (first + heads) * XD)
        return (self.parts[:, :, cols].rearrange("p s (c n) -> p s c n", c=DC),
                self.raw[:, cols].rearrange("p (c n) -> p c n", c=DC))


class RopeTables:

    def __init__(self, g, a, room):
        self.a = a
        self.posi = g.sb("posi", [P, NTAB], I32)
        self.pos = g.sb("pos", [P, NTAB])
        self.inv = g.sb("inv", [P, RH])
        self.nw = g.sb("nw", [P, 2, XD])
        self.neg = g.sb("nwneg", [P, 2, RH])
        self.ang = g.sb("ang", [P, NTAB, RH])
        self.turns = g.sb("turns", [P, NTAB, RH])
        self.red = g.sb("red", [P, 2, NTAB, RH])
        self.tab_c, self.tab_s = (room[:, NTAB * XD * k:NTAB * XD * (k + 1)].rearrange("p (n d) -> p n d", d=XD) for k in range(2))
        self.loaded, self.step, self.trig, self.made = (g.sem(f"tab_{n}") for n in ("loaded", "step", "trig", "made"))
        self.steps = 0

    def load(self, sp):
        a = self.a
        moved(sp, self.loaded, [(self.posi[:, :], a["pos"]), (self.inv[:, :], a["inv"].to_broadcast([P, RH])),
                                (self.nw[:, 0, :], a["kw"].to_broadcast([P, XD])),
                                (self.nw[:, 1, :], a["qw"].to_broadcast([P, XD]))])

    def then(self, dve, ins):
        self.steps += 1
        ins.then_inc(self.step, 1)
        dve.wait_ge(self.step, self.steps)

    def angles(self, dve):
        ang, turns = self.ang[:, :, :], self.turns[:, :, :]
        dve.wait_ge(self.loaded, 64)
        self.then(dve, dve.tensor_copy(self.pos[:, :], self.posi[:, :]))
        self.then(dve, dve.tensor_scalar(self.neg[:, :, :], self.nw[:, :, RH:XD], -1.0, None, ALU.mult))
        self.then(dve, dve.tensor_tensor(ang, bcast(self.pos[:, :], 2, RH), bcast(self.inv[:, :], 1, NTAB), ALU.mult))
        self.then(dve, dve.tensor_scalar(turns, ang, 1.0 / TWO_PI, None, ALU.mult))

    def rounded(self, dve):
        turns = self.turns[:, :, :]
        self.then(dve, dve.tensor_scalar(turns, turns, ROUND, None, ALU.add))
        self.then(dve, dve.tensor_scalar(turns, turns, -ROUND, None, ALU.add))

    def reduced(self, dve, i):
        red = self.red[:, 0, :, :]
        self.then(dve, dve.scalar_tensor_tensor(red, self.turns[:, :, :], -(PI_A, PI_B, PI_C)[i], red if i else self.ang[:, :, :],
                                                ALU.mult, ALU.add))

    def shifted(self, dve, i):
        turns, red, cos, both = self.turns[:, :, :], self.red[:, 0, :, :], self.red[:, 1, :, :], self.red[:, :, :, :]
        if i == 0:
            self.then(dve, dve.tensor_scalar(turns, red, TWO_PI / 4, -TWO_PI, ALU.is_gt, ALU.mult))
        elif i == 1:
            self.then(dve, dve.scalar_tensor_tensor(cos, red, TWO_PI / 4, turns, ALU.add, ALU.add))
        else:
            self.then(dve, dve.tensor_scalar(both, both, PI_MAX, -PI_MAX, ALU.min, ALU.max))

    def sines(self, act):
        act.wait_ge(self.step, 9 + 3)
        act.activation(self.red[:, :, :, :], self.red[:, :, :, :], ACT.Sin).then_inc(self.trig, 1)

    def product(self, pool, i):
        sine, which, half = i // 4, i // 2 % 2, i % 2
        r = (slice(0, B), slice(B, NTAB))[which]
        n = r.stop - r.start
        mine = slice(RH * half, RH * half + RH)
        if sine:
            dst, w = self.tab_s, self.nw[:, which, 0:RH] if half else self.neg[:, which, :]
        else:
            dst, w = self.tab_c, self.nw[:, which, mine]
        if i == 0:
            pool.wait_ge(self.trig, 1)
        pool.tensor_tensor(dst[:, r, mine], self.red[:, 1 - sine, r, :], bcast(w, 1, n), ALU.mult).then_inc(self.made, 1)
        pool.wait_ge(self.made, i + 1)


def attention128(nc, C, w):
    x, ident, neghalf, ctxT = C["x"], C["ident"], C["neghalf"], C["ctxT"]
    tc, ts = C["rope"].tab_c, C["rope"].tab_s
    m = Store(nc)
    NSQ = XH + 2 * KVH
    with m.stack:
        sb, ps = m.sb, m.ps
        wq, wk, wv, wo, loaded = (w[k] for k in ("wq", "wk", "wv", "wo", "loaded"))
        st = sb("xst", [P, 2, 6])
        mv = sb("xmv", [P, 2, 4])
        hn = sb("xhn", [P, 2, D])
        kv = sb("xkv", [P, 2, 2, DC, 2, KEYS], F16)
        qr = sb("xqr", [P, NSQ, XD])
        t2 = sb("xt2", [P, 2, 4, XD])
        sq = sb("xsq", [P, 2, 4, XD])
        ss = sb("xss", [P, NSQ])
        sv = sb("xsv", [P, NSQ])
        sr = sb("xsr", [P, NSQ])
        V = sb("xV", [P, 2, 2, KVH, XD])
        QT = sb("xQT", [P, 2, XH, S])
        KT = sb("xKT", [P, 2 * KVH, KEYS])
        hs = sb("xhs", [P, 2, 2, DC, P], F16)
        E = sb("xE", [P, XH, KEYS])
        mx = sb("xmx", [P, XH])
        nb = sb("xnb", [P, XH])
        sm = sb("xsm", [P, XH])
        rc = sb("xrc", [P, XH])
        PT = sb("xPT", [P, 2, 4, P])
        OT = sb("xOT", [P, XH, 2, S])
        p_r = [ps(f"xpr{i}", [P, 4, XD]) for i in range(2)]
        p_t = [ps(f"xpt{i}", [P, 4, P]) for i in range(2)]
        p_s = [ps(f"xps{i}", [P, 4, KEYS]) for i in range(2)]
        p_o = [ps(f"xpo{i}", [P, 512]) for i in range(2)]
        (stat_ok, var_ok, rstd_ok, hn_ok, ctx_ok, r_ok, sq_ok, rope_ok, v_out, add_ok, ms_ok, sr_ok, ss_ok,
         scaled, t_ok, t_out, s_ok, max_ok, nb_ok, exp_ok, rc_ok, e_ok, o_ok, o_out, proj_ok, x_ok, high_ok, chigh_ok) = m.sems(
            "x", "stat_ok var_ok rstd_ok hn_ok ctx_ok r_ok sq_ok rope_ok v_out add_ok ms_ok sr_ok ss_ok"
                 " scaled t_ok t_out s_ok max_ok nb_ok exp_ok rc_ok e_ok o_ok o_out proj_ok x_ok high_ok chigh_ok")
        FIRST_T, STEP_T = 6, 11
        T_K, T_P, T_Q, T_H = (0, 1), (2, 3, 4, 6), (5, 7, 8, 10), 9

        def turns(n, u):
            base = n * STEP_T + FIRST_T
            if type(n) is int and n == NT - 1:
                base -= 1
                return base, lambda k: (base + k) % 2
            return base, lambda k: (u + k) % 2

        def t_q(n, i):
            return T_Q[i] - (i == 3 and not there(n + 2))

        block = m.stack.enter_context(nc.Block())

        @block.gpsimd
        def _(pool):
            def root(n, u):
                pool.wait_ge(var_ok, n + 1)
                pool.tensor_tensor(mv[:, u, 3:4], mv[:, u, 2:3], neghalf[:, 0:1], ALU.pow).then_inc(rstd_ok, 1)

            def add(n, k):
                pool.wait_ge(rope_ok, n * 6 + k + 1)
                blk = qr[:, 4 * k:4 * k + 4, :]
                pool.tensor_tensor(blk, blk, t2[:, k % 2, :, :], ALU.add).then_inc(add_ok, 1)

            def rms_root(n, part):
                pool.wait_ge(ms_ok, n * 2 + part + 1)
                c = RMS[part]
                pool.tensor_tensor(sr[:, c], sv[:, c], neghalf[:, 0:1].to_broadcast([P, c.stop - c.start]), ALU.pow).then_inc(sr_ok, 1)

            def step(n1, u1):
                for k in range(4):
                    add(n1, k)
                rms_root(n1, 0)
                add(n1, 4)
                if type(n1) is not int or 1 <= n1 < NT - 1:
                    root(n1 + 1, 1 - u1)
                add(n1, 5)
                rms_root(n1, 1)

            root(0, 0)
            root(1, 1)
            step(0, 0)
            step(1, 1)
            with pool.Fori(0, (NT - 4) // 2) as i:
                step(i * 2 + 2, 0)
                step(i * 2 + 3, 1)
            step(NT - 2, 0)
            step(NT - 1, 1)

        @block.scalar
        def _(act):
            def turned(j, dst, src):
                act.wait_ge(t_ok, j + 1)
                act.activation(dst, src, ACT.Copy).then_inc(t_out, 1)

            def own(t):
                return t.rearrange("p c (b k) -> p c b k", b=2)

            def h_out(n, u, j, bank):
                act.wait_ge(t_ok, j + 1)
                act.activation(hs[:, u, 0, :, :], p_t[bank][:, 0:DC, :], ACT.Copy, scale=H_UP)
                act.activation(kv[:, u, 0, :, :, S:KEYS], own(p_t[bank][:, 0:DC, :]), ACT.Copy, scale=H_UP).then_inc(high_ok, 1)
                act.activation(kv[:, u, 0, :, :, 0:S], own(ctxT[:, :, bass.ds(n * P, P)]), ACT.Copy, scale=H_UP).then_inc(chigh_ok, 1)

            def qk_out(j, i, bank):
                if i < 4:
                    dst = QT[:, :, 4 * i:4 * i + 4, :]
                    turned(j, dst.rearrange("p b h q -> p h b q"), p_t[bank][:, :, :].rearrange("p h (b q) -> p h b q", b=2))
                else:
                    turned(j, KT[:, 4 * (i - 4):4 * (i - 4) + 4, :], p_t[bank][:, :, :])

            def square(n, k):
                act.wait_ge(r_ok, n * 8 + k + 1)
                act.activation(sq[:, SQI[k] % 2, :, :], p_r[k % 2][:, :, :], ACT.Square).then_inc(sq_ok, 1)

            def v_copy(n, u, k):
                act.wait_ge(r_ok, n * 8 + k + 1)
                act.activation(V[:, u, (k - 5) // 2, :, :], p_r[k % 2][:, :, :], ACT.Copy, scale=1.0 / (H_UP * W_UP)).then_inc(v_out, 1)

            def exps(n, k):
                act.wait_ge(nb_ok, n * 4 + k + 1)
                for i in range(4):
                    c = 4 * k + i
                    ins = act.activation(E[:, c, :], p_s[k % 2][:, i, :], ACT.Exp, bias=nb[:, c:c + 1], scale=XSCALE,
                                         accum_out=sm[:, c:c + 1])
                ins.then_inc(exp_ok, 1)

            def pt_copy(n, k, j, bank):
                turned(j, PT[:, k % 2, :, :], p_t[bank][:, :, :])

            def o_copy(n, u, k):
                act.wait_ge(o_ok, n * 4 + k + 1)
                act.activation(OT[:, 8 * (k % 2):8 * (k % 2) + 8, k // 2, :],
                               p_o[(u + k) % 2][:, :].rearrange("p (h q) -> p h q", q=S), ACT.Copy).then_inc(o_out, 1)

            def early(n, u):
                h_out(0, 0, 0, 0)
                for k in (0, 1, 2, 3, 4):
                    square(0, k)
                    if k == 1:
                        h_out(1, 1, 1, 1)
                v_copy(0, 0, 5)
                square(0, 6)
                v_copy(0, 0, 7)
                act.wait_ge(t_out, 2)
                for i in range(4):
                    qk_out(2 + i, i, i % 2)

            def mixed(n, u, n1, u1):
                base, bank = turns(n, u)
                square(n1, 0)
                qk_out(base + T_K[0], 4, bank(T_K[0]))
                square(n1, 1)
                qk_out(base + T_K[1], 5, bank(T_K[1]))
                square(n1, 2)
                exps(n, 0)
                square(n1, 3)
                exps(n, 1)
                square(n1, 4)
                pt_copy(n, 0, base + T_P[0], bank(T_P[0]))
                v_copy(n1, u1, 5)
                pt_copy(n, 1, base + T_P[1], bank(T_P[1]))
                o_copy(n, u, 0)
                exps(n, 2)
                o_copy(n, u, 1)
                square(n1, 6)
                exps(n, 3)
                pt_copy(n, 2, base + T_P[2], bank(T_P[2]))
                qk_out(base + T_Q[0], 0, bank(T_Q[0]))
                v_copy(n1, u1, 7)
                pt_copy(n, 3, base + T_P[3], bank(T_P[3]))
                qk_out(base + T_Q[1], 1, bank(T_Q[1]))
                o_copy(n, u, 2)
                qk_out(base + T_Q[2], 2, bank(T_Q[2]))
                if there(n + 2):
                    h_out(n + 2, u, base + T_H, bank(T_H))
                o_copy(n, u, 3)
                if there(n + 2):
                    act.wait_ge(t_out, base + T_H + 1)
                qk_out(base + t_q(n, 3), 3, bank(t_q(n, 3)))

            def late(n, u):
                base, bank = turns(n, u)
                qk_out(base, 4, bank(0))
                qk_out(base + 1, 5, bank(1))
                exps(n, 0)
                exps(n, 1)
                pt_copy(n, 0, base + 2, bank(2))
                pt_copy(n, 1, base + 3, bank(3))
                o_copy(n, u, 0)
                exps(n, 2)
                o_copy(n, u, 1)
                exps(n, 3)
                pt_copy(n, 2, base + 4, bank(4))
                pt_copy(n, 3, base + 5, bank(5))
                o_copy(n, u, 2)
                o_copy(n, u, 3)

            skewed(act, early, mixed, late)

        @block.tensor
        def _(pe):
            def turn_h(n, u, j, bank):
                pe.wait_ge(hn_ok, n + 1)
                for c in range(DC):
                    ins = pe.transpose(p_t[bank][:, c, :], hn[:, u, P * c:P * c + P], ident[:, :])
                ins.then_inc(t_ok, 1)

            def fill(n, u, k, first=False):
                freed = {0: (rope_ok, n * 6), 1: (v_out, n * 2), 2: (rope_ok, n * 6 + 1), 3: (rope_ok, n * 6 + 2),
                         4: (rope_ok, n * 6 + 3), 5: (rope_ok, n * 6 + 4), 6: (rope_ok, n * 6 + 5), 7: (v_out, n * 2 + 1)}
                pe.wait_ge(*freed[k])
                i = 0
                for c in range(DC):
                    for sw, sx in PASSES:
                        if k < 4:
                            lhs, rhs = hs[:, u, sx, c, :], wq[:, sw, c, 512 * k:512 * k + 512]
                        else:
                            lhs, rhs = kv[:, u, sx, c, (k - 4) // 2, :], (wk, wv)[k % 2][:, sw, c, :]
                        ins = pe.matmul(p_r[k % 2][:, :, :].rearrange("p h d -> p (h d)"), lhs, rhs, start=(i == 0), stop=(i == 5))
                        i += 1
                ins.then_inc(r_ok, 1)

            def scores(n, k):
                b, half = k // 2, k % 2
                pe.wait_ge(exp_ok, n * 4 + max(k - 1, 0))
                for i in range(4):
                    h = 8 * half + 2 * i
                    ins = pe.matmul(p_s[k % 2][:, i, :], QT[:, b, h:h + 2, :].rearrange("p h q -> p (h q)"),
                                    KT[:, KVH * b + h // 4, :], start=True, stop=True)
                ins.then_inc(s_ok, 1)

            def turn_probs(n, k, j, bank):
                pe.wait_ge(e_ok, n * 4 + k + 1)
                pe.wait_ge(t_out, j - 1)
                for i in range(4):
                    ins = pe.transpose(p_t[bank][:, i, :], E[:, 4 * k + i, :], ident[:, :])
                ins.then_inc(t_ok, 1)

            def pv(n, u, k, j):
                pe.wait_ge(t_out, j + 1)
                if k == 1:
                    pe.wait_ge(x_ok, n)
                else:
                    pe.wait_ge(o_out, n * 4 + max(k - 1, 0))
                if k == 0:
                    pe.wait_ge(v_out, n * 2 + 2)
                for g in range(2):
                    ins = pe.matmul(p_o[(u + k) % 2][:, 256 * g:256 * g + 256], V[:, u, k // 2, 2 * (k % 2) + g, :],
                                    PT[:, k % 2, 2 * g:2 * g + 2, :].rearrange("p i q -> p (i q)"), start=True, stop=True)
                ins.then_inc(o_ok, 1)

            def project(n, u, quarter):
                if quarter == 0:
                    pe.wait_ge(o_out, n * 4 + 4)
                for h in range(4 * quarter, 4 * quarter + 4):
                    ins = pe.matmul(p_o[u][:, 0:D], OT[:, h, :, :].rearrange("p b q -> p (b q)"), wo[:, h, :],
                                    start=(h == 0), stop=(h == XH - 1))
                if quarter == 3:
                    ins.then_inc(proj_ok, 1)

            def turn_qk(n, i, j, bank):
                pe.wait_ge(scaled, n * 6 + i + 1)
                pe.wait_ge(t_out, j - 1)
                for c in range(4):
                    ins = pe.transpose(p_t[bank][:, c, :], qr[:, 4 * i + c, :], ident[:, :])
                ins.then_inc(t_ok, 1)

            pe.wait_ge(loaded, 64)

            def early(n, u):
                turn_h(0, 0, 0, 0)
                pe.wait_ge(t_out, 1)
                for k in range(8):
                    if k == 2:
                        turn_h(1, 1, 1, 1)
                    if k == 4:
                        pe.wait_ge(ctx_ok, 1)
                    fill(0, 0, k)
                for i in range(4):
                    turn_qk(0, i, 2 + i, i % 2)

            def mixed(n, u, n1, u1):
                base, bank = turns(n, u)

                def project_before(quarter):
                    if there(n - 1):
                        project(n - 1, 1 - u, quarter)

                pe.wait_ge(t_out, base - 1)
                fill(n1, u1, 0)
                turn_qk(n, 4, base + T_K[0], bank(T_K[0]))
                project_before(0)
                fill(n1, u1, 1)
                turn_qk(n, 5, base + T_K[1], bank(T_K[1]))
                project_before(1)
                pe.wait_ge(t_out, base + 2)
                scores(n, 0)
                fill(n1, u1, 2)
                scores(n, 1)
                project_before(2)
                fill(n1, u1, 3)
                project_before(3)
                pe.wait_ge(ctx_ok, n1 + 1)
                fill(n1, u1, 4)
                turn_probs(n, 0, base + T_P[0], bank(T_P[0]))
                fill(n1, u1, 5)
                turn_probs(n, 1, base + T_P[1], bank(T_P[1]))
                pv(n, u, 0, base + T_P[0])
                scores(n, 2)
                pv(n, u, 1, base + T_P[1])
                scores(n, 3)
                fill(n1, u1, 6)
                turn_probs(n, 2, base + T_P[2], bank(T_P[2]))
                turn_qk(n1, 0, base + T_Q[0], bank(T_Q[0]))
                fill(n1, u1, 7)
                turn_probs(n, 3, base + T_P[3], bank(T_P[3]))
                turn_qk(n1, 1, base + T_Q[1], bank(T_Q[1]))
                pv(n, u, 2, base + T_P[2])
                turn_qk(n1, 2, base + T_Q[2], bank(T_Q[2]))
                if there(n + 2):
                    pe.wait_ge(t_out, base + T_H - 1)
                    turn_h(n + 2, u, base + T_H, bank(T_H))
                pv(n, u, 3, base + T_P[3])
                turn_qk(n1, 3, base + t_q(n, 3), bank(t_q(n, 3)))

            def late(n, u):
                base, bank = turns(n, u)
                turn_qk(n, 4, base, bank(0))
                turn_qk(n, 5, base + 1, bank(1))
                for quarter in range(4):
                    project(n - 1, 1 - u, quarter)
                pe.wait_ge(t_out, base + 2)
                scores(n, 0)
                scores(n, 1)
                turn_probs(n, 0, base + 2, bank(2))
                turn_probs(n, 1, base + 3, bank(3))
                pv(n, u, 0, base + 2)
                scores(n, 2)
                pv(n, u, 1, base + 3)
                scores(n, 3)
                turn_probs(n, 2, base + 4, bank(4))
                turn_probs(n, 3, base + 5, bank(5))
                pv(n, u, 2, base + 4)
                pv(n, u, 3, base + 5)
                for quarter in range(4):
                    project(n, u, quarter)

            skewed(pe, early, mixed, late)

        @block.vector
        def _(dve):
            def tile_of(n):
                return x[:, bass.ds(n, 1), :].rearrange("p a d -> p (a d)")

            def norm_a(n, u):
                dve.bn_stats(st[:, u, :], tile_of(n))
                dve.drain()
                dve.bn_aggr(mv[:, u, 0:2], st[:, u, :]).then_inc(stat_ok, 1)
                dve.wait_ge(stat_ok, n + 1)
                dve.tensor_scalar(mv[:, u, 2:3], mv[:, u, 1:2], 1e-5, None, ALU.add).then_inc(var_ok, 1)

            def norm_b(n, u):
                dve.wait_ge(rstd_ok, n + 1)
                dve.tensor_scalar(hn[:, u, :], tile_of(n), mv[:, u, 0:1], mv[:, u, 3:4], ALU.subtract, ALU.mult).then_inc(hn_ok, 1)

            def low(n, u, bank):
                own = lambda t: t.rearrange("p c (b k) -> p c b k", b=2)
                dve.wait_ge(high_ok, n + 1)
                dve.scalar_tensor_tensor(hs[:, u, 1, :, :], p_t[bank][:, 0:DC, :], H_UP, hs[:, u, 0, :, :], ALU.mult, ALU.subtract)
                dve.scalar_tensor_tensor(kv[:, u, 1, :, :, S:KEYS], own(p_t[bank][:, 0:DC, :]), H_UP, kv[:, u, 0, :, :, S:KEYS],
                                         ALU.mult, ALU.subtract).then_inc(t_out, 1)
                dve.wait_ge(chigh_ok, n + 1)
                dve.scalar_tensor_tensor(kv[:, u, 1, :, :, 0:S], own(ctxT[:, :, bass.ds(n * P, P)]), H_UP, kv[:, u, 0, :, :, 0:S],
                                         ALU.mult, ALU.subtract).then_inc(ctx_ok, 1)

            def rope(n, i):
                k = RING[i]
                src, blk = p_r[k % 2], qr[:, 4 * i:4 * i + 4, :]
                row = n + B if i < 4 else n * 2 + (i - 4)
                dve.wait_ge(sq_ok, n * 6 + i + 1)
                if type(n) is not int or n * 6 + i > 1:
                    dve.wait_ge(add_ok, n * 6 + i - 1)
                cosw = tc[:, bass.ds(row, 1), :].rearrange("p a d -> p (a d)")
                sinw = ts[:, bass.ds(row, 1), :].rearrange("p a d -> p (a d)")
                dve.tensor_reduce(ss[:, 4 * i:4 * i + 4], sq[:, i % 2, :, :], AX.X, ALU.add).then_inc(ss_ok, 1)
                dve.tensor_tensor(blk, src[:, :, :], bcast(cosw, 1, 4), ALU.mult)
                for half in range(2):
                    mine, other = slice(RH * half, RH * half + RH), slice(RH * (1 - half), RH * (1 - half) + RH)
                    ins = dve.tensor_tensor(t2[:, i % 2, :, mine], src[:, :, other], bcast(sinw[:, mine], 1, 4), ALU.mult)
                ins.then_inc(rope_ok, 1)

            def mean_square(n, part):
                dve.wait_ge(ss_ok, n * 6 + (4, 6)[part])
                dve.tensor_scalar(sv[:, RMS[part]], ss[:, RMS[part]], 1.0 / XD, 1e-6 * (H_UP * W_UP) ** 2, ALU.mult, ALU.add).then_inc(ms_ok, 1)

            def scale(n, i):
                dve.wait_ge(sr_ok, n * 2 + i // 4 + 1)
                dve.wait_ge(add_ok, n * 6 + i + 1)
                blk = qr[:, 4 * i:4 * i + 4, :]
                dve.tensor_tensor(blk, blk, bcast(sr[:, 4 * i:4 * i + 4], 2, XD), ALU.mult).then_inc(scaled, 1)

            def maxes(n, k):
                c = slice(4 * k, 4 * k + 4)
                dve.wait_ge(s_ok, n * 4 + k + 1)
                dve.tensor_reduce(mx[:, c], p_s[k % 2][:, :, :], AX.X, ALU.max).then_inc(max_ok, 1)
                dve.wait_ge(max_ok, n * 4 + k + 1)
                dve.tensor_scalar(nb[:, c], mx[:, c], -XSCALE, None, ALU.mult).then_inc(nb_ok, 1)

            def normalise(n, k):
                c = slice(4 * k, 4 * k + 4)
                dve.wait_ge(exp_ok, n * 4 + k + 1)
                dve.reciprocal(rc[:, c], sm[:, c]).then_inc(rc_ok, 1)
                dve.wait_ge(rc_ok, n * 4 + k + 1)
                dve.tensor_tensor(E[:, c, :], E[:, c, :], bcast(rc[:, c], 2, KEYS), ALU.mult).then_inc(e_ok, 1)

            def residual(n, u):
                dve.wait_ge(proj_ok, n + 1)
                dve.tensor_tensor(tile_of(n), tile_of(n), p_o[u][:, 0:D], ALU.add).then_inc(x_ok, 1)

            dve.wait_ge(C["rope"].made, 8)

            def early(n, u):
                norm_a(0, 0)
                norm_b(0, 0)
                low(0, 0, 0)
                norm_a(1, 1)
                norm_b(1, 1)
                for i in range(4):
                    rope(0, i)
                    if i == 0:
                        low(1, 1, 1)
                mean_square(0, 0)
                rope(0, 4)
                rope(0, 5)
                mean_square(0, 1)
                for i in range(6):
                    scale(0, i)

            def mixed(n, u, n1, u1):
                rope(n1, 0)
                rope(n1, 1)
                maxes(n, 0)
                rope(n1, 2)
                maxes(n, 1)
                normalise(n, 0)
                rope(n1, 3)
                mean_square(n1, 0)
                normalise(n, 1)
                if there(n - 1):
                    residual(n - 1, 1 - u)
                rope(n1, 4)
                if there(n + 2):
                    norm_a(n + 2, u)
                maxes(n, 2)
                scale(n1, 0)
                maxes(n, 3)
                normalise(n, 2)
                rope(n1, 5)
                mean_square(n1, 1)
                normalise(n, 3)
                scale(n1, 1)
                if there(n + 2):
                    norm_b(n + 2, u)
                for i in range(2, 6):
                    scale(n1, i)
                if there(n + 2):
                    low(n + 2, u, turns(n, u)[1](T_H))

            def late(n, u):
                maxes(n, 0)
                maxes(n, 1)
                residual(n - 1, 1 - u)
                normalise(n, 0)
                normalise(n, 1)
                maxes(n, 2)
                maxes(n, 3)
                normalise(n, 2)
                normalise(n, 3)
                residual(n, u)

            skewed(dve, early, mixed, late)


SQI = {0: 0, 1: 1, 2: 2, 3: 3, 4: 4, 6: 5}
RING = (0, 1, 2, 3, 4, 6)
RMS = (slice(0, XH), slice(XH, XH + 2 * KVH))


E1, K1, I1 = 64, 8, 64
NPAIR = E1 // 2 + 1
WROWS = 2 * NPAIR
CH = 512
NCH = B * S // CH


def moe_dense(nc, C, a, out):
    x, ident, neghalf = C["x"], C["ident"], C["neghalf"]
    m = Store(nc)
    wt_dram = nc.dram_tensor("wt_dram", [WROWS, B * S], F32, kind="Internal").ap()
    with m.stack:
        hs = m.sb("m1hs", [P, 2, DC, B * S], F16)
        NR = 3
        GU = DC * 2 * P
        raw = m.sb("m1raw", [P, NR, GU + D])
        ws = m.sb("m1ws", [P, NR, 2, GU + D], F16)
        w_in = [m.sem(f"m1_w_in{u}") for u in range(NR)]
        high_ok, prep_ok = m.sems("m1", "high_ok prep_ok")

        def load_raw(sp, p, u):
            sp.dma_start(raw[:, u, :], a["m1_w"][bass.ds(p, 1), :, :].rearrange("a p n -> p (a n)")).then_inc(w_in[u], 16)

        def low_part(pool, p, u):
            pool.wait_ge(high_ok, p + 1)
            pool.tensor_tensor(ws[:, u, 1, :], raw[:, u, :], ws[:, u, 0, :], ALU.subtract).then_inc(prep_ok, 1)

        def scaled_raw(act, u):
            act.activation(raw[:, u, :], raw[:, u, :], ACT.Copy, scale=W_UP).then_inc(high_ok, 1)

        r = Store(nc)
        with r.stack:
            gate = r.sb("m1gate", [P, DC, E1 + 1])
            st = r.sb("m1st", [P, NT, 6])
            mv = r.sb("m1mv", [P, NT, 2])
            ve = r.sb("m1ve", [P, NT])
            rstd = r.sb("m1rstd", [P, NT])
            hn = r.sb("m1hn", [P, 2, D])
            hT = r.sb("m1hT", [P, 2, DC, P])
            lg = r.sb("m1lg", [P, NT, E1 + 1])
            top = r.sb("m1top", [P, NT, 8])
            rest = r.sb("m1rest", [P, NT, E1])
            df = r.sb("m1df", [P, NT, E1])
            ex = r.sb("m1ex", [P, NT, E1])
            sg1 = r.sb("m1sg1", [P, NT, 1])
            sm = r.sb("m1sm", [P, 2, NT])
            rc = r.sb("m1rc", [P, 2, NT])
            W = r.sb("m1W", [P, NT, WROWS])
            WT = r.sb("m1WT", [WROWS, B * S])
            p_t = [r.ps(f"m1pt{i}", [P, DC, P]) for i in range(2)]
            p_l = [r.ps(f"m1pl{i}", [P, 512]) for i in range(2)]
            p_w = [r.ps(f"m1pw{i}", [P, CH]) for i in range(NCH)]
            (loaded, stat_ok, var_ok, rstd_ok, hn_ok, t_ok, hT_ok, hi_ok, lo_ok, l_ok, lg_ok, top_ok, ex_ok,
             step, W_ok, w_ok, WT_ok, stored) = r.sems(
                "m1", "loaded stat_ok var_ok rstd_ok hn_ok t_ok hT_ok hi_ok lo_ok l_ok lg_ok top_ok ex_ok"
                      " step W_ok w_ok WT_ok stored")
            with nc.Block() as block:
                @block.sync
                def _(sp):
                    moved(sp, loaded, [(gate[:, :, :], a["m1_gate"])])
                    for p in range(NR):
                        load_raw(sp, p, p)
                    for q in range(NCH):
                        sp.wait_ge(WT_ok, q + 1)
                        sp.dma_start(wt_dram[:, CH * q:CH * q + CH], WT[:, CH * q:CH * q + CH]).then_inc(stored, 16)
                    sp.wait_ge(stored, 16 * NCH)

                @block.gpsimd
                def _(pool):
                    pool.wait_ge(var_ok, 1)
                    pool.tensor_tensor(rstd[:, :], ve[:, :], neghalf[:, 0:1].to_broadcast([P, NT]), ALU.pow).then_inc(rstd_ok, 1)
                    pool.memset(W[:, :, E1 + 1:WROWS], 0.0).then_inc(W_ok, 1)
                    for p in range(NR):
                        low_part(pool, p, p)

                @block.scalar
                def _(act):
                    def inputs(n, u):
                        act.wait_ge(t_ok, n + 1)
                        act.activation(hT[:, u, :, :], p_t[u][:, :, :], ACT.Copy).then_inc(hT_ok, 1)
                        act.activation(hs[:, 0, :, bass.ds(n * P, P)], p_t[u][:, :, :], ACT.Copy, scale=H_UP).then_inc(hi_ok, 1)

                    def logits(n, u):
                        act.wait_ge(l_ok, n + 1)
                        act.activation(lg[:, bass.ds(n, 1), :].rearrange("p a e -> p (a e)"), p_l[u][:, 0:E1 + 1], ACT.Copy).then_inc(lg_ok, 1)

                    def mixed(n, u, n1, u1):
                        inputs(n1, u1)
                        logits(n, u)
                    skewed(act, inputs, mixed, logits)
                    act.wait_ge(lg_ok, NT)
                    act.activation(sg1[:, :, :], lg[:, :, E1:E1 + 1], ACT.Exp, scale=-1.0).then_inc(ex_ok, 1)
                    act.wait_ge(top_ok, NT + 1)
                    act.activation(ex[:, :, :], df[:, :, :], ACT.Exp).then_inc(ex_ok, 1)
                    for p in range(NR):
                        act.wait_ge(w_in[p], 16)
                        act.activation(ws[:, p, 0, :], raw[:, p, :], ACT.Copy, scale=W_UP)
                        scaled_raw(act, p)
                    for q in range(NCH):
                        act.wait_ge(w_ok, q + 1)
                        act.activation(WT[:, CH * q:CH * q + CH], p_w[q][0:WROWS, :], ACT.Copy).then_inc(WT_ok, 1)

                @block.tensor
                def _(pe):
                    def turn(n, u):
                        pe.wait_ge(hn_ok, n + 1)
                        if type(n) is not int or n >= 2:
                            pe.wait_ge(lo_ok, n - 1)
                        for c in range(DC):
                            ins = pe.transpose(p_t[u][:, c, :], hn[:, u, P * c:P * c + P], ident[:, :])
                        ins.then_inc(t_ok, 1)

                    def route(n, u):
                        pe.wait_ge(hT_ok, n + 1)
                        if type(n) is not int or n >= 1:
                            pe.wait_ge(lg_ok, n)
                        for c in range(DC):
                            ins = pe.matmul(p_l[u][:, 0:E1 + 1], hT[:, u, c, :], gate[:, c, :], start=(c == 0), stop=(c == DC - 1))
                        ins.then_inc(l_ok, 1)

                    pe.wait_ge(loaded, 16)

                    def mixed(n, u, n1, u1):
                        turn(n1, u1)
                        route(n, u)
                    skewed(pe, turn, mixed, route)
                    pe.wait_ge(W_ok, 3)
                    for n in range(NT):
                        o = P * n % CH
                        ins = pe.transpose(p_w[P * n // CH][0:WROWS, o:o + P], W[:, n, :], ident[:, :])
                        if o + P == CH:
                            ins.then_inc(w_ok, 1)

                @block.vector
                def _(dve):
                    for n in range(NT):
                        dve.bn_stats(st[:, n, :], x[:, n, :])
                    dve.drain()
                    for n in range(NT):
                        ins = dve.bn_aggr(mv[:, n, :], st[:, n, :])
                    ins.then_inc(stat_ok, 1)
                    dve.wait_ge(stat_ok, 1)
                    dve.tensor_scalar(ve[:, :], mv[:, :, 1], 1e-5, None, ALU.add).then_inc(var_ok, 1)
                    dve.wait_ge(rstd_ok, 1)

                    def norm(n, u):
                        if type(n) is not int or n >= 2:
                            dve.wait_ge(t_ok, n - 1)
                        dve.tensor_scalar(hn[:, u, :], x[:, bass.ds(n, 1), :].rearrange("p a d -> p (a d)"),
                                          mv[:, bass.ds(n, 1), 0:1].rearrange("p a b -> p (a b)"), rstd[:, bass.ds(n, 1)],
                                          ALU.subtract, ALU.mult).then_inc(hn_ok, 1)

                    def low(n, u):
                        dve.wait_ge(hi_ok, n + 1)
                        cols = bass.ds(n * P, P)
                        dve.scalar_tensor_tensor(hs[:, 1, :, cols], p_t[u][:, :, :], H_UP, hs[:, 0, :, cols],
                                                 ALU.mult, ALU.subtract).then_inc(lo_ok, 1)

                    def mixed(n, u, n1, u1):
                        norm(n1, u1)
                        low(n, u)
                    skewed(dve, norm, mixed, low)
                    for n in range(NT):
                        dve.wait_ge(lg_ok, n + 1)
                        dve.max(top[:, n, :], lg[:, n, 0:E1]).then_inc(top_ok, 1)
                    dve.wait_ge(top_ok, NT)
                    dve.tensor_tensor(df[:, :, :], lg[:, :, 0:E1], top[:, :, 0:1].to_broadcast([P, NT, E1]), ALU.subtract).then_inc(top_ok, 1)
                    for n in range(NT):
                        dve.match_replace(rest[:, n, :], top[:, n, :], lg[:, n, 0:E1], -3.0e38).then_inc(step, 1)
                    dve.wait_ge(step, NT)
                    dve.tensor_tensor(rest[:, :, :], rest[:, :, :], lg[:, :, 0:E1], ALU.not_equal).then_inc(step, 1)
                    dve.wait_ge(ex_ok, 1)
                    dve.tensor_scalar(sm[:, 1, :], sg1[:, :, 0], 1.0, None, ALU.add)
                    dve.wait_ge(step, NT + 1)
                    dve.wait_ge(ex_ok, 2)
                    dve.tensor_tensor(ex[:, :, :], ex[:, :, :], rest[:, :, :], ALU.mult).then_inc(step, 1)
                    dve.wait_ge(step, NT + 2)
                    dve.tensor_reduce(sm[:, 0, :], ex[:, :, :], AX.X, ALU.add).then_inc(step, 1)
                    dve.wait_ge(step, NT + 3)
                    dve.reciprocal(rc[:, :, :], sm[:, :, :]).then_inc(step, 1)
                    dve.wait_ge(step, NT + 4)
                    dve.tensor_tensor(W[:, :, 0:E1], ex[:, :, :], bcast(rc[:, 0, :], 2, E1), ALU.mult).then_inc(W_ok, 1)
                    dve.tensor_copy(W[:, :, E1:E1 + 1], bcast(rc[:, 1, :], 2, 1)).then_inc(W_ok, 1)

        yT = m.sb("m1yT", [P, DC, B * S])
        e = Store(nc)
        with e.stack:
            Wb = e.sb("m1Wb", [P, NR, B * S])
            sg = e.sb("m1sg", [P, 2, CH])
            ac = e.sb("m1ac", [P, 2, CH])
            ap = e.sb("m1ap", [P, 2, 2, CH], F16)
            p_g = [e.ps(f"m1pg{i}", [P, CH]) for i in range(2)]
            p_u = [e.ps(f"m1pu{i}", [P, CH]) for i in range(2)]
            turns_in = p_g + p_u
            p_y = [[e.ps(f"m1py{c}{q}", [P, CH]) for q in range(NCH)] for c in range(DC)]
            (g_ok, u_ok, silu_ok, sw_ok, act_ok, ah_ok, al_ok, y_ok, yT_ok, turned, x_ok, out_ok) = e.sems(
                "e1", "g_ok u_ok silu_ok sw_ok act_ok ah_ok al_ok y_ok yT_ok turned x_ok out_ok")
            b_in = [e.sem(f"e1_b_in{u}") for u in range(NR)]

            def part(ap_, u, s, c, which):
                return ap_[:, u, s, P * (2 * c + which):P * (2 * c + which) + P]

            def over_pairs(eng, body):
                body(0, 0, 0)
                with eng.Fori(0, (NPAIR - 6) // NR) as i:
                    body(i * NR + 1, 1, i)
                    body(i * NR + 2, 2, i)
                    body(i * NR + 3, 0, i + 1)
                for p in range(NPAIR - 5, NPAIR):
                    body(p, p % NR, p // NR)

            def is_pair(p):
                return type(p) is not int or 0 <= p < NPAIR

            with nc.Block() as block:
                @block.sync
                def _(sp):
                    def load_b(p, u):
                        for h in range(2):
                            sp.dma_start(Wb[64 * h:64 * h + 64, u, :],
                                         wt_dram[bass.ds(p * 2 + h, 1), :].to_broadcast([64, B * S])).then_inc(b_in[u], 16)
                    for p in range(NR):
                        load_b(p, p)

                    def pair(p, u, r):
                        if is_pair(p + NR):
                            sp.wait_ge(prep_ok, p + 1)
                            load_raw(sp, p + NR, u)
                            sp.wait_ge(sw_ok, p * 2 + 2)
                            load_b(p + NR, u)
                    over_pairs(sp, pair)
                    rows = out.rearrange("(n p) d -> p n d", p=P)
                    for n in range(NT):
                        sp.wait_ge(x_ok, n + 1)
                        sp.dma_start(rows[:, n, :], x[:, n, :]).then_inc(out_ok, 16)
                    sp.wait_ge(out_ok, 16 * NT)

                @block.gpsimd
                def _(pool):
                    def pair(p, u, r):
                        if is_pair(p + 2) and not (type(p) is int and p == 0):
                            low_part(pool, p + 2, (u + 2) % NR)
                    over_pairs(pool, pair)

                @block.scalar
                def _(act):
                    def silu(j, q):
                        act.wait_ge(g_ok, j + 1)
                        act.activation(sg[:, q, :], p_g[q][:, :], ACT.Silu, scale=1.0 / (H_UP * W_UP)).then_inc(silu_ok, 1)

                    def ahigh(j, q):
                        act.wait_ge(act_ok, j + 1)
                        act.activation(ap[:, q, 0, :], ac[:, q, :], ACT.Copy).then_inc(ah_ok, 1)

                    silu(0, 0)

                    def pair(p, u, r):
                        prep = is_pair(p + 2) and not (type(p) is int and p == 0)
                        u2 = (u + 2) % NR
                        ahigh(p * 2, 0)
                        if prep:
                            act.wait_ge(w_in[u2], (r + (u > 0)) * 16 + 16)
                            act.wait_ge(y_ok, p * 2)
                            act.activation(ws[:, u2, 0, :], raw[:, u2, :], ACT.Copy, scale=W_UP)
                        silu(p * 2 + 1, 1)
                        ahigh(p * 2 + 1, 1)
                        if prep:
                            scaled_raw(act, u2)
                        if is_pair(p + 1):
                            silu(p * 2 + 2, 0)
                    over_pairs(act, pair)
                    for q in range(NCH):
                        act.wait_ge(y_ok, 2 * NPAIR - 1 + q)
                        for c in range(DC):
                            act.activation(yT[:, c, CH * q:CH * q + CH], p_y[c][q][:, :], ACT.Copy, scale=1.0 / W_UP).then_inc(yT_ok, 1)

                @block.tensor
                def _(pe):
                    def hidden(p, u, q):
                        j = p * 2 + q
                        pe.wait_ge(prep_ok, p + 1)
                        if not (type(p) is int and p == 0):
                            pe.wait_ge(act_ok, j - 1)
                        for which, bank, ok in ((0, p_g[q], g_ok), (1, p_u[q], u_ok)):
                            k = 0
                            for c in range(DC):
                                for sw, sh in PASSES:
                                    ins = pe.matmul(bank[:, :], part(ws, u, sw, c, which), hs[:, sh, c, CH * q:CH * q + CH],
                                                    start=(k == 0), stop=(k == 5))
                                    k += 1
                            ins.then_inc(ok, 1)

                    def down(p, u, q):
                        j = p * 2 + q
                        first, last = (type(p) is int and p == k for k in (0, NPAIR - 1))
                        pe.wait_ge(al_ok, j + 1)
                        for c in range(DC):
                            for k, (sw, sa) in enumerate(PASSES):
                                ins = pe.matmul(p_y[c][q][:, :], ws[:, u, sw, GU + P * c:GU + P * c + P], ap[:, q, sa, :],
                                                start=(first and k == 0), stop=(last and k == 2), skip_group_check=True)
                        ins.then_inc(y_ok, 1)

                    hidden(0, 0, 0)

                    def pair(p, u, r):
                        hidden(p, u, 1)
                        down(p, u, 0)
                        if is_pair(p + 1):
                            hidden(p + 1, (u + 1) % NR, 0)
                        down(p, u, 1)
                    over_pairs(pe, pair)
                    pe.wait_ge(act_ok, 2 * NPAIR)
                    for n in range(NT):
                        pe.wait_ge(yT_ok, DC * (P * n // CH + 1))
                        if n >= 4:
                            pe.wait_ge(x_ok, n - 3)
                        for c in range(DC):
                            ins = pe.transpose(turns_in[n % 4][:, P * c:P * c + P], yT[:, c, P * n:P * n + P], ident[:, :])
                        ins.then_inc(turned, 1)

                @block.vector
                def _(dve):
                    def weigh(p, u, r, q):
                        dve.wait_ge(b_in[u], r * 32 + 32)
                        dve.wait_ge(silu_ok, p * 2 + q + 1)
                        dve.tensor_tensor(sg[:, q, :], sg[:, q, :], Wb[:, u, CH * q:CH * q + CH], ALU.mult).then_inc(sw_ok, 1)

                    def times_up(p, q):
                        j = p * 2 + q
                        dve.wait_ge(sw_ok, j + 1)
                        dve.wait_ge(u_ok, j + 1)
                        dve.scalar_tensor_tensor(ac[:, q, :], p_u[q][:, :], 1.0 / (H_UP * W_UP), sg[:, q, :],
                                                 ALU.mult, ALU.mult).then_inc(act_ok, 1)

                    def alow(p, q):
                        j = p * 2 + q
                        dve.wait_ge(ah_ok, j + 1)
                        dve.tensor_tensor(ap[:, q, 1, :], ac[:, q, :], ap[:, q, 0, :], ALU.subtract).then_inc(al_ok, 1)

                    weigh(0, 0, 0, 0)
                    times_up(0, 0)

                    def pair(p, u, r):
                        alow(p, 0)
                        weigh(p, u, r, 1)
                        times_up(p, 1)
                        alow(p, 1)
                        if is_pair(p + 1):
                            weigh(p + 1, (u + 1) % NR, r + (u == NR - 1), 0)
                            times_up(p + 1, 0)
                    over_pairs(dve, pair)
                    for n in range(NT):
                        dve.wait_ge(turned, n + 1)
                        dve.tensor_tensor(x[:, n, :], x[:, n, :], turns_in[n % 4][:, 0:D], ALU.add).then_inc(x_ok, 1)


E0, K0, I0 = 32, 4, 128
CAP = 2 * B * S * K0 // E0
SLOTS = E0 * CAP
ST = CAP // P
DROPPED = 2.0 ** 20


class SlotRows:

    def __init__(self, g, C, rope):
        self.C, self.rope = C, rope
        self.w4 = g.sb("w4", [P, NT, K0])
        self.slot = g.sb("slot", [P, 2, NT, K0], U32)
        self.rows = g.sb("rows", [P, 2, K0, D])
        self.fetched = [g.sem(f"fetched{u}") for u in range(2)]
        self.weighed, self.folded, self.added = (g.sem(n) for n in ("weighed", "folded", "added"))

    def fetch(self, pool, n):
        if n >= 2:
            pool.wait_ge(self.added, n - 1)
        for k in range(K0):
            pool.indirect_dma_start(self.rows[:, n % 2, k, :], None, self.C["slots_out"],
                                    bass.IndirectOffsetOnAxis(ap=self.slot[:, 0, n, k:k + 1], axis=0),
                                    bounds_check=SLOTS - 1, oob_is_err=False).then_inc(self.fetched[n % 2], 16)

    def weigh(self, act, n, u):
        act.wait_ge(self.fetched[u], (n - u) * 8 * K0 + 16 * K0)
        for k in range(K0):
            w = self.w4[:, bass.ds(n, 1), k:k + 1].rearrange("p a k -> p (a k)")
            ins = act.activation(self.rows[:, u, k, :], self.rows[:, u, k, :], ACT.Copy, scale=w)
        ins.then_inc(self.weighed, 1)

    def fold(self, pool, n):
        r = self.rows[:, n % 2, :, :]
        pool.wait_ge(self.weighed, n + 1)
        pool.tensor_tensor(r[:, 0:2, :], r[:, 0:2, :], r[:, 2:4, :], ALU.add).then_inc(self.folded, 1)
        pool.wait_ge(self.folded, 2 * n + 1)
        pool.tensor_tensor(r[:, 0, :], r[:, 0, :], r[:, 1, :], ALU.add).then_inc(self.folded, 1)
        pool.wait_ge(self.folded, 2 * n + 2)

    def add(self, dve, n, u):
        dve.wait_ge(self.folded, n * 2 + 2)
        xt = self.C["x"][:, bass.ds(n, 1), :].rearrange("p a d -> p (a d)")
        dve.tensor_tensor(xt, xt, self.rows[:, u, 0, :], ALU.add).then_inc(self.added, 1)
        dve.drain()


def moe_slots(nc, C, a, rows):
    x, ident, neghalf = C["x"], C["ident"], C["neghalf"]
    slots_in, slots_out, rope = C["slots_in"], C["slots_out"], rows.rope
    w4, slot = rows.w4, rows.slot
    m = Store(nc)
    with m.stack:
        hs = m.sb("m0hs", [P, 2, DC, B * S], F16)
        h2 = m.sb("m0h2", [P, NT, D])
        scattered = m.sem("m0_scattered")
        GU = DC * 2 * P
        rg = m.sb("m0rg", [P, 2, GU])
        rd = m.sb("m0rd", [P, 2, D])
        wg = m.sb("m0wg", [P, 2, 2, GU], F16)
        wd = m.sb("m0wd", [P, 2, 2, D], F16)
        rs_ = m.sb("m0rs", [P, GU + D])
        ws = m.sb("m0ws", [P, 2, GU + D], F16)
        gin = [m.sem(f"m0_gin{u}") for u in range(2)]
        din = [m.sem(f"m0_din{u}") for u in range(2)]
        sin, sh_ok, sl_ok, gh_ok, gl_ok, dh_ok, dl_ok = m.sems("m0", "sin sh_ok sl_ok gh_ok gl_ok dh_ok dl_ok")

        def load_g(sp, k, u):
            if type(k) is not int or k >= 2:
                sp.wait_ge(gl_ok, k - 1)
            sp.dma_start(rg[:, u, :], a["m0_wgu"][bass.ds(k, 1), :, :].rearrange("a p n -> p (a n)")).then_inc(gin[u], 16)

        def load_d(sp, k, u):
            if type(k) is not int or k >= 2:
                sp.wait_ge(dl_ok, k - 1)
            sp.dma_start(rd[:, u, :], a["m0_wd"][bass.ds(k, 1), :, :].rearrange("a p n -> p (a n)")).then_inc(din[u], 16)

        def low_g(pool, k, u):
            pool.wait_ge(gh_ok, k + 1)
            pool.tensor_tensor(wg[:, u, 1, :], rg[:, u, :], wg[:, u, 0, :], ALU.subtract).then_inc(gl_ok, 1)

        def low_d(pool, k, u):
            pool.wait_ge(dh_ok, k + 1)
            pool.tensor_tensor(wd[:, u, 1, :], rd[:, u, :], wd[:, u, 0, :], ALU.subtract).then_inc(dl_ok, 1)

        def scatter(pool, n):
            for k in range(K0):
                pool.indirect_dma_start(slots_in, bass.IndirectOffsetOnAxis(ap=slot[:, 1, n, k:k + 1], axis=0),
                                        h2[:, n, :], None, bounds_check=SLOTS - 1, oob_is_err=False).then_inc(scattered, 16)

        r = Store(nc)
        with r.stack:
            HT = NT // 2
            gate = r.sb("m0gate", [P, DC, E0])
            normw = r.sb("m0normw", [P, D])
            eids = r.sb("m0eids", [P, E0])
            before = r.sb("m0before", [P, P])
            ones = r.sb("m0ones", [P, P])
            st = r.sb("m0st", [P, NT, 6])
            mv = r.sb("m0mv", [P, NT, 2])
            ve = r.sb("m0ve", [P, NT])
            rstd = r.sb("m0rstd", [P, NT])
            ms = r.sb("m0ms", [P, NT])
            rr = r.sb("m0rr", [P, NT])
            hn = r.sb("m0hn", [P, NT, D])
            hT = r.sb("m0hT", [P, 2, DC, P])
            lg = r.sb("m0lg", [P, NT, E0])
            top = r.sb("m0top", [P, NT, 8])
            idx = r.sb("m0idx", [P, NT, 8], U32)
            idf = r.sb("m0idf", [P, HT, K0])
            df = r.sb("m0df", [P, NT, K0])
            ex = r.sb("m0ex", [P, NT, K0])
            sm = r.sb("m0sm", [P, 2, HT])
            OH = r.sb("m0OH", [P, HT, K0, E0])
            M = r.sb("m0M", [P, NT, E0])
            Mh = r.sb("m0Mh", [P, E0])
            sv = r.sb("m0sv", [P, 2, HT, E0])
            pk = r.sb("m0pk", [P, 2, HT, K0, E0])
            sf = r.sb("m0sf", [P, 2, HT, K0])
            p_t = [r.ps(f"m0pt{i}", [P, DC, P]) for i in range(2)]
            p_l = [r.ps(f"m0pl{i}", [P, 512]) for i in range(2)]
            p_p = [r.ps(f"m0pp{i}", [P, 512]) for i in range(2)]
            (loaded, const_ok, stat_ok, var_ok, rstd_ok, ms_ok, rr_ok, hn_ok, h2_ok, t_ok, hT_ok, hi_ok, lo_ok,
             l_ok, lg_ok, top_ok, df_ok, ex_ok, step, M_ok, pos_ok, slot_ok) = r.sems(
                "m0", "loaded const_ok stat_ok var_ok rstd_ok ms_ok rr_ok hn_ok h2_ok t_ok hT_ok hi_ok lo_ok"
                      " l_ok lg_ok top_ok df_ok ex_ok step M_ok pos_ok slot_ok")
            with nc.Block() as block:
                @block.sync
                def _(sp):
                    moved(sp, loaded, [(gate[:, :, :], a["m0_gate"]), (normw[:, :], a["m0_normw"].to_broadcast([P, D])),
                                       (eids[:, :], a["eids"].to_broadcast([P, E0])), (before[:, :], a["before"])])
                    sp.dma_start(rs_[:, :], a["m0_ws"]).then_inc(sin, 16)
                    load_g(sp, 0, 0)
                    load_g(sp, 1, 1)
                    load_d(sp, 0, 0)
                    load_d(sp, 1, 1)
                    rope.load(sp)

                @block.gpsimd
                def _(pool):
                    pool.memset(ones[:, :], 1.0).then_inc(const_ok, 1)
                    minus = neghalf[:, 0:1].to_broadcast([P, NT])
                    pool.wait_ge(var_ok, 1)
                    pool.tensor_tensor(rstd[:, :], ve[:, :], minus, ALU.pow).then_inc(rstd_ok, 1)
                    pool.wait_ge(ms_ok, 1)
                    pool.tensor_tensor(rr[:, :], ms[:, :], minus, ALU.pow).then_inc(rr_ok, 1)
                    pool.wait_ge(sh_ok, 1)
                    pool.tensor_tensor(ws[:, 1, :], rs_[:, :], ws[:, 0, :], ALU.subtract).then_inc(sl_ok, 1)
                    low_g(pool, 0, 0)
                    low_g(pool, 1, 1)
                    low_d(pool, 0, 0)
                    pool.wait_ge(C["zero_ok"], 16)
                    pool.wait_ge(slot_ok, 1)
                    for n in range(HT):
                        scatter(pool, n)

                @block.scalar
                def _(act):
                    def inputs(n, u):
                        act.wait_ge(t_ok, n + 1)
                        act.activation(hT[:, u, :, :], p_t[u][:, :, :], ACT.Copy).then_inc(hT_ok, 1)
                        act.activation(hs[:, 0, :, bass.ds(n * P, P)], p_t[u][:, :, :], ACT.Copy, scale=H_UP).then_inc(hi_ok, 1)

                    def logits(n, u):
                        act.wait_ge(l_ok, n + 1)
                        act.activation(lg[:, bass.ds(n, 1), :].rearrange("p a e -> p (a e)"), p_l[u][:, 0:E0], ACT.Copy).then_inc(lg_ok, 1)

                    def high(w, raw, done):
                        act.activation(w, raw, ACT.Copy, scale=W_UP)
                        act.activation(raw, raw, ACT.Copy, scale=W_UP).then_inc(done, 1)

                    for g in range(2):
                        for n in range(HT * g, HT * g + HT):
                            inputs(n, n % 2)
                            if n > HT * g:
                                logits(n - 1, (n - 1) % 2)
                        logits(HT * g + HT - 1, 1)
                        if g == 0:
                            act.wait_ge(sin, 16)
                            high(ws[:, 0, :], rs_[:, :], sh_ok)
                            for u in range(2):
                                act.wait_ge(gin[u], 16)
                                high(wg[:, u, 0, :], rg[:, u, :], gh_ok)
                            act.wait_ge(din[0], 16)
                            high(wd[:, 0, 0, :], rd[:, 0, :], dh_ok)
                        act.wait_ge(df_ok, g + 1)
                        act.activation(ex[:, HT * g:HT * g + HT, :], df[:, HT * g:HT * g + HT, :], ACT.Exp).then_inc(ex_ok, 1)

                @block.tensor
                def _(pe):
                    def turn(n, u):
                        pe.wait_ge(h2_ok, n + 1)
                        if type(n) is not int or n >= 2:
                            pe.wait_ge(lo_ok, n - 1)
                        for c in range(DC):
                            ins = pe.transpose(p_t[u][:, c, :], h2[:, bass.ds(n, 1), P * c:P * c + P].rearrange("p a d -> p (a d)"), ident[:, :])
                        ins.then_inc(t_ok, 1)

                    def route(n, u):
                        pe.wait_ge(hT_ok, n + 1)
                        if n >= 1:
                            pe.wait_ge(lg_ok, n)
                        for c in range(DC):
                            ins = pe.matmul(p_l[u][:, 0:E0], hT[:, u, c, :], gate[:, c, :], start=(c == 0), stop=(c == DC - 1))
                        ins.then_inc(l_ok, 1)

                    def places(g):
                        pe.wait_ge(M_ok, g + 1)
                        out, mine = p_p[g][:, 0:HT * E0], M[:, HT * g:HT * g + HT, :].rearrange("p t e -> p (t e)")
                        ins = pe.matmul(out, before[:, :], mine, start=True, stop=False, skip_group_check=True)
                        for k in range(1, HT):
                            ins = pe.matmul(out[:, E0 * k:], ones[:, :], mine[:, 0:E0 * (HT - k)], start=False,
                                            stop=g == 0 and k == HT - 1, skip_group_check=True)
                        if g:
                            ins = pe.matmul(out.rearrange("p (t e) -> p t e", t=HT), ones[:, :], bcast(Mh[:, :], 1, HT),
                                            start=False, stop=True, skip_group_check=True)
                        ins.then_inc(pos_ok, 1)

                    pe.wait_ge(loaded, 64)
                    pe.wait_ge(const_ok, 1)
                    for g in range(2):
                        turn(HT * g, 0)
                        for n in range(HT * g, HT * g + HT):
                            if n + 1 < HT * g + HT:
                                turn(n + 1, (n + 1) % 2)
                            route(n, n % 2)
                        places(g)

                @block.vector
                def _(dve):
                    for n in range(NT):
                        dve.bn_stats(st[:, n, :], x[:, n, :])
                    dve.drain()
                    for n in range(NT):
                        ins = dve.bn_aggr(mv[:, n, :], st[:, n, :])
                    ins.then_inc(stat_ok, 1)
                    dve.wait_ge(stat_ok, 1)
                    dve.tensor_scalar(ve[:, :], mv[:, :, 1], 1e-5, None, ALU.add).then_inc(var_ok, 1)
                    dve.wait_ge(rstd_ok, 1)
                    dve.tensor_tensor(ms[:, :], mv[:, :, 1], rstd[:, :], ALU.mult).then_inc(step, 1)
                    dve.wait_ge(step, 1)
                    dve.tensor_tensor(ms[:, :], ms[:, :], rstd[:, :], ALU.mult).then_inc(step, 1)
                    dve.wait_ge(step, 2)
                    dve.tensor_scalar(ms[:, :], ms[:, :], 1e-6, None, ALU.add).then_inc(ms_ok, 1)

                    def norm(n, u):
                        dve.tensor_scalar(hn[:, bass.ds(n, 1), :].rearrange("p a d -> p (a d)"),
                                          x[:, bass.ds(n, 1), :].rearrange("p a d -> p (a d)"),
                                          mv[:, bass.ds(n, 1), 0:1].rearrange("p a b -> p (a b)"), rstd[:, bass.ds(n, 1)],
                                          ALU.subtract, ALU.mult).then_inc(hn_ok, 1)
                        dve.wait_ge(rr_ok, 1)
                        dve.wait_ge(hn_ok, n + 1)
                        dve.scalar_tensor_tensor(h2[:, bass.ds(n, 1), :].rearrange("p a d -> p (a d)"),
                                                 hn[:, bass.ds(n, 1), :].rearrange("p a d -> p (a d)"),
                                                 rr[:, bass.ds(n, 1)], normw[:, :], ALU.mult, ALU.mult).then_inc(h2_ok, 1)

                    def low(n, u):
                        dve.wait_ge(hi_ok, n + 1)
                        cols = bass.ds(n * P, P)
                        dve.scalar_tensor_tensor(hs[:, 1, :, cols], p_t[u][:, :, :], H_UP, hs[:, 0, :, cols],
                                                 ALU.mult, ALU.subtract).then_inc(lo_ok, 1)

                    done = [2]

                    def then(ins):
                        done[0] += 1
                        ins.then_inc(step, 1)
                        dve.wait_ge(step, done[0])

                    def choose(g):
                        tiles = slice(HT * g, HT * g + HT)
                        for n in range(HT * g, HT * g + HT):
                            dve.wait_ge(lg_ok, n + 1)
                            ins = dve.max(top[:, n, :], lg[:, n, :])
                        ins.then_inc(top_ok, 1)
                        dve.wait_ge(top_ok, g * 2 + 1)
                        dve.tensor_tensor(df[:, tiles, :], top[:, tiles, 0:K0], top[:, tiles, 0:1].to_broadcast([P, HT, K0]),
                                          ALU.subtract).then_inc(df_ok, 1)
                        for n in range(HT * g, HT * g + HT):
                            ins = dve.max_index(idx[:, n, :], top[:, n, :], lg[:, n, :])
                        ins.then_inc(top_ok, 1)
                        dve.wait_ge(top_ok, g * 2 + 2)
                        then(dve.tensor_copy(idf[:, :, :], idx[:, tiles, 0:K0]))
                        then(dve.tensor_tensor(OH[:, :, :, :], bcast(bcast(eids[:, :], 1, K0), 1, HT), bcast(idf[:, :, :], 3, E0), ALU.is_equal))
                        ins = dve.tensor_reduce(M[:, tiles, :], OH[:, :, :, :].rearrange("p t k e -> p t e k"), AX.X, ALU.add)
                        if g == 0:
                            then(ins)
                            ins = dve.tensor_reduce(Mh[:, :], M[:, tiles, :].rearrange("p t e -> p e t"), AX.X, ALU.add)
                        ins.then_inc(M_ok, 1)
                        dve.wait_ge(ex_ok, g + 1)
                        then(dve.tensor_reduce(sm[:, 0, :], ex[:, tiles, :], AX.X, ALU.add))
                        then(dve.reciprocal(sm[:, 1, :], sm[:, 0, :]))
                        dve.tensor_tensor(w4[:, tiles, :], ex[:, tiles, :], bcast(sm[:, 1, :], 2, K0), ALU.mult)
                        if g == 1:
                            dve.tensor_tensor(x[:, :, :], x[:, :, :], hn[:, :, :], ALU.add)
                        dve.wait_ge(pos_ok, g + 1)
                        place = p_p[g][:, 0:HT * E0].rearrange("p (t e) -> p t e", t=HT)
                        dve.tensor_scalar(sv[:, 0, :, :], place, CAP - 1.0, None, ALU.min)
                        then(dve.tensor_scalar(sv[:, 1, :, :], place, float(CAP), DROPPED, ALU.is_ge, ALU.mult))
                        then(dve.scalar_tensor_tensor(sv[:, 0, :, :], bcast(eids[:, :], 1, HT), float(CAP), sv[:, 0, :, :], ALU.mult, ALU.add))
                        then(dve.tensor_tensor(sv[:, 1, :, :], sv[:, 1, :, :], sv[:, 0, :, :], ALU.add))
                        for j in range(2):
                            ins = dve.tensor_tensor(pk[:, j, :, :, :], OH[:, :, :, :], bcast(sv[:, j, :, :], 2, K0), ALU.mult)
                        then(ins)
                        for j in range(2):
                            ins = dve.tensor_reduce(sf[:, j, :, :], pk[:, j, :, :, :], AX.X, ALU.add)
                        then(ins)
                        dve.tensor_copy(slot[:, :, tiles, :], sf[:, :, :, :]).then_inc(slot_ok, 1)

                    dve.wait_ge(loaded, 64)

                    for g in range(2):
                        for n in range(HT * g, HT * g + HT):
                            norm(n, n % 2)
                            if n > HT * g:
                                low(n - 1, (n - 1) % 2)
                        low(HT * g + HT - 1, 1)
                        choose(g)

        e = Store(nc)
        with e.stack:
            xg = e.sb("m0xg", [P, 2, ST, D])
            xs = e.sb("m0xs", [P, 2, 2, DC, CAP], F16)
            sg = e.sb("m0sg", [P, 2, CAP])
            ac = e.sb("m0ac", [P, 2, CAP])
            ap = e.sb("m0ap", [P, 2, 2, CAP], F16)
            yo = e.sb("m0yo", [P, 2, ST, D])
            ssg = e.sb("m0ssg", [P, 2, CH])
            sac = e.sb("m0sac", [P, 2, CH])
            sap = e.sb("m0sap", [P, 2, 2, CH], F16)
            p_x = [e.ps(f"m0px{i}", [P, DC, CAP]) for i in range(2)]
            p_h = [e.ps(f"m0ph{i}", [P, 2, CAP]) for i in range(2)]
            p_y = [e.ps(f"m0py{i}", [P, ST, D]) for i in range(2)]
            p_s = [e.ps(f"m0ps{i}", [P, CH]) for i in range(2)]
            xin = [e.sem(f"e0_xin{u}") for u in range(2)]
            stored = [e.sem(f"e0_stored{u}") for u in range(2)]
            (su_ok, ssilu_ok, sact_ok, sah_ok, sal_ok, sy_ok, sx_ok,
             xt_ok, xh_ok, xl_ok, gu_ok, silu_ok, act_ok, ah_ok, al_ok, y_ok, yo_ok) = e.sems(
                "e0", "su_ok ssilu_ok sact_ok sah_ok sal_ok sy_ok sx_ok"
                      " xt_ok xh_ok xl_ok gu_ok silu_ok act_ok ah_ok al_ok y_ok yo_ok")

            def periods(eng, body):
                for k in range(3):
                    body(k, k % 2)
                with eng.Fori(0, (E0 - 6) // 2) as i:
                    body(i * 2 + 3, 1)
                    body(i * 2 + 4, 0)
                for k in range(E0 - 3, E0):
                    body(k, k % 2)

            def has(k):
                return type(k) is not int or 0 <= k < E0

            with nc.Block() as block:
                @block.sync
                def _(sp):
                    def load_x(k, u):
                        if type(k) is not int or k >= 2:
                            sp.wait_ge(xt_ok, k - 1)
                        sp.dma_start(xg[:, u, :, :], slots_in[bass.ds(k * CAP, CAP), :].rearrange("(s p) d -> p s d", p=P)).then_inc(xin[u], 16)

                    def store(k, u):
                        sp.wait_ge(yo_ok, k + 1)
                        sp.dma_start(slots_out[bass.ds(k * CAP, CAP), :].rearrange("(s p) d -> p s d", p=P), yo[:, u, :, :]).then_inc(stored[u], 16)

                    sp.wait_ge(scattered, 16 * NT * K0)
                    load_x(0, 0)
                    load_x(1, 1)
                    load_x(2, 0)
                    load_g(sp, 2, 0)
                    load_x(3, 1)
                    load_g(sp, 3, 1)
                    load_d(sp, 2, 0)

                    def period(k, u):
                        if type(k) is not int or k >= 1:
                            if has(k + 3):
                                load_x(k + 3, 1 - u)
                                load_g(sp, k + 3, 1 - u)
                            if has(k + 2):
                                load_d(sp, k + 2, u)
                            store(k - 1, 1 - u)
                    periods(sp, period)
                    store(E0 - 1, 1)
                    for u in range(2):
                        sp.wait_ge(stored[u], 16 * E0 // 2)

                @block.gpsimd
                def _(pool):
                    for n in range(NT // 2, NT):
                        scatter(pool, n)

                    def period(k, u):
                        if has(k + 2):
                            low_g(pool, k + 2, u)
                        if has(k + 1):
                            low_d(pool, k + 1, 1 - u)
                    periods(pool, period)
                    for u in range(2):
                        pool.wait_ge(stored[u], 16 * E0 // 2)
                    rows.fetch(pool, 0)

                @block.scalar
                def _(act):
                    for q in range(NCH):
                        act.wait_ge(su_ok, q + 1)
                        act.activation(ssg[:, q, :], p_s[0][:, :], ACT.Silu, scale=1.0 / (H_UP * W_UP)).then_inc(ssilu_ok, 1)
                        act.wait_ge(sact_ok, q + 1)
                        act.activation(sap[:, q, 0, :], sac[:, q, :], ACT.Copy).then_inc(sah_ok, 1)

                    def x_high(k, u):
                        act.wait_ge(xt_ok, k + 1)
                        act.activation(xs[:, u, 0, :, :], p_x[u][:, :, :], ACT.Copy, scale=H_UP).then_inc(xh_ok, 1)

                    def silu(k, u):
                        act.wait_ge(gu_ok, k + 1)
                        act.activation(sg[:, u, :], p_h[u][:, 0, :], ACT.Silu, scale=1.0 / (H_UP * W_UP)).then_inc(silu_ok, 1)

                    def a_high(k, u):
                        act.wait_ge(act_ok, k + 1)
                        act.activation(ap[:, u, 0, :], ac[:, u, :], ACT.Copy).then_inc(ah_ok, 1)

                    def y_out(k, u):
                        act.wait_ge(y_ok, k + 1)
                        if type(k) is not int or k >= 2:
                            act.wait_ge(stored[u], (k - u) * 8)
                        act.activation(yo[:, u, :, :], p_y[u][:, :, :], ACT.Copy, scale=1.0 / W_UP).then_inc(yo_ok, 1)

                    x_high(0, 0)
                    x_high(1, 1)

                    def period(k, u):
                        silu(k, u)
                        if has(k + 2):
                            x_high(k + 2, u)
                        a_high(k, u)
                        if has(k - 1):
                            y_out(k - 1, 1 - u)
                    periods(act, period)
                    y_out(E0 - 1, 1)
                    rope.sines(act)

                @block.tensor
                def _(pe):
                    pe.wait_ge(sl_ok, 1)
                    for q in range(NCH):
                        if q >= 1:
                            pe.wait_ge(sact_ok, q)
                        for which in range(2):
                            k = 0
                            for c in range(DC):
                                for sw, sh in PASSES:
                                    ins = pe.matmul(p_s[which][:, :], ws[:, sw, P * (2 * c + which):P * (2 * c + which) + P],
                                                    hs[:, sh, c, CH * q:CH * q + CH], start=(k == 0), stop=(k == 5))
                                    k += 1
                        ins.then_inc(su_ok, 1)
                    for n in range(NT):
                        q, o = n * P // CH, n * P % CH
                        pe.wait_ge(sal_ok, q + 1)
                        if n >= 2:
                            pe.wait_ge(sx_ok, n - 1)
                        for k, (sw, sa) in enumerate(PASSES):
                            ins = pe.matmul(p_y[n % 2][:, 0, :], sap[:, q, sa, o:o + P], ws[:, sw, GU:GU + D],
                                            start=(k == 0), stop=(k == 2))
                        ins.then_inc(sy_ok, 1)

                    def turn(k, u):
                        pe.wait_ge(xin[u], (k - u) * 8 + 16)
                        if type(k) is not int or k >= 2:
                            pe.wait_ge(xl_ok, k - 1)
                        for c in range(DC):
                            for s in range(ST):
                                ins = pe.transpose(p_x[u][:, c, P * s:P * s + P], xg[:, u, s, P * c:P * c + P], ident[:, :])
                        ins.then_inc(xt_ok, 1)

                    def hidden(k, u):
                        pe.wait_ge(xl_ok, k + 1)
                        pe.wait_ge(gl_ok, k + 1)
                        if type(k) is not int or k >= 2:
                            pe.wait_ge(act_ok, k - 1)
                        for which in range(2):
                            i = 0
                            for c in range(DC):
                                for sw, sx in PASSES:
                                    ins = pe.matmul(p_h[u][:, which, :], wg[:, u, sw, P * (2 * c + which):P * (2 * c + which) + P],
                                                    xs[:, u, sx, c, :], start=(i == 0), stop=(i == 5))
                                    i += 1
                        ins.then_inc(gu_ok, 1)

                    def down(k, u):
                        pe.wait_ge(al_ok, k + 1)
                        pe.wait_ge(dl_ok, k + 1)
                        if type(k) is not int or k >= 2:
                            pe.wait_ge(yo_ok, k - 1)
                        elif k < 2:
                            pe.wait_ge(sx_ok, NT)
                        for s in range(ST):
                            for i, (sw, sa) in enumerate(PASSES):
                                ins = pe.matmul(p_y[u][:, s, :], ap[:, u, sa, P * s:P * s + P], wd[:, u, sw, :],
                                                start=(i == 0), stop=(i == 2))
                        ins.then_inc(y_ok, 1)

                    turn(0, 0)
                    turn(1, 1)

                    def period(k, u):
                        hidden(k, u)
                        if has(k + 2):
                            turn(k + 2, u)
                        if has(k - 1):
                            down(k - 1, 1 - u)
                    periods(pe, period)
                    down(E0 - 1, 1)

                @block.vector
                def _(dve):
                    def high_g(k, u):
                        dve.wait_ge(gin[u], (k - u) * 8 + 16)
                        if type(k) is not int or k >= 2:
                            dve.wait_ge(gu_ok, k - 1)
                        dve.tensor_scalar(wg[:, u, 0, :], rg[:, u, :], W_UP, None, ALU.mult)
                        dve.tensor_scalar(rg[:, u, :], rg[:, u, :], W_UP, None, ALU.mult).then_inc(gh_ok, 1)

                    def high_d(k, u):
                        dve.wait_ge(din[u], (k - u) * 8 + 16)
                        if type(k) is not int or k >= 2:
                            dve.wait_ge(y_ok, k - 1)
                        dve.tensor_scalar(wd[:, u, 0, :], rd[:, u, :], W_UP, None, ALU.mult)
                        dve.tensor_scalar(rd[:, u, :], rd[:, u, :], W_UP, None, ALU.mult).then_inc(dh_ok, 1)

                    def x_low(k, u):
                        dve.wait_ge(xh_ok, k + 1)
                        dve.scalar_tensor_tensor(xs[:, u, 1, :, :], p_x[u][:, :, :], H_UP, xs[:, u, 0, :, :],
                                                 ALU.mult, ALU.subtract).then_inc(xl_ok, 1)

                    def times_up(k, u):
                        dve.wait_ge(silu_ok, k + 1)
                        dve.scalar_tensor_tensor(ac[:, u, :], p_h[u][:, 1, :], 1.0 / (H_UP * W_UP), sg[:, u, :],
                                                 ALU.mult, ALU.mult).then_inc(act_ok, 1)

                    def a_low(k, u):
                        dve.wait_ge(ah_ok, k + 1)
                        dve.tensor_tensor(ap[:, u, 1, :], ac[:, u, :], ap[:, u, 0, :], ALU.subtract).then_inc(al_ok, 1)

                    rope.angles(dve)
                    for q in range(NCH):
                        if q == 1:
                            rope.rounded(dve)
                        dve.wait_ge(ssilu_ok, q + 1)
                        dve.scalar_tensor_tensor(sac[:, q, :], p_s[1][:, :], 1.0 / (H_UP * W_UP), ssg[:, q, :],
                                                 ALU.mult, ALU.mult).then_inc(sact_ok, 1)
                        dve.wait_ge(sah_ok, q + 1)
                        dve.tensor_tensor(sap[:, q, 1, :], sac[:, q, :], sap[:, q, 0, :], ALU.subtract).then_inc(sal_ok, 1)
                    for n in range(NT):
                        dve.wait_ge(sy_ok, n + 1)
                        dve.scalar_tensor_tensor(x[:, n, :], p_y[n % 2][:, 0, :], 1.0 / W_UP, x[:, n, :],
                                                 ALU.mult, ALU.add).then_inc(sx_ok, 1)
                    for i in range(3):
                        rope.reduced(dve, i)
                    x_low(0, 0)
                    x_low(1, 1)

                    def period(k, u):
                        times_up(k, u)
                        if has(k + 2):
                            high_g(k + 2, u)
                            x_low(k + 2, u)
                        a_low(k, u)
                        if has(k + 1):
                            high_d(k + 1, 1 - u)
                    periods(dve, period)
                    for i in range(3):
                        rope.shifted(dve, i)
                    dve.wait_ge(sx_ok, NT)


def decoder(nc, a, out):
    g = Store(nc, last=True)
    with g.stack:
        C = {"x": g.sb("x", [P, NT, D]), "ident": g.sb("ident", [P, P]), "hmask": g.sb("hmask", [P, HG]),
             "neghalf": g.sb("neghalf", [P, 1]), "ctxT": g.sb("ctxT", [P, DC, B * S]), "hi": g.sb("hi", [P, B]),
             "cmask": g.sb("cmask", [P, S]), "rs": g.sb("rs", [P, 1])}
        mi = g.sb("mi", [P, B], I32)
        C["slots_in"] = nc.dram_tensor("slots_in", [SLOTS, D], F32, kind="Internal").ap()
        C["slots_out"] = nc.dram_tensor("slots_out", [SLOTS, D], F32, kind="Internal").ap()
        C["zero_ok"] = zero_ok = g.sem("zero_ok")
        zeros = g.sb("zeros", [P, 1024])
        zeroed = g.sem("zeroed")
        in_sem, mask_ok = g.sem("in_sem"), g.sem("mask_ok")
        def weights(g, tag, names, rows):
            w = {k: g.sb(f"{tag}_{k}", [P, DC, D]) for k in ("wq", "wk", "wv", "wo")}
            w.update({k: g.sb(f"{tag}_{k}", [P, DC]) for k in names})
            w.update({k: g.sb(f"{tag}_{k}", [P, D]) for k in rows})
            pairs = [(t[:, :, :] if len(t.shape) == 3 else t[:, :],
                      a[f"{tag}_{k}"].to_broadcast([P, D]) if k in rows else a[f"{tag}_{k}"]) for k, t in w.items()]
            w["loaded"], w["count"] = g.sem(f"{tag}_loaded"), 16 * len(pairs)
            return w, pairs

        w_a1, load_a1 = weights(g, "a1", (), ())
        w_x = {"wo": g.sb("xwo", [P, XH, D]), "loaded": g.sem("x_loaded")}
        split = Split(g, w_x["loaded"])
        load_x = [(w_x["wo"][:, :, :], a["x_wo"])]
        for k, first, heads in (("wq", 0, XH), ("wk", XH, KVH), ("wv", XH + KVH, KVH)):
            w_x[k], dst = split.block(first, heads)
            load_x.append((dst, a[f"x_{k}"]))
        first = Store(nc)
        w_a0, load_a0 = weights(first, "a0", ("bq", "bk"), ("bv", "bo"))
        w_c0, load_c0 = weights(first, "c0", ("bq", "bk"), ("bv", "bo", "gamma", "beta"))
        with nc.Block() as block:
            @block.sync
            def _(sp):
                n = moved(sp, in_sem, [
                    (C["x"][:, :, :], a["x"]), (C["ident"][:, :], a["ident"]), (C["hmask"][:, :], a["hmask"]),
                    (C["cmask"][:, :], a["cmask"]), (mi[:, :], a["mask"]), (C["rs"][:, :], a["rs"].to_broadcast([P, 1]))])
                moved(sp, w_a0["loaded"], load_a0)
                sp.wait_ge(in_sem, n)

            @block.vector
            def _(dve):
                dve.memset(zeros[:, :], 0.0).then_inc(zeroed, 1)
                dve.memset(C["neghalf"][:, :], -0.5)
                dve.wait_ge(in_sem, 16 * 6)
                dve.tensor_scalar(C["hi"][:, :], mi[:, :], 0.5, 100.0 / QSCALE, ALU.is_gt, ALU.mult).then_inc(mask_ok, 1)
                dve.wait_ge(mask_ok, 1)
                dve.tensor_scalar(C["hi"][:, :], C["hi"][:, :], -50.0 / QSCALE, None, ALU.add).then_inc(mask_ok, 1)
                dve.tensor_scalar(C["rs"][:, :], C["rs"][:, :], 0.0, 0.3, ALU.max, ALU.min).then_inc(mask_ok, 1)
                dve.wait_ge(mask_ok, 3)

        def ahead(sp):
            sp.dma_start(C["ctxT"][:, :, :], a["ctxT"]).then_inc(w_c0["loaded"], 16)
            moved(sp, w_c0["loaded"], load_c0)
            w_c0["count"] += 16
            sp.dma_start(C["slots_in"].rearrange("(p a s) d -> p a (s d)", p=P, a=16), bcast(zeros[:, :], 1, 16)).then_inc(zero_ok, 16)
            moved(sp, w_a1["loaded"], load_a1)
            moved(sp, w_x["loaded"], load_x)

        with first.stack:
            attention16(nc, C, "a0", "self", w_a0, ahead=ahead)
            attention16(nc, C, "c0", "cross", w_c0, split=split)
        rows = SlotRows(g, C, RopeTables(g, a, split.raw))
        C["rope"] = rows.rope
        moe_slots(nc, C, a, rows)
        attention16(nc, C, "a1", "causal", w_a1, slots=rows)
        attention128(nc, C, w_x)
        moe_dense(nc, C, a, out)


def kernel(**inputs):
    import concourse.bacc as bacc
    from concourse.bass_utils import run_bass_kernel_spmd as run

    nc = bacc.Bacc("TRN2", target_bir_lowering=False, num_devices=1)
    v = {k: np.asarray(t) for k, t in inputs.items()}

    def chunked(t):
        return t.reshape(t.shape[0] // P, P, -1).transpose(1, 0, 2)

    def column(t):
        return t.reshape(DC, P).T

    arrays = {
        "x": v["x"].reshape(NT, P, D).transpose(1, 0, 2),
        "ctxT": chunked(v["ctx_2048"].reshape(B * S, D).T),
        "mask": np.concatenate([v["mask_BxS2_ik0"].T] * 2),
        "rs": v["L0_xattn_residual_scale"].reshape(1, 1),
        "ident": np.eye(P, dtype=np.float32),
        "hmask": (np.arange(P)[:, None] // HD == np.arange(HG)).astype(np.float32),
        "cmask": np.where(np.arange(S) > np.arange(P)[:, None] % S, np.float32(-1e9 / QSCALE), np.float32(0)),
    }
    for tag, qkv, bias, wo, bo in (("a0", "L0_attn_Wqkv_w", "L0_attn_Wqkv_b", "L0_attn_out_w", "L0_attn_out_b"),
                                   ("a1", "L1_attn_w_qkv", None, "L1_attn_w_o", None)):
        for i, n in enumerate("qkv"):
            arrays[f"{tag}_w{n}"] = chunked(v[qkv][D * i:D * i + D].T)
            if bias:
                part = v[bias][D * i:D * i + D]
                arrays[f"{tag}_b{n}"] = part.reshape(1, D) if n == "v" else column(part)
        arrays[f"{tag}_wo"] = chunked(v[wo].T)
        if bo:
            arrays[f"{tag}_bo"] = v[bo].reshape(1, D)
    for n in "qkvo":
        arrays[f"c0_w{n}"] = chunked(v[f"L0_xattn_W{n}"].T)
        part = v[f"L0_xattn_b{n}"]
        arrays[f"c0_b{n}"] = column(part) if n in "qk" else part.reshape(1, D)
    arrays["c0_gamma"] = v["L0_xattn_ln_gamma"].reshape(1, D)
    arrays["c0_beta"] = v["L0_xattn_ln_beta"].reshape(1, D)

    pos, itok = v["pos_BxS2"].T, v["itok_BxS_4096_4607"]
    arrays["pos"] = np.concatenate([np.concatenate([pos, itok.T]), itok.reshape(NT, P).T], axis=1)
    arrays["inv"] = (np.float32(1) / np.float32(10000) ** (np.arange(0, XD, 2, dtype=np.float32) / np.float32(XD))).reshape(1, RH)
    arrays["qw"] = v["L1_xattn_q_norm_w"].reshape(1, XD)
    arrays["kw"] = v["L1_xattn_k_norm_w"].reshape(1, XD)
    for n in "qkvo":
        arrays[f"x_w{n}"] = chunked(v[f"L1_xattn_W{n}"].T)
    def gate_up(t):
        return t.reshape(-1, DC, P, 2, I0).transpose(0, 2, 1, 3, 4).reshape(-1, P, DC * 2 * I0)

    arrays["m0_wgu"] = gate_up(v["L0_ffn_w13"])
    arrays["m0_wd"] = v["L0_ffn_w2"]
    shared = gate_up(np.concatenate([v["L0_ffn_shared_gate_w"], v["L0_ffn_shared_up_w"]], axis=1))[0]
    arrays["m0_ws"] = np.concatenate([shared, v["L0_ffn_shared_down_w"]], axis=1)
    arrays["m0_gate"] = chunked(v["L0_ffn_gate_w"].T)
    arrays["m0_normw"] = v["L0_ffn_norm_w"].reshape(1, D)
    arrays["eids"] = np.arange(E0, dtype=np.float32).reshape(1, E0)
    arrays["before"] = np.triu(np.ones((P, P), np.float32), 1)
    def with_shared(experts, shared):
        return np.concatenate([experts, shared[None], np.zeros_like(shared[None])])

    gu = with_shared(v["L1_ffn_gu_w"].reshape(E1, 2, I1, D), np.stack([v["L1_ffn_sh_gate_w"], v["L1_ffn_sh_up_w"]]))
    gu = gu.reshape(NPAIR, 2, 2, I1, DC, P).transpose(0, 5, 4, 2, 1, 3)
    dp = with_shared(v["L1_ffn_dp_w"], v["L1_ffn_sh_down_w"]).transpose(0, 2, 1)
    arrays["m1_w"] = np.concatenate([gu.reshape(NPAIR, P, -1), dp.reshape(NPAIR, P, D)], axis=2)
    arrays["m1_gate"] = chunked(np.concatenate([v["L1_ffn_gate_w"], v["L1_ffn_sh_gate1_w"]]).T)
    arrays = {k: np.ascontiguousarray(t) for k, t in arrays.items()}
    a = {k: nc.dram_tensor(f"in_{k}", t.shape, mybir.dt.from_np(t.dtype), kind="ExternalInput").ap()
         for k, t in arrays.items()}
    out = nc.dram_tensor("out_x", [B * S, D], F32, kind="ExternalOutput").ap()
    decoder(nc, a, out)
    r = run(nc, [{f"in_{k}": t for k, t in arrays.items()}], core_ids=[0])
    return r.results[0]["out_x"].reshape(B, S, D)
```
